# Optimizing a Trainium2 kernel written in Bass

```python
import numpy as np
import jax
import jax.numpy as jnp

def _softmax(x, axis=-1):
    return jax.nn.softmax(x, axis=axis)

def _gelu(x):
    return jax.nn.gelu(x, approximate=True)

def _silu(x):
    return jax.nn.silu(x)

def _sigmoid(x):
    return jax.nn.sigmoid(x)

def _layernorm(x, axis=-1, eps=1e-05):
    m = jnp.mean(x, axis=axis, keepdims=True)
    v = jnp.var(x, axis=axis, keepdims=True)
    return (x - m) / jnp.sqrt(v + eps)

def _scatter_add(tgt, idx, src, axis=0):
    return tgt.at[idx].add(src)

def _segment_sum(src, seg, n):
    return jax.ops.segment_sum(src, seg, n)
kernel_name = 'mk_seq_preln_d1_jaxref_r4_c52efc'

def setup_inputs(seed: int=0):
    np.random.seed(seed)
    _w = jnp.asarray

    def _L0_attn_setup():
        import jax, jax.numpy as jnp
        import numpy as np
        import math
        D_MODEL = 256
        NUM_HEADS = 16
        D_HEAD = D_MODEL // NUM_HEADS
        BATCH = 4
        SEQ = 512

        def _trunc_normal(key, shape, sd):
            return sd * jax.random.truncated_normal(key, -3.0, 3.0, shape, dtype=jnp.float32)
        key = jax.random.key(seed)
        kx, kq, kk, kv, ko = jax.random.split(key, 5)
        sd = (2.0 / (NUM_HEADS * D_HEAD + D_MODEL)) ** 0.5
        x = jax.random.normal(kx, (BATCH, SEQ, D_MODEL), dtype=jnp.float32)
        WQ = _trunc_normal(kq, (NUM_HEADS, D_HEAD, D_MODEL), sd)
        WK = _trunc_normal(kk, (NUM_HEADS, D_HEAD, D_MODEL), sd)
        WV = _trunc_normal(kv, (NUM_HEADS, D_HEAD, D_MODEL), sd)
        WO = _trunc_normal(ko, (NUM_HEADS, D_MODEL, D_HEAD), sd)
        return {'x': x, 'WQ': WQ, 'WK': WK, 'WV': WV, 'WO': WO}
    _L0_attn_in = _L0_attn_setup()

    def _L0_ffn_setup():
        import jax, jax.numpy as jnp
        import numpy as np
        NUM_EXPERTS = 8
        TOP_K = 2
        ROUTE_SCALE = 1.0
        DIM = 256
        HID = 256
        B, S = (2, 1024)
        key = jax.random.key(seed)
        ks = jax.random.split(key, 9)
        sc = 0.05
        return {'x': jax.random.normal(ks[0], (B, S, DIM), dtype=jnp.float32), 'gate_w': jax.random.normal(ks[1], (NUM_EXPERTS, DIM), dtype=jnp.float32) * sc, 'w1': jax.random.normal(ks[2], (NUM_EXPERTS, HID, DIM), dtype=jnp.float32) * sc, 'w2': jax.random.normal(ks[3], (NUM_EXPERTS, DIM, HID), dtype=jnp.float32) * sc, 'w3': jax.random.normal(ks[4], (NUM_EXPERTS, HID, DIM), dtype=jnp.float32) * sc, 'sw1': jax.random.normal(ks[5], (HID, DIM), dtype=jnp.float32) * sc, 'sw2': jax.random.normal(ks[6], (DIM, HID), dtype=jnp.float32) * sc, 'sw3': jax.random.normal(ks[7], (HID, DIM), dtype=jnp.float32) * sc, 'expert_bias': jnp.zeros((NUM_EXPERTS,), dtype=jnp.float32)}
    _L0_ffn_in = _L0_ffn_setup()
    _d = {'L0_attn_x': _L0_attn_in['x'], 'L0_attn_WQ': _L0_attn_in['WQ'], 'L0_attn_WK': _L0_attn_in['WK'], 'L0_attn_WV': _L0_attn_in['WV'], 'L0_attn_WO': _L0_attn_in['WO'], 'L0_ffn_gate_w': _L0_ffn_in['gate_w'], 'L0_ffn_w1': _L0_ffn_in['w1'], 'L0_ffn_w2': _L0_ffn_in['w2'], 'L0_ffn_w3': _L0_ffn_in['w3'], 'L0_ffn_sw1': _L0_ffn_in['sw1'], 'L0_ffn_sw2': _L0_ffn_in['sw2'], 'L0_ffn_sw3': _L0_ffn_in['sw3'], 'L0_ffn_expert_bias': _L0_ffn_in['expert_bias']}
    _x0 = _d['L0_attn_x']
    _d['L0_attn_x'] = jax.random.normal(jax.random.fold_in(jax.random.key(seed), 1), (16, 512, 256), dtype=_x0.dtype)
    del _x0
    return _d

def reference(L0_attn_x, L0_attn_WQ, L0_attn_WK, L0_attn_WV, L0_attn_WO, L0_ffn_gate_w, L0_ffn_w1, L0_ffn_w2, L0_ffn_w3, L0_ffn_sw1, L0_ffn_sw2, L0_ffn_sw3, L0_ffn_expert_bias):

    def _L0_attn_ref(x, WQ, WK, WV, WO):
        import jax, jax.numpy as jnp
        import numpy as np
        import math
        D_MODEL = 256
        NUM_HEADS = 16
        D_HEAD = D_MODEL // NUM_HEADS
        BATCH = 4
        SEQ = 512

        def _trunc_normal(key, shape, sd):
            return sd * jax.random.truncated_normal(key, -3.0, 3.0, shape, dtype=jnp.float32)
        Q = jnp.einsum('bsd,hkd->bhsk', x, WQ)
        K = jnp.einsum('bsd,hkd->bhsk', x, WK)
        V = jnp.einsum('bsd,hkd->bhsk', x, WV)
        d_k = Q.shape[-1]
        scores = jnp.einsum('bhqd,bhkd->bhqk', Q, K) / math.sqrt(d_k)
        seq_len = x.shape[-2]
        causal = jnp.tril(jnp.ones((seq_len, seq_len), dtype=bool))
        scores = jnp.where(causal, scores, -jnp.inf)
        probs = jax.nn.softmax(scores, axis=-1)
        attn = jnp.einsum('bhqk,bhkv->bhqv', probs, V)
        return jnp.einsum('bhsv,hdv->bsd', attn, WO)

    def _L0_ffn_ref(x, gate_w, w1, w2, w3, sw1, sw2, sw3, expert_bias):
        import jax, jax.numpy as jnp
        import numpy as np
        NUM_EXPERTS = 8
        TOP_K = 2
        ROUTE_SCALE = 1.0
        DIM = 256
        HID = 256
        B, S = (2, 1024)
        bs, slen, dim = x.shape
        xf = x.reshape(-1, dim)
        scores = jax.nn.sigmoid((xf @ gate_w.T).astype(jnp.float32))
        _, sel = jax.lax.top_k(scores + expert_bias[None, :], TOP_K)
        top_scores = jnp.take_along_axis(scores, sel, axis=1) * ROUTE_SCALE
        flat_sel = sel.reshape(-1)
        order = jnp.argsort(flat_sel, stable=True)
        scores_sorted = top_scores.reshape(-1)[order]
        tok_idx = order // TOP_K
        expert_ids = flat_sel[order]
        routed = xf[tok_idx]
        routed = (routed.astype(jnp.float32) * scores_sorted[:, None]).astype(x.dtype)
        out_r = jnp.zeros_like(routed)
        for e in range(NUM_EXPERTS):
            m = (expert_ids == e)[:, None]
            h = jax.nn.silu(routed @ w1[e].T) * (routed @ w3[e].T)
            out_r = out_r + jnp.where(m, h @ w2[e].T, jnp.zeros((), routed.dtype))
        shared = jax.nn.silu(xf @ sw1.T) * (xf @ sw3.T) @ sw2.T
        out_r = (out_r.astype(jnp.float32) * scores_sorted[:, None]).astype(x.dtype)
        out = shared.at[tok_idx].add(out_r)
        return out.reshape(bs, slen, dim)
    x = L0_attn_x
    x = x + _L0_attn_ref(_layernorm(x, axis=-1), L0_attn_WQ, L0_attn_WK, L0_attn_WV, L0_attn_WO)
    x = x + _L0_ffn_ref(_layernorm(x, axis=-1), L0_ffn_gate_w, L0_ffn_w1, L0_ffn_w2, L0_ffn_w3, L0_ffn_sw1, L0_ffn_sw2, L0_ffn_sw3, L0_ffn_expert_bias)
    return x

_drawn_inputs = setup_inputs


def setup_inputs(seed=0):
    import zlib

    import numpy as np

    out = dict(_drawn_inputs(seed))
    spreads = {'L0_ffn_expert_bias': (0.0, 0.1)}
    factors = {}
    for name, (base, spread) in spreads.items():
        noise = np.random.default_rng([zlib.crc32(name.encode()), seed]).standard_normal(out[name].shape)
        drawn = base * np.exp(spread * noise) if base else spread * noise
        out[name] = jnp.asarray(drawn.astype(out[name].dtype))
    for name, factor in factors.items():
        out[name] = (out[name] * factor).astype(out[name].dtype)
    return out
```

```python
import contextlib

import numpy as np
import concourse.bass as bass
import concourse.mybir as mybir
from concourse.alu_op_type import AluOpType as ALU

F32 = mybir.dt.float32
BF16 = mybir.dt.bfloat16
I32 = mybir.dt.int32
U32 = mybir.dt.uint32
ACT = mybir.ActivationFunctionType
AX = mybir.AxisListType

P = 128
NB, S, D = 16, 512, 256
H, DH = 16, 16
TB = S // P
NT = NB * TB
KB = D // P
GH = 4
NG = H // GH
NE, HID = 8, 256
EPS = 1e-5
QSCALE = 0.25
NPROD = 6
Q_PART = (0, 0, 1, 1, 0, 2)
K_PART = (0, 1, 0, 1, 2, 0)
ROWS1 = NPROD * DH
ROWS2 = ROWS1 + 2
MASKED = -1e30

ST_TILES = 2 * NT + NE
SLOTS = ST_TILES * P


class Batch:

    def __init__(self, c, i=None):
        self.c, self.i = c, i

    def times(self, per_batch, more=0):
        v = per_batch * self.c + more
        return v if self.i is None else self.i * (2 * per_batch) + v

    first = property(lambda self: self.i is None and self.c == 0)
    last = property(lambda self: self.i is None and self.c == NB - 1)
    odd = property(lambda self: self.c % 2)
    next = property(lambda self: Batch(self.c + 1, self.i))
    prev = property(lambda self: Batch(self.c - 1, self.i))


def settle(eng, passed):
    eng.sem_inc(passed, 1)


def batches(eng):
    yield Batch(0)
    yield Batch(1)
    with eng.Fori(0, (NB - 4) // 2) as i:
        yield Batch(2, i)
        yield Batch(3, i)
    yield Batch(NB - 2)
    yield Batch(NB - 1)


TASKS = (
    ("OT", "Q0", "K0"),
    ("OT", "Q1", "K1", "AT0", "AT1"),
    ("OT", "V0", "V1"),
    ("OT", "WO0", "WO1", "X0", "X1"),
)
PER_BATCH = sum(len(t) for t in TASKS)
PRO = tuple((t, 0) for t in ("X0", "X1", "Q0", "K0", "Q1", "K1", "V0", "V1")) + (("X0", 1), ("X1", 1))
OT_LAG = 2
EARLY_MAX = 7


def tasks(b, g):
    out = []
    for t in TASKS[g]:
        if t == "OT" and b.first and g < OT_LAG:
            continue
        if t[:2] in ("AT", "WO") and b.first:
            continue
        if t[0] in "QKV" and b.last:
            continue
        if t[0] == "X" and b.i is None and b.c >= NB - 2:
            continue
        out.append(t)
    return out


def misc_no(b, g, t):
    n = sum(len(tasks(b, k)) for k in range(g)) + tasks(b, g).index(t)
    if b.first:
        return len(PRO) + n
    lack = PER_BATCH - sum(len(tasks(Batch(0), k)) for k in range(NG)) + (2 if b.last else 0)
    return b.times(PER_BATCH, len(PRO) - lack + n)


def misc_bank(b, g, t):
    return misc_no(Batch(b.c), g, t) % 2


def whose(b, g, t):
    if t == "OT":
        return (b.prev, g + NG - OT_LAG) if g < OT_LAG else (b, g - OT_LAG)
    return (b.prev if t[:2] in ("AT", "WO") else b.next.next if t[0] == "X" else b.next), None


def two_before(b, g, t):
    here = [(b, k, x) for k in range(g + 1) for x in tasks(b, k)]
    here = here[:[x[1:] for x in here].index((g, t))]
    if len(here) >= 2:
        sb, k, x = here[-2]
        return x, *whose(sb, k, x)
    if b.first:
        t, n = PRO[len(here) - 2]
        return t, Batch(n), None
    prev = [(b.prev, k, x) for k in range(NG) for x in tasks(b.prev, k)]
    sb, k, x = prev[len(here) - 2]
    return x, *whose(sb, k, x)


def due(b, g, u):
    return [t for k, t in enumerate(tasks(b, g)) if 2 * k + 2 == u]


def kb_place(j, kb):
    pair, i = divmod(j, 2)
    if kb == 0:
        return pair, 3 * i, 0, S
    if kb == 1:
        return pair, 3 * i + 1, P, S - P
    if kb == 3:
        return pair, 3 * i + 1, 0, P
    return pair, 2, 2 * P * i, 2 * P


PAIR_BANKS = (((0, 0),), ((0, 3), (0, 1)), ((0, 2), (1, 2)), ((1, 0),), ((1, 3), (1, 1)))
MAX_UNITS = ((0, (0, 1, 2, 3)), (1, (0, 1)), (1, (2, 3)),
             (2, (0,)), (2, (1,)), (2, (2,)), (2, (3,)),
             (3, (0,)), (3, (1,)), (3, (2,)), (3, (3,)))
NMU = len(MAX_UNITS)
U1 = NMU + 1
U2 = 10
LAG = 3
TURN = 12
MID_LAG = 3
PLACES = LAG + U2
PV_AT = (4, 6, 8, 10)
EARLY = 4


def attention(nc, ctx, T, x_dram, wqk_dram, wv_dram, wo_dram):
    sb = lambda name, shape, dt=F32: ctx.enter_context(nc.sbuf_tensor(name, shape, dt))
    sem = lambda name: ctx.enter_context(nc.semaphore(name))
    x, mean, rstd, stats = T.x, T.mean, T.rstd, T.stats

    xn = sb("xn", [P, TB, D])
    xnT = sb("xnT", [P, KB, S])
    qf = sb("qf", [P, 2, S])
    rem = sb("rem", [P, 2, S])
    part = sb("part", [P, 2, 2, 3, S], BF16)
    QS = sb("QS", [P, H, S], BF16)
    KS = sb("KS", [P, H, S], BF16)
    V = sb("V_sb", [P, 2, TB, H, 2 * DH])
    PR = sb("PR", [P, 2, 2, 5, S])
    O = sb("O_sb", [P, 2, S])
    attn = sb("attn", [P, TB, D])
    attnT = sb("attnT", [P, KB, S])
    rec = sb("rec", [P, TB, GH])
    mx = sb("mx", [P, 2, GH, TB])
    nm = sb("nm", [GH * TB, 2, 2, P], BF16)
    wqk = sb("wqk_sb", [P, KB, 2 * D])
    wv = sb("wv_sb", [P, KB, D])
    wo = sb("wo_sb", [P, KB, D])
    identb = sb("identb", [P, P], BF16)
    tri = sb("tri", [P, P], BF16)

    score = ctx.enter_context(nc.psum_tensor("score", [P, 3, S], F32))
    logit = ctx.enter_context(nc.psum_tensor("logit", [P, 2, S], F32))
    opsum = ctx.enter_context(nc.psum_tensor("opsum", [P, S], F32))
    misc = ctx.enter_context(nc.psum_tensor("misc", [P, 2, S], F32))

    x_in = [sem(f"x_in{q}") for q in range(4)]
    w_in = sem("w_in")
    const_a, const_ready = sem("const_a"), sem("const_ready")
    stat_ready, std_ready, rstd_ready = sem("stat_ready"), sem("std_ready"), sem("rstd_ready")
    xn_ready = sem("xn_ready")
    misc_full = sem("misc_full")
    misc_free = [sem("misc_free0"), sem("misc_free1")]
    qf_ready, rem_ready, mid_ready, parts_ready = sem("qf_ready"), sem("rem_ready"), sem("mid_ready"), sem("parts_ready")
    high_ready = sem("high_ready")
    stacked = [sem("stacked0"), sem("stacked1")]
    max_full, max_free = sem("max_full"), sem("max_free")
    nm_high = sem("nm_high")
    nm_ready = sem("nm_ready")
    nm_in = [sem("nm_in0"), sem("nm_in1")]
    logit_full, logit_free = sem("logit_full"), sem("logit_free")
    masked = sem("masked")
    o_full, o_free = sem("o_full"), sem("o_free")
    rec_ready, attn_ready = sem("rec_ready"), sem("attn_ready")
    v_ready, xnT_ready, attnT_ready = sem("v_ready"), sem("xnT_ready"), sem("attnT_ready")
    x_out = sem("x_out")
    ones_ready = sem("ones_ready")

    xv = x_dram.rearrange("(n p) d -> p n d", p=P)
    block = ctx.enter_context(nc.Block())
    HALF = (("Q0", "K0"), ("Q1", "K1"))

    def proj(t):
        half, qk = int(t[1]), "QK".index(t[0])
        return half, qk, 2 * half + qk

    TAIL = misc_no(Batch(NB - 1), 3, tasks(Batch(NB - 1), 3)[-1]) + 1
    TAIL_AT = TAIL + 2
    TAIL_USES = len(tasks(Batch(NB - 1), NG - 1))

    @block.sync
    def _(sp):
        q = NT // 4
        sp.dma_start(x[:, 0:q, :], xv[:, 0:q, :]).then_inc(x_in[0], 16)
        sp.dma_start(wqk[:], wqk_dram.rearrange("(k p) n -> p k n", p=P)).then_inc(w_in, 16)
        sp.dma_start(wv[:], wv_dram.rearrange("(k p) n -> p k n", p=P)).then_inc(w_in, 16)
        sp.dma_start(wo[:], wo_dram.rearrange("(k p) n -> p k n", p=P)).then_inc(w_in, 16)
        for k in range(1, 4):
            sp.dma_start(x[:, q * k:q * (k + 1), :], xv[:, q * k:q * (k + 1), :]).then_inc(x_in[k], 16)

        def stack(b, half):
            for s in (parts_ready, high_ready, mid_ready):
                sp.wait_ge(s, b.times(4, 2 * half + 2))
            settle(sp, T.passed)
            if not b.first:
                sp.wait_ge(logit_full, b.prev.times(NG * U2, (2 * half + 2) * U2))
            for qk, (dst, order) in enumerate(((QS, Q_PART), (KS, K_PART))):
                for r in range(NPROD):
                    src = part[:, half, qk, order[r], :]
                    sp.dma_start(dst[DH * r:DH * r + DH, 8 * half:8 * half + 8, :], src).then_inc(stacked[half], 16)

        def maxima(b, g):
            par = g % 2
            sp.wait_ge(nm_ready, b.times(NG, g + 1))
            for k in range(2):
                dst = QS[ROWS1 + k:ROWS1 + k + 1, GH * g:GH * g + GH, :].rearrange("p h (t q) -> p h t q", t=TB)
                sp.dma_start(dst, nm[:, par, k, :]).then_inc(nm_in[par], 16)

        stack(Batch(0), 0)
        stack(Batch(0), 1)
        maxima(Batch(0), 0)
        for b in batches(sp):
            if not b.first:
                stack(b, 1)
            maxima(b, 1)
            maxima(b, 2)
            if not b.last:
                stack(b.next, 0)
            maxima(b, 3)
            if not b.last:
                maxima(b.next, 0)

    @block.gpsimd
    def _(pool):
        ident = T.ident
        pool.memset(ident[:], 0.0).then_inc(const_a, 1)
        pool.memset(identb[:], 0.0).then_inc(const_a, 1)
        pool.memset(tri[:], 0.0).then_inc(const_a, 1)
        pool.memset(V[:, :, :, :, DH:], 1.0).then_inc(ones_ready, 1)
        pool.wait_ge(const_a, 3)
        for a in (ident, identb):
            pool.affine_select(out=a[:], in_=a[:], compare_op=ALU.not_equal, fill=1.0, base=0,
                               pattern=[[-1, P]], channel_multiplier=1).then_inc(const_ready, 1)
        pool.affine_select(out=tri[:], in_=tri[:], compare_op=ALU.is_ge, fill=MASKED, base=0,
                           pattern=[[-1, P]], channel_multiplier=1).then_inc(const_ready, 1)

        def split_rem(b, t):
            half, qk, n = proj(t)
            pool.wait_ge(high_ready, b.times(4, n + 1))
            if not (b.first and n < 2):
                pool.wait_ge(parts_ready, b.times(4, n - 1))
            pool.tensor_tensor(rem[:, n % 2, :], qf[:, n % 2, :], part[:, half, qk, 0, :], ALU.subtract).then_inc(rem_ready, 1)

        def split_low(b, t):
            half, qk, n = proj(t)
            pool.wait_ge(mid_ready, b.times(4, n + 1))
            pool.tensor_tensor(part[:, half, qk, 2, :], rem[:, n % 2, :], part[:, half, qk, 1, :], ALU.subtract).then_inc(parts_ready, 1)

        def mask_pair(b, g, pair):
            pool.wait_ge(logit_free, b.times(NG * U2, g * U2 + 5 * pair + 5))
            settle(pool, T.passed)
            blocks = PR[:, g % 2, pair].rearrange("p k (c q) -> p (k c) q", q=P)
            sels = (blocks[:, 0:20:4, :], blocks[:, 5:18:12, :], blocks[:, 10, :])
            for k, v in enumerate(sels):
                pool.affine_select(out=v, in_=v, compare_op=ALU.is_ge, fill=0.0, base=0,
                                   pattern=([[0, v.shape[1]]] if k < 2 else []) + [[1, P]], channel_multiplier=-1).then_inc(masked, 1)

        for t, _ in PRO:
            if t[0] in "QK":
                split_rem(Batch(0), t)
                split_low(Batch(0), t)
        for b in batches(pool):
            for g in range(NG):
                split = [t for t in tasks(b, g) if t[0] in "QK"]
                for t in split:
                    split_rem(b.next, t)
                for t in split[:1]:
                    split_low(b.next, t)
                mask_pair(b, g, 0)
                for t in split[1:]:
                    split_low(b.next, t)
                mask_pair(b, g, 1)

    @block.scalar
    def _(act):
        def root(part):
            lo, hi = (0, EARLY * TB) if part == 0 else (EARLY * TB, NT)
            act.wait_ge(stat_ready, 5 * (part + 1))
            act.activation(rstd[:, lo:hi], rstd[:, lo:hi], ACT.Sqrt).then_inc(std_ready, 1)

        root(0)

        def evac(b, t, n, bank):
            if t[:2] in ("OT", "WO"):
                return
            src = misc[:, bank, :]
            act.wait_ge(misc_full, n + 1)
            if t[0] == "X":
                act.activation(xnT[:, int(t[1]), :], src, ACT.Copy).then_inc(xnT_ready, 1)
            elif t[0] in "QK":
                half, qk, k = proj(t)
                if not (b.first and k < 2):
                    act.wait_ge(parts_ready, b.times(4, k - 1))
                if not b.first:
                    act.wait_ge(stacked[half], b.times(16 * 2 * NPROD))
                act.activation(qf[:, k % 2, :], src, ACT.Copy, scale=QSCALE if qk == 0 else 1.0).then_inc(qf_ready, 1)
                act.wait_ge(qf_ready, b.times(4, k + 1))
                act.activation(part[:, half, qk, 0, :], qf[:, k % 2, :], ACT.Copy).then_inc(high_ready, 1)
            elif t[0] == "V":
                i = int(t[1])
                act.activation(V[:, b.odd, 2 * i:2 * i + 2, :, 0:DH],
                               src.rearrange("p (t h d) -> p t h d", t=2, h=H), ACT.Copy).then_inc(v_ready, 1)
            elif t[:2] == "AT":
                act.activation(attnT[:, int(t[2]), :], src, ACT.Copy).then_inc(attnT_ready, 1)

        def step(b, g):
            for u in range(PLACES):
                if u >= LAG:
                    n = g * U2 + u - LAG
                    act.wait_ge(logit_full, b.times(NG * U2, n + 1))
                    if u == LAG and not (b.first and g < 2):
                        act.wait_ge(o_full, b.times(NG, g - 1))
                    act.activation(PR[:, g % 2, (u - LAG) // 5, (u - LAG) % 5, :], logit[:, n % 2, :], ACT.Exp).then_inc(logit_free, 1)
                for t in due(b, g, u):
                    evac(whose(b, g, t)[0], t, misc_no(b, g, t), misc_bank(b, g, t))
            if not (b.first and g == 0):
                evac_o(b, g - 1)

        def evac_o(b, g):
            act.wait_ge(o_full, b.times(NG, g + 1))
            if not (b.first and g < 2):
                act.wait_ge(rec_ready, b.times(NG, g - 1))
            act.activation(O[:, g % 2, :], opsum[:], ACT.Copy).then_inc(o_free, 1)

        for n, (t, k) in enumerate(PRO):
            evac(Batch(k), t, n, n % 2)
        for b in batches(act):
            for g in range(NG):
                step(b, g)
                if b.first and g == NG - 1:
                    root(1)
        last = Batch(NB)
        evac_o(last, -1)
        for k in range(2):
            n = TAIL_AT + k
            evac(last.prev, f"AT{k}", n, n % 2)

    @block.tensor
    def _(pe):
        ident = T.ident

        def emptied(kind, who, g):
            if kind[0] == "X":
                return xnT_ready, who.times(2, int(kind[1]) + 1)
            if kind[0] in "QK":
                return qf_ready, who.times(4, proj(kind)[2] + 1)
            if kind[0] == "V":
                return v_ready, who.times(2, int(kind[1]) + 1)
            if kind == "OT":
                return attn_ready, who.times(NG, g + 1)
            if kind[:2] == "AT":
                return attnT_ready, who.times(2, int(kind[2]) + 1)
            return x_out, who.times(2, int(kind[2]) + 1)

        def do(t, b, g, k, before):
            bank = misc[:, k, :]
            if before:
                pe.wait_ge(*emptied(*before))
            if t[0] == "X":
                k = int(t[1])
                pe.wait_ge(xn_ready, b.times(TB, TB))
                for tt in range(TB):
                    mm = pe.transpose(bank[:, tt * P:(tt + 1) * P], xn[:, tt, k * P:(k + 1) * P], ident[:])
            elif t[0] in "QK":
                half, qk, _ = proj(t)
                pe.wait_ge(xnT_ready, b.times(2, 2))
                m = 2 * qk + half
                for k in range(KB):
                    mm = pe.matmul(bank, wqk[:, k, m * P:(m + 1) * P], xnT[:, k, :], start=(k == 0), stop=(k == KB - 1))
            elif t[0] == "V":
                pe.wait_ge(xnT_ready, b.times(2, 2))
                for tt in range(2):
                    tile = 2 * int(t[1]) + tt
                    for k in range(KB):
                        mm = pe.matmul(bank[:, tt * D:(tt + 1) * D], xnT[:, k, tile * P:(tile + 1) * P], wv[:, k, :],
                                       start=(k == 0), stop=(k == KB - 1))
            elif t == "OT":
                pe.wait_ge(o_free, b.times(NG, g + 1))
                for tt in range(TB):
                    mm = pe.transpose(bank[:, tt * P:(tt + 1) * P], O[:, g % 2, tt * P:(tt + 1) * P], ident[:])
            elif t[:2] == "AT":
                k = int(t[2])
                pe.wait_ge(attn_ready, b.times(NG, NG))
                for tt in range(TB):
                    mm = pe.transpose(bank[:, tt * P:(tt + 1) * P], attn[:, tt, k * P:(k + 1) * P], ident[:])
            elif t[:2] == "WO":
                pe.wait_ge(attnT_ready, b.times(2, 2))
                for tt in range(2):
                    tile = 2 * int(t[2]) + tt
                    for k in range(KB):
                        mm = pe.matmul(bank[:, tt * D:(tt + 1) * D], attnT[:, k, tile * P:(tile + 1) * P], wo[:, k, :],
                                       start=(k == 0), stop=(k == KB - 1))
            mm.then_inc(misc_full, 1)

        def max_unit(b, g, u):
            n = g * U1 + u
            if not (b.first and n < 3):
                pe.wait_ge(max_free, b.times(NG * U1, n - 2))
            if u == 0 and g % 2 == 0:
                pe.wait_ge(stacked[g // 2], b.times(16 * 2 * NPROD, 16 * 2 * NPROD))
            bank = score[:, n % 3, :]
            qt, heads = MAX_UNITS[u]
            cols = (qt + 1) * P
            for k, j in enumerate(heads):
                h = GH * g + j
                out = bank[:, k * cols:(k + 1) * cols]
                pe.matmul(out, QS[0:ROWS1, h, qt * P:(qt + 1) * P], KS[0:ROWS1, h, 0:cols], start=True, stop=False)
                mm = pe.matmul(out[:, cols - P:cols], identb[:], tri[:], start=False, stop=True)
            mm.then_inc(max_full, 1)

        def max_turn(b, g):
            n = g * U1 + NMU
            pe.wait_ge(max_free, b.times(NG * U1, n))
            pe.transpose(score[0:GH * TB, n % 3, 0:P], mx[:, g % 2].rearrange("p j t -> p (j t)"), ident[:]).then_inc(max_full, 1)

        def logit_unit(b, g, u):
            n = g * U2 + u
            if not (b.first and n < 2):
                pe.wait_ge(logit_free, b.times(NG * U2, n - 1))
            if u == 0:
                pe.wait_ge(nm_in[g % 2], b.times(64, 32 * (g // 2) + 32))
            pair = u // 5
            for i, kb in PAIR_BANKS[u % 5]:
                j = 2 * pair + i
                _, _, off, cols = kb_place(j, kb)
                h = GH * g + j
                mm = pe.matmul(logit[:, n % 2, off:off + cols], KS[0:ROWS2, h, kb * P:(kb + 1) * P],
                               QS[0:ROWS2, h, kb * P:S], start=True, stop=True)
            mm.then_inc(logit_full, 1)

        def pv(b, g, kb):
            if kb == 0:
                if not (b.first and g == 0):
                    pe.wait_ge(o_free, b.times(NG, g))
                pe.wait_ge(masked, b.times(NG * 6, 6 * g + 6))
                pe.wait_ge(v_ready, b.times(2, 2))
            for j in range(GH):
                pair, bank, off, cols = kb_place(j, kb)
                mm = pe.matmul(opsum[32 * j:32 * j + 32, kb * P:S], V[:, b.odd, kb, GH * g + j, :],
                               PR[:, g % 2, pair, bank, off:off + cols], start=(kb == 0), stop=(kb == TB - 1))
            if kb == TB - 1:
                mm.then_inc(o_full, 1)

        pe.wait_ge(const_ready, 3)
        pe.wait_ge(ones_ready, 2)
        pe.wait_ge(w_in, 48)
        for n, (t, k) in enumerate(PRO):
            do(t, Batch(k), None, n % 2, (PRO[n - 2][0], Batch(PRO[n - 2][1]), None) if n >= 2 else None)
            if n == EARLY_MAX:
                for u in range(NMU):
                    max_unit(Batch(0), 0, u)
                max_turn(Batch(0), 0)
        for b in batches(pe):
            for g in range(NG):
                ahead = None if b.last and g == NG - 1 else (b, g + 1) if g < NG - 1 else (b.next, 0)
                before = (b, g - 1) if g else None if b.first else (b.prev, NG - 1)
                ts = tasks(b, g)
                for u in range(PLACES):
                    if ahead and u < NMU:
                        max_unit(*ahead, u)
                    if ahead and u == TURN:
                        max_turn(*ahead)
                    if u >= LAG:
                        logit_unit(b, g, u - LAG)
                    if u % 2 and ts:
                        t = ts.pop(0)
                        do(t, *whose(b, g, t), misc_bank(b, g, t), two_before(b, g, t))
                    if before and u in PV_AT:
                        pv(*before, PV_AT.index(u))
        last = Batch(NB - 1)
        end = [(x, *whose(last, NG - 1, x)) for x in tasks(last, NG - 1)]
        for t, g in (("OT", 2), ("OT", 3), ("AT0", None), ("AT1", None), ("WO0", None), ("WO1", None)):
            if (t, g) == ("OT", 3):
                for kb in range(TB):
                    pv(last, NG - 1, kb)
            do(t, last, g, (TAIL + len(end) - TAIL_USES) % 2, end[-2])
            end.append((t, last, g))

    @block.vector
    def _(dve):
        dve.memset(KS[ROWS1:P, :, :], 1.0).then_inc(ones_ready, 1)
        def statistics(tiles_done, n):
            with dve.Fori(0, n) as i:
                for k in range(TB):
                    t = i * TB + (tiles_done + k)
                    dve.bn_stats(flat(dyn(stats, t)), flat(dyn(x, t))).then_inc(T.bn, 1)

        def deviations(part):
            lo, hi = (0, EARLY * TB) if part == 0 else (EARLY * TB, NT)
            dve.wait_ge(T.bn, hi)
            norm_stats(dve, T, stat_ready, 5 * part, lo, hi)

        def invert(part):
            lo, hi = (0, EARLY * TB) if part == 0 else (EARLY * TB, NT)
            dve.wait_ge(std_ready, part + 1)
            dve.reciprocal(rstd[:, lo:hi], rstd[:, lo:hi]).then_inc(rstd_ready, 1)
            dve.wait_ge(rstd_ready, part + 1)

        dve.wait_ge(x_in[0], 16)
        statistics(0, EARLY)
        deviations(0)
        invert(0)

        def norm(b):
            if not b.first:
                dve.wait_ge(xnT_ready, b.times(2))
            for tt in range(TB):
                t = b.times(TB, tt)
                sl = (lambda a: a[:, t:t + 1]) if b.i is None else (lambda a: a[:, bass.ds(t, 1)])
                xin = (x[:, t, :] if b.i is None else x[:, bass.ds(t, 1), :].rearrange("p a d -> p (a d)"))
                dve.tensor_scalar(xn[:, tt, :], xin, sl(mean), sl(rstd), ALU.subtract, ALU.mult).then_inc(xn_ready, 1)

        def reduce_max(b, g, u):
            n = g * U1 + u
            qt, heads = MAX_UNITS[u]
            cols = (qt + 1) * P
            dve.wait_ge(max_full, b.times(NG * U1, n + 1))
            dve.tensor_reduce(mx[:, g % 2, heads[0]:heads[0] + len(heads), qt],
                              score[:, n % 3, 0:cols * len(heads)].rearrange("p (j k) -> p j k", k=cols),
                              AX.X, ALU.max).then_inc(max_free, 1)

        def max_parts(b, g):
            n = g * U1 + NMU
            dve.wait_ge(max_full, b.times(NG * U1, n + 1))
            if not (b.first and g < 2):
                dve.wait_ge(nm_in[g % 2], b.times(64, 32 * (g // 2)))
            src = score[0:GH * TB, n % 3, 0:P]
            dve.tensor_scalar(nm[:, g % 2, 0, :], src, -1.0, None, ALU.mult).then_inc(nm_high, 1)
            dve.wait_ge(nm_high, b.times(NG, g + 1))
            dve.scalar_tensor_tensor(out=nm[:, g % 2, 1, :], in0=src, scalar=-1.0, in1=nm[:, g % 2, 0, :],
                                     op0=ALU.mult, op1=ALU.subtract).then_inc(nm_ready, 1)
            dve.wait_ge(nm_ready, b.times(NG, g + 1))
            dve.sem_inc(max_free, 1)

        def split_mid(b, t):
            half, qk, n = proj(t)
            dve.wait_ge(rem_ready, b.times(4, n + 1))
            dve.tensor_copy(part[:, half, qk, 1, :], rem[:, n % 2, :]).then_inc(mid_ready, 1)

        def scale_out(b, g, n, bank):
            v = misc[:, bank, :].rearrange("p (t j c) -> p t j c", t=TB, j=GH)
            dve.wait_ge(misc_full, n + 1)
            if g == 0 and not b.first:
                dve.wait_ge(attnT_ready, b.times(2))
            if not (b.first and g == 0):
                dve.wait_ge(attn_ready, b.times(NG, g))
            dve.reciprocal(rec[:], v[:, :, :, DH]).then_inc(rec_ready, 1)
            dve.wait_ge(rec_ready, b.times(NG, g + 1))
            out = attn[:, :, GH * DH * g:GH * DH * (g + 1)].rearrange("p t (j c) -> p t j c", j=GH)
            dve.tensor_tensor(out, v[:, :, :, 0:DH], rec[:].unsqueeze(3).to_broadcast([P, TB, GH, DH]), ALU.mult).then_inc(attn_ready, 1)

        def add_out(b, k, n, bank):
            dve.wait_ge(misc_full, n + 1)
            t0 = b.times(TB, 2 * k)
            xs = x[:, t0:t0 + 2, :] if b.i is None else x[:, bass.ds(t0, 2), :]
            dve.tensor_tensor(xs, misc[:, bank, :].rearrange("p (t d) -> p t d", t=2), xs, ALU.add).then_inc(x_out, 1)
            dve.wait_ge(x_out, b.times(2, k + 1))
            for i in range(2):
                t = b.times(TB, 2 * k + i)
                if b.i is None:
                    dve.bn_stats(stats[:, t, :], x[:, t, :]).then_inc(T.bn, 1)
                else:
                    dve.bn_stats(stats[:, bass.ds(t, 1), :].rearrange("p a s -> p (a s)"),
                                 x[:, bass.ds(t, 1), :].rearrange("p a d -> p (a d)")).then_inc(T.bn, 1)

        def empty(t, b, g, n, bank):
            if t == "OT":
                scale_out(b, g, n, bank)
            elif t[:2] == "WO":
                add_out(b, int(t[2]), n, bank)

        def maxima(b, g):
            for u in range(NMU):
                reduce_max(b, g, u)
            max_parts(b, g)

        norm(Batch(0))
        for n, (t, _) in enumerate(PRO):
            if t[0] in "QK":
                split_mid(Batch(0), t)
            if t == "X1" and n == 1:
                norm(Batch(1))
            if n == EARLY_MAX:
                maxima(Batch(0), 0)
        for b in batches(dve):
            for g in range(NG):
                ahead = None if b.last and g == NG - 1 else (b, g + 1) if g < NG - 1 else (b.next, 0)
                for u in range(PLACES):
                    if ahead and u < NMU:
                        reduce_max(*ahead, u)
                    for t in due(b, g, u):
                        empty(t, *whose(b, g, t), misc_no(b, g, t), misc_bank(b, g, t))
                    for t in due(b, g, u - MID_LAG):
                        if t[0] in "QK":
                            split_mid(whose(b, g, t)[0], t)
                    if ahead and u == TURN:
                        max_parts(*ahead)
                if b.first:
                    if g < 3:
                        dve.wait_ge(x_in[g + 1], 16)
                    statistics((EARLY + 3 * g) * TB, 3)
                    if g == NG - 1:
                        deviations(1)
                if b.i is None and b.c == 1 and g == 0:
                    invert(1)
                if g == 1 and not (b.i is None and b.c >= NB - 2):
                    norm(b.next.next)
        last = Batch(NB - 1)
        for k, g in enumerate((2, 3)):
            scale_out(last, g, TAIL + k, (TAIL + k) % 2)
        for k in range(2):
            add_out(last, k, TAIL_AT + 2 + k, (TAIL_AT + 2 + k) % 2)


def norm_stats(dve, T, done, had, lo, hi):
    s, mean, rstd, tmp = T.stats[:, lo:hi], T.mean[:, lo:hi], T.rstd[:, lo:hi], T.tmp[:, lo:hi]
    n = T.norm_steps
    dve.tensor_tensor(mean, s[:, :, 1], s[:, :, 4], ALU.add).then_inc(done, 1)
    dve.tensor_tensor(tmp, s[:, :, 1], s[:, :, 4], ALU.subtract).then_inc(done, 1)
    dve.tensor_tensor(rstd, s[:, :, 2], s[:, :, 5], ALU.add).then_inc(done, 1)
    dve.wait_ge(done, had + 3)
    dve.tensor_scalar(mean, mean, 0.5, None, ALU.mult).then_inc(n, 1)
    dve.tensor_tensor(tmp, tmp, tmp, ALU.mult).then_inc(n, 1)
    dve.tensor_scalar(rstd, rstd, 1.0 / D, EPS, ALU.mult, ALU.add).then_inc(n, 1)
    T.norm_done += 3
    dve.wait_ge(n, T.norm_done)
    dve.scalar_tensor_tensor(out=rstd, in0=tmp, scalar=0.25, in1=rstd, op0=ALU.mult, op1=ALU.add).then_inc(done, 2)


class Tensors:
    pass


def shared(nc, ctx):
    T = Tensors()
    sb = lambda name, shape, dt=F32: ctx.enter_context(nc.sbuf_tensor(name, shape, dt))
    T.x = sb("x_sb", [P, NT, D])
    T.mean, T.rstd, T.tmp = (sb(n, [P, NT]) for n in ("mean", "rstd", "tmp"))
    T.stats = sb("stats", [P, NT, 6])
    T.ident = sb("ident", [P, P])
    T.bn = ctx.enter_context(nc.semaphore("bn"))
    T.norm_steps = ctx.enter_context(nc.semaphore("norm_steps"))
    T.norm_done = 0
    T.passed = ctx.enter_context(nc.semaphore("passed"))
    return T


def attention_weights(WQ, WK, WV, WO):
    def cols(w):
        return w.reshape(2, H // 2, DH, D).transpose(3, 0, 2, 1).reshape(D, D)
    wqk = np.concatenate([cols(WQ), cols(WK)], axis=1)
    return (np.ascontiguousarray(wqk), np.ascontiguousarray(WV.reshape(H * DH, D).T),
            np.ascontiguousarray(WO.transpose(0, 2, 1).reshape(H * DH, D)))


BLK = 4
PAD_TILES = ST_TILES + NE
ROW = D + 1
RESULTS = 2 * NT * P
PADS = NE + ST_TILES - 2 * NT
BIG = 1e30
LOG2P = 7


CREDIT = 1


def first_apart(eng, n):
    yield 0
    with eng.Fori(1, n) as i:
        yield i


def dyn(a, start, n=1):
    return a[:, bass.ds(start, n)]


def flat(a):
    return a.rearrange("p a b -> p (a b)")


def gate(nc, ctx, T, gw_dram, bias_dram, sorted_dram):
    sb = lambda name, shape, dt=F32: ctx.enter_context(nc.sbuf_tensor(name, shape, dt))
    sem = lambda name: ctx.enter_context(nc.semaphore(name))
    x, mean, rstd = T.x, T.mean, T.rstd
    xn = sb("xn2", [P, 2, BLK, D])
    gw = sb("gw", [P, KB, NE])
    gs = sb("gs", [NE, 2, S])
    score = sb("gate_score", [P, NT, NE])
    tr = ctx.enter_context(nc.psum_tensor("tr", [P, 2, KB, S], F32))
    gp = ctx.enter_context(nc.psum_tensor("gp", [P, 2, S], F32))
    gt = ctx.enter_context(nc.psum_tensor("gt", [P, 2, S], F32))
    gw_in, pad_in, bias_in = sem("gw_in"), sem("pad_in"), sem("bias_in")
    stat, std, rs = sem("g_stat"), sem("g_std"), sem("g_rstd")
    xn_ready, tr_full, xT_a, xT_d = sem("g_xn"), sem("g_tr_full"), sem("g_xT_act"), sem("g_xT_dve")
    gp_full, gs_ready, gt_full, score_ready = sem("gp_full"), sem("gs_ready"), sem("gt_full"), sem("score_ready")
    zero_ready = sem("zero_ready")
    zero = sb("zero", [P, PADS, ROW])

    desc = sb("desc", [P, NE])
    desc_i = sb("desc_i", [P, NE], I32)
    bias = sb("bias", [P, NE])
    biased = sb("biased", [P, NT, NE])
    one1 = sb("one1", [P, NT, NE])
    one2 = sb("one2", [P, NT, NE])
    scr = sb("scr", [P, NT, NE])
    both = sb("both", [P, NT * NE], BF16)
    best = sb("best", [P, NT])
    before = sb("before", [P, P], BF16)
    ones = sb("ones_b", [P, P], BF16)
    pad = NT // 2
    pre = sb("pre", [P, 2, pad + NT, NE])
    tiles = sb("tiles", [P, NE])
    tiles_i = sb("tiles_i", [P, NE], I32)
    first = sb("first", [P, 2, NE + NE])
    jt = sb("jt", [P, ST_TILES])
    jt_i = sb("jt_i", [P, ST_TILES], I32)
    et = sb("et", [P, ST_TILES])
    slot_f = sb("slot_f", [P, NT])
    pad_f = sb("pad_f", [P, NE])
    pad_g = sb("pad_g", [P, NE])
    pad_i = sb("pad_i", [P, NE], U32)
    row_i = sb("row_i", [P, NE], I32)
    row_f = sb("row_f", [P, NE])
    c = sem("route")
    consts, both_ready, cnt_full = sem("g_consts"), sem("both_ready"), sem("cnt_full")
    ca = sem("g_const_a")

    block = ctx.enter_context(nc.Block())

    @block.sync
    def _(sp):
        sp.dma_start(gw[:], gw_dram.rearrange("(k p) n -> p k n", p=P)).then_inc(gw_in, 16)
        sp.dma_start(bias[:], bias_dram.rearrange("(a n) -> a n", a=1).partition_broadcast(P)).then_inc(bias_in, 16)
        sp.wait_ge(zero_ready, 2)
        for t in range(2 * NT, ST_TILES):
            sp.dma_start(sorted_dram[t * P:(t + 1) * P, :], zero[:, NE + t - 2 * NT, :]).then_inc(pad_in, 16)
        sp.wait_ge(pad_in, 16 * (ST_TILES - 2 * NT))

    @block.gpsimd
    def _(pool):
        pool.memset(before[:], 1.0).then_inc(ca, 1)
        pool.memset(ones[:], 1.0).then_inc(consts, 1)
        pool.memset(zero[:], 0.0).then_inc(zero_ready, 1)
        pool.wait_ge(zero_ready, 1)
        pool.iota(zero[:, :, D:ROW].bitcast(I32).rearrange("p k a -> p (k a)"), pattern=[[P, PADS]], base=RESULTS, channel_multiplier=1).then_inc(zero_ready, 1)
        pool.iota(desc_i[:], pattern=[[-1, NE]], base=NE, channel_multiplier=0).then_inc(consts, 1)
        pool.iota(jt_i[:], pattern=[[1, ST_TILES]], base=0, channel_multiplier=0).then_inc(consts, 1)
        pool.iota(row_i[:], pattern=[[P, NE]], base=ST_TILES * P, channel_multiplier=1).then_inc(consts, 1)
        pool.iota(T.dest[:], pattern=[[P, NT], [NT * P, 2]], base=0, channel_multiplier=1).then_inc(consts, 1)
        pool.wait_ge(ca, 1)
        pool.affine_select(out=before[:], in_=before[:], compare_op=ALU.is_gt, fill=0.0, base=0,
                           pattern=[[1, P]], channel_multiplier=-1).then_inc(consts, 1)
        pool.wait_ge(T.routed, 1)
        pool.wait_ge(pad_in, 16 * (ST_TILES - 2 * NT))
        for e in range(NE):
            pool.indirect_dma_start(out=sorted_dram[:, :], out_offset=bass.IndirectOffsetOnAxis(ap=pad_i[:, e:e + 1], axis=0),
                                    in_=zero[:, e, :], in_offset=None).then_inc(T.padded, 16)
        pool.wait_ge(T.padded, 16 * NE)

    @block.scalar
    def _(act):
        act.wait_ge(stat, 5)
        act.activation(rstd[:], rstd[:], ACT.Sqrt).then_inc(std, 1)
        with act.Fori(0, NT // BLK // 2) as i:
            for u in range(2):
                act.wait_ge(tr_full, i * 4 + (2 * u + 1))
                act.activation(T.xT[:, 0, bass.ds((i * 2 + u) * S, S)], tr[:, u, 0, :], ACT.Copy).then_inc(xT_a, 1)
            for u in range(2):
                act.wait_ge(gt_full, i * 2 + (u + 1))
                act.activation(flat(score[:, bass.ds((i * 2 + u) * BLK, BLK), :]), gt[:, u, 0:BLK * NE], ACT.Sigmoid).then_inc(score_ready, 1)

    @block.tensor
    def _(pe):
        pe.wait_ge(gw_in, 16)

        def turn(n, u):
            pe.wait_ge(xn_ready, n + 1)
            for k in range(KB):
                for tt in range(BLK):
                    mm = pe.transpose(tr[:, u, k, tt * P:(tt + 1) * P], xn[:, u, tt, k * P:(k + 1) * P], T.ident[:])
                mm.then_inc(tr_full, 1)

        def logits(n, u):
            pe.wait_ge(xT_a, n + 1)
            pe.wait_ge(xT_d, n + 1)
            for k in range(KB):
                mm = pe.matmul(gp[0:NE, u, :], gw[:, k, :], T.xT[:, k, bass.ds(n * S, S)], start=(k == 0), stop=(k == KB - 1))
            mm.then_inc(gp_full, 1)

        def back(n, u):
            pe.wait_ge(gs_ready, n + 1)
            settle(pe, T.passed)
            for tt in range(BLK):
                mm = pe.transpose(gt[:, u, tt * NE:(tt + 1) * NE], gs[:, u, tt * P:(tt + 1) * P], T.ident[0:NE, 0:NE])
            mm.then_inc(gt_full, 1)

        pe.sem_inc(score_ready, CREDIT)
        with pe.Fori(0, NT // BLK // 2) as i:
            pe.wait_ge(score_ready, i * 2 + CREDIT)
            for f in (turn, logits, back):
                for u in range(2):
                    f(i * 2 + u, u)

        pe.wait_ge(consts, 6)
        pe.wait_ge(both_ready, 1)
        pe.matmul(gp[:, 0, :], before[:], both[:], start=True, stop=True).then_inc(cnt_full, 1)
        pe.matmul(gp[:, 1, :], ones[:], both[:], start=True, stop=True).then_inc(cnt_full, 1)

    @block.vector
    def _(dve):
        norm_stats(dve, T, stat, 0, 0, NT)
        dve.wait_ge(std, 1)
        dve.reciprocal(rstd[:], rstd[:]).then_inc(rs, 1)
        dve.wait_ge(rs, 1)
        with dve.Fori(0, NT // BLK // 2) as i:
            for u in range(2):
                for tt in range(BLK):
                    t = i * (2 * BLK) + (u * BLK + tt)
                    ins = dve.tensor_scalar(xn[:, u, tt, :], flat(dyn(x, t)), dyn(mean, t), dyn(rstd, t), ALU.subtract, ALU.mult)
                ins.then_inc(xn_ready, 1)
            for u in range(2):
                n = i * 2 + u
                dve.wait_ge(tr_full, n * 2 + 2)
                dve.tensor_copy(T.xT[:, 1, bass.ds(n * S, S)], tr[:, u, 1, :]).then_inc(xT_d, 1)
            for u in range(2):
                dve.wait_ge(gp_full, i * 2 + (u + 1))
                dve.tensor_copy(gs[:, u, :], gp[0:NE, u, :]).then_inc(gs_ready, 1)

        n = [0]

        def step(ins):
            n[0] += 1
            ins.then_inc(c, 1)
            dve.wait_ge(c, n[0])

        per_e = lambda a: a.unsqueeze(1).to_broadcast([P, NT, NE])
        per_t = lambda a: a.unsqueeze(2).to_broadcast([P, NT, NE])
        dve.wait_ge(consts, 6)
        dve.wait_ge(bias_in, 16)
        dve.wait_ge(score_ready, NT // BLK + CREDIT)
        step(dve.tensor_copy(desc[:], desc_i[:]))
        step(dve.tensor_copy(jt[:], jt_i[:]))
        step(dve.tensor_copy(row_f[:], row_i[:]))
        step(dve.memset(pre[:, :, 0:pad, :], 0.0))
        step(dve.memset(first[:, :, 0:NE], 0.0))
        step(dve.tensor_tensor(biased[:], score[:], per_e(bias[:]), ALU.add))
        for one, s in ((one1, T.s1), (one2, T.s2)):
            step(dve.tensor_reduce(best[:], biased[:], AX.X, ALU.max))
            step(dve.tensor_tensor(scr[:], biased[:], per_t(best[:]), ALU.is_equal))
            step(dve.tensor_tensor(scr[:], scr[:], per_e(desc[:]), ALU.mult))
            step(dve.tensor_reduce(best[:], scr[:], AX.X, ALU.max))
            step(dve.tensor_tensor(one[:], per_e(desc[:]), per_t(best[:]), ALU.is_equal))
            step(dve.tensor_tensor(scr[:], one[:], score[:], ALU.mult))
            step(dve.tensor_reduce(s[:], scr[:], AX.X, ALU.add))
            if one is one1:
                step(dve.scalar_tensor_tensor(out=biased[:], in0=one[:], scalar=-BIG, in1=biased[:], op0=ALU.mult, op1=ALU.add))
        dve.tensor_tensor(both[:], one1[:].rearrange("p t e -> p (t e)"), one2[:].rearrange("p t e -> p (t e)"), ALU.add).then_inc(both_ready, 1)
        step(dve.tensor_tensor(T.r1[:], rstd[:], T.s1[:], ALU.mult))
        step(dve.tensor_tensor(T.r2[:], rstd[:], T.s2[:], ALU.mult))
        dve.wait_ge(cnt_full, 2)
        total = gp[:, 1, :].rearrange("p (t e) -> p t e", e=NE)
        inner = gp[:, 0, :].rearrange("p (t e) -> p t e", e=NE)
        step(dve.tensor_copy(pre[:, 0, pad:, :], total))
        a, k = 0, 1
        while k < NT:
            step(dve.tensor_tensor(pre[:, 1 - a, pad:, :], pre[:, a, pad:, :], pre[:, a, pad - k:pad + NT - k, :], ALU.add))
            a, k = 1 - a, 2 * k
        step(dve.tensor_scalar(tiles_i[:], pre[:, a, pad + NT - 1, :], float(P - 1), None, ALU.add))
        step(dve.tensor_scalar(tiles_i[:], tiles_i[:], LOG2P, None, ALU.logical_shift_right))
        step(dve.tensor_copy(tiles[:], tiles_i[:]))
        step(dve.tensor_copy(first[:, 0, NE:], tiles[:]))
        f, k = 0, 1
        while k < NE:
            step(dve.tensor_tensor(first[:, 1 - f, NE:], first[:, f, NE:], first[:, f, NE - k:2 * NE - k], ALU.add))
            f, k = 1 - f, 2 * k
        ends = first[:, f, NE:]
        starts = first[:, f, NE - 1:2 * NE - 1]
        step(dve.tensor_scalar(et[:], jt[:], ends[:, 0:1], None, ALU.is_ge))
        for e in range(1, NE - 1):
            step(dve.scalar_tensor_tensor(out=et[:], in0=jt[:], scalar=ends[:, e:e + 1], in1=et[:], op0=ALU.is_ge, op1=ALU.add))
        step(dve.tensor_copy(T.expert[:], et[0:1, :]))
        step(dve.tensor_tensor(scr[:], pre[:, a, pad:, :], total, ALU.subtract))
        step(dve.tensor_tensor(scr[:], scr[:], inner, ALU.add))
        step(dve.tensor_scalar(pad_g[:], starts, float(P), None, ALU.mult))
        step(dve.tensor_tensor(biased[:], scr[:], per_e(pad_g[:]), ALU.add))
        for k, one in enumerate((one1, one2)):
            step(dve.tensor_tensor(scr[:], one[:], biased[:], ALU.mult))
            step(dve.tensor_reduce(slot_f[:], scr[:], AX.X, ALU.add))
            step(dve.tensor_copy(T.slot[:, :, k], slot_f[:]))
        step(dve.tensor_scalar(pad_f[:], ends, 1.0, float(P), ALU.subtract, ALU.mult))
        step(dve.tensor_scalar(pad_f[:], pad_f[:], row_f[:, 0:1], float(-ST_TILES * P), ALU.add, ALU.add))
        step(dve.tensor_scalar(pad_g[:], tiles[:], 0.0, None, ALU.is_equal))
        step(dve.tensor_tensor(row_f[:], row_f[:], pad_f[:], ALU.subtract))
        step(dve.tensor_tensor(row_f[:], row_f[:], pad_g[:], ALU.mult))
        step(dve.tensor_tensor(pad_f[:], pad_f[:], row_f[:], ALU.add))
        dve.tensor_copy(pad_i[:], pad_f[:]).then_inc(T.routed, 1)


def shared_expert(nc, ctx, T, sw13_dram, sw2_dram, sorted_dram):
    sb = lambda name, shape, dt=F32: ctx.enter_context(nc.sbuf_tensor(name, shape, dt))
    sem = lambda name: ctx.enter_context(nc.semaphore(name))
    x, mean = T.x, T.mean
    w13 = sb("sw13", [P, KB, 2 * HID])
    w2 = sb("sw2", [P, KB, D])
    rows = sb("rows", [P, BLK, 2, ROW])
    idx = sb("idx", [P, BLK, 2], U32)
    g = sb("s_gate", [P, KB, S])
    hT = sb("s_hT", [P, KB, S])
    up = ctx.enter_context(nc.psum_tensor("s_up", [P, KB, 2, S], F32))
    down = ctx.enter_context(nc.psum_tensor("s_down", [P, 2, 2, D], F32))
    w_in = sem("s_w_in")
    rows_ready = sem("rows_ready")
    scattered = [sem(f"scattered{k}") for k in range(BLK)]
    up_full, g_ready, h_ready, down_full, x_done = sem("up_full"), sem("g_ready"), sem("h_ready"), sem("down_full"), sem("x_done")
    NBLK = NT // BLK
    block = ctx.enter_context(nc.Block())

    @block.sync
    def _(sp):
        sp.dma_start(w13[:], sw13_dram.rearrange("(k p) n -> p k n", p=P)).then_inc(w_in, 16)
        sp.dma_start(w2[:], sw2_dram.rearrange("(k p) n -> p k n", p=P)).then_inc(w_in, 16)
        sp.wait_ge(w_in, 32)

    @block.gpsimd
    def _(pool):
        with pool.Fori(0, NBLK) as i:
            for tt in range(BLK):
                pool.wait_ge(rows_ready, i * BLK + (tt + 1))
                settle(pool, T.passed)
                for k in range(2):
                    pool.indirect_dma_start(out=sorted_dram[:, :],
                                            out_offset=bass.IndirectOffsetOnAxis(ap=idx[:, tt, k:k + 1], axis=0),
                                            in_=rows[:, tt, k, :], in_offset=None).then_inc(scattered[tt], 16)
        for tt in range(BLK):
            pool.wait_ge(scattered[tt], 32 * NBLK)

    @block.tensor
    def _(pe):
        pe.wait_ge(w_in, 32)
        pe.sem_inc(x_done, CREDIT)
        with pe.Fori(0, NBLK) as i:
            xT = T.xT[:, :, bass.ds(i * S, S)]
            for m in range(KB):
                for w in range(2):
                    for k in range(KB):
                        mm = pe.matmul(up[:, m, w, :], w13[:, k, w * HID + m * P:w * HID + (m + 1) * P], xT[:, k, :],
                                       start=(k == 0), stop=(k == KB - 1))
                    mm.then_inc(up_full, 1)
            pe.wait_ge(h_ready, i * KB + (KB + CREDIT))
            pe.wait_ge(x_done, i * 2 + CREDIT)
            for pair in range(2):
                for tt in range(2):
                    for k in range(KB):
                        mm = pe.matmul(down[:, pair, tt, :], hT[:, k, (2 * pair + tt) * P:(2 * pair + tt + 1) * P],
                                       w2[:, k, :], start=(k == 0), stop=(k == KB - 1))
                mm.then_inc(down_full, 1)

    @block.scalar
    def _(act):
        act.sem_inc(h_ready, CREDIT)
        with act.Fori(0, NBLK) as i:
            for m in range(KB):
                act.wait_ge(up_full, i * (2 * KB) + (2 * m + 1))
                act.wait_ge(h_ready, i * KB + CREDIT)
                act.activation(g[:, m, :], up[:, m, 0, :], ACT.Silu).then_inc(g_ready, 1)

    @block.vector
    def _(dve):
        for i in first_apart(dve, NBLK):
            for tt in range(BLK):
                t = i * BLK + tt
                if not isinstance(i, int):
                    dve.wait_ge(scattered[tt], i * 32)
                for k, r in enumerate((T.r1, T.r2)):
                    dve.tensor_scalar(rows[:, tt, k, 0:D], flat(dyn(x, t)), dyn(mean, t), dyn(r, t), ALU.subtract, ALU.mult)
                dve.tensor_copy(rows[:, tt, :, D:ROW].bitcast(I32).rearrange("p k a -> p (k a)"), flat(dyn(T.dest, t)))
                dve.tensor_copy(idx[:, tt, :], flat(dyn(T.slot, t))).then_inc(rows_ready, 1)
            for m in range(KB):
                dve.wait_ge(up_full, i * (2 * KB) + (2 * m + 2))
                dve.wait_ge(g_ready, i * KB + (m + 1))
                dve.tensor_tensor(hT[:, m, :], g[:, m, :], up[:, m, 1, :], ALU.mult).then_inc(h_ready, 1)
            for pair in range(2):
                dve.wait_ge(down_full, i * 2 + (pair + 1))
                dve.wait_ge(rows_ready, i * BLK + BLK)
                xs = x[:, bass.ds(i * BLK + 2 * pair, 2), :]
                dve.tensor_tensor(xs, down[:, pair], xs, ALU.add).then_inc(x_done, 1)


RING = 8


class Step:

    def __init__(self, c, i=None):
        self.c, self.i = c, i

    def times(self, k, more=0):
        return k * self.c + more if self.i is None else self.i * (RING * k) + (k * self.c + more)

    @property
    def ring(self):
        return self.c % RING

    def uses(self, k, more=0):
        v = k * (self.c // RING) + more
        return v if self.i is None else self.i * k + v

    def back(self, n):
        return Step(self.c - n, self.i)


def experts(nc, ctx, T, w13_dram, w2_dram, sorted_dram, result_dram):
    sb = lambda name, shape, dt=F32: ctx.enter_context(nc.sbuf_tensor(name, shape, dt))
    sem = lambda name: ctx.enter_context(nc.semaphore(name))
    rows = sb("e_rows", [P, RING, ROW])
    xT = sb("e_xT", [P, 2, KB, P])
    g = sb("e_gate", [P, 2, HID])
    h = sb("e_h", [P, 2, HID])
    hT = sb("e_hT", [P, 2, KB, P])
    y = sb("e_y", [P, RING, D])
    ps = lambda name, n: ctx.enter_context(nc.psum_tensor(name, [P, n, S], F32))
    px, pu, ph, py = ps("e_px", 1), ps("e_pu", 2), ps("e_ph", 1), ps("e_py", 2)
    rows_in = [sem(f"e_rows_in{k}") for k in range(RING)]
    sent = [sem(f"e_sent{k}") for k in range(RING)]
    px_full, xT_ready, pu_full, g_ready, h_ready = sem("px_full"), sem("e_xT_ready"), sem("pu_full"), sem("e_g_ready"), sem("e_h_ready")
    ph_full, hT_ready, py_full, y_ready = sem("ph_full"), sem("e_hT_ready"), sem("py_full"), sem("y_ready")
    w13, w2 = T.w13, T.w2

    LAST = ST_TILES + 3

    def steps(eng):
        for j in range(RING):
            yield Step(j)
        with eng.Fori(0, ST_TILES // RING - 1) as i:
            for u in range(RING):
                yield Step(RING + u, i)
        for j in range(ST_TILES, LAST):
            yield Step(j)

    def tile(s, lag):
        b = s.back(lag)
        return b if s.i is not None or 0 <= b.c < ST_TILES else None

    block = ctx.enter_context(nc.Block())

    @block.sync
    def _(sp):
        def load(t):
            k = t.ring
            if t.c >= RING:
                sp.wait_ge(sent[k], t.uses(16))
            settle(sp, T.passed)
            r = t.times(P)
            src = sorted_dram[r:r + P, :] if t.i is None else sorted_dram[bass.ds(r, P), :]
            sp.dma_start(rows[:, k, :], src).then_inc(rows_in[k], 16)

        for s in steps(sp):
            t = tile(s, 0)
            if t:
                load(t)

    @block.tensor
    def _(pe):
        pe.wait_ge(T.w_in, 32)
        for s in steps(pe):
            if t := tile(s, 0):
                k = t.ring
                pe.wait_ge(rows_in[k], t.uses(16, 16))
                if t.c:
                    pe.wait_ge(xT_ready, t.times(1))
                for kb in range(KB):
                    mm = pe.transpose(px[:, 0, kb * P:(kb + 1) * P], rows[:, k, kb * P:(kb + 1) * P], T.ident[:])
                mm.then_inc(px_full, 1)
            if t := tile(s, 1):
                pe.wait_ge(xT_ready, t.times(1, 1))
                if t.c >= 2:
                    pe.wait_ge(h_ready, t.times(1, -1))
                settle(pe, T.passed)
                e = pe.value_load(T.expert[0:1, bass.ds(t.times(1), 1)] if t.i is not None else T.expert[0:1, t.c:t.c + 1],
                                  min_val=0, max_val=NE - 1)
                for kb in range(KB):
                    mm = pe.matmul(pu[:, t.c % 2, :], xT[:, t.c % 2, kb, :], w13[:, bass.ds(e * KB + kb, 1), :].rearrange("p a n -> p (a n)"),
                                   start=(kb == 0), stop=(kb == KB - 1))
                mm.then_inc(pu_full, 1)
            if t := tile(s, 2):
                pe.wait_ge(h_ready, t.times(1, 1))
                if t.c:
                    pe.wait_ge(hT_ready, t.times(1))
                for kb in range(KB):
                    mm = pe.transpose(ph[:, 0, kb * P:(kb + 1) * P], h[:, t.c % 2, kb * P:(kb + 1) * P], T.ident[:])
                mm.then_inc(ph_full, 1)
            if t := tile(s, 3):
                pe.wait_ge(hT_ready, t.times(1, 1))
                if t.c >= 2:
                    pe.wait_ge(y_ready, t.times(1, -1))
                settle(pe, T.passed)
                e = pe.value_load(T.expert[0:1, bass.ds(t.times(1), 1)] if t.i is not None else T.expert[0:1, t.c:t.c + 1],
                                  min_val=0, max_val=NE - 1)
                for kb in range(KB):
                    mm = pe.matmul(py[:, t.c % 2, 0:D], hT[:, t.c % 2, kb, :], w2[:, bass.ds(e * KB + kb, 1), :].rearrange("p a n -> p (a n)"),
                                   start=(kb == 0), stop=(kb == KB - 1))
                mm.then_inc(py_full, 1)

    @block.scalar
    def _(act):
        for s in steps(act):
            if t := tile(s, 0):
                act.wait_ge(px_full, t.times(1, 1))
                if t.c >= 2:
                    act.wait_ge(pu_full, t.times(1, -1))
                act.activation(flat(xT[:, t.c % 2]), px[:, 0, 0:D], ACT.Copy).then_inc(xT_ready, 1)
            if t := tile(s, 1):
                act.wait_ge(pu_full, t.times(1, 1))
                if t.c >= 2:
                    act.wait_ge(h_ready, t.times(1, -1))
                act.activation(g[:, t.c % 2, :], pu[:, t.c % 2, 0:HID], ACT.Silu).then_inc(g_ready, 1)
            if t := tile(s, 3):
                k = t.ring
                act.wait_ge(py_full, t.times(1, 1))
                if t.c >= RING:
                    act.wait_ge(sent[k], t.uses(16))
                act.activation(y[:, k, :], py[:, t.c % 2, 0:D], ACT.Copy).then_inc(y_ready, 1)

    @block.vector
    def _(dve):
        for s in steps(dve):
            if t := tile(s, 1):
                dve.wait_ge(g_ready, t.times(1, 1))
                if t.c >= 2:
                    dve.wait_ge(ph_full, t.times(1, -1))
                dve.tensor_tensor(h[:, t.c % 2, :], g[:, t.c % 2, :], pu[:, t.c % 2, HID:2 * HID], ALU.mult).then_inc(h_ready, 1)
            if t := tile(s, 2):
                dve.wait_ge(ph_full, t.times(1, 1))
                if t.c >= 2:
                    dve.wait_ge(py_full, t.times(1, -1))
                dve.tensor_copy(flat(hT[:, t.c % 2]), ph[:, 0, 0:HID]).then_inc(hT_ready, 1)

    @block.gpsimd
    def _(pool):
        for s in steps(pool):
            if t := tile(s, 3):
                k = t.ring
                pool.wait_ge(y_ready, t.times(1, 1))
                settle(pool, T.passed)
                pool.indirect_dma_start(out=result_dram[:, :],
                                        out_offset=bass.IndirectOffsetOnAxis(ap=rows[:, k, D:ROW].bitcast(U32), axis=0),
                                        in_=y[:, k, :], in_offset=None).then_inc(sent[k], 16)
        for k in range(RING):
            pool.wait_ge(sent[k], 16 * (ST_TILES // RING))


def combine(nc, ctx, T, result_dram, out_dram):
    sb = lambda name, shape, dt=F32: ctx.enter_context(nc.sbuf_tensor(name, shape, dt))
    sem = lambda name: ctx.enter_context(nc.semaphore(name))
    RING = 4
    x = T.x
    y = sb("c_y", [P, RING, 2, BLK, D])
    y_in = [sem(f"y_in{k}") for k in range(RING)]
    half, ready, stored = sem("c_half"), sem("c_ready"), sem("c_stored")
    src = result_dram[0:RESULTS, :].rearrange("(c t p) d -> p c t d", c=2, p=P)
    dst = out_dram.rearrange("(t p) d -> p t d", p=P)
    NBLK = NT // BLK
    block = ctx.enter_context(nc.Block())

    @block.sync
    def _(sp):
        for k in range(RING):
            for c in range(2):
                sp.dma_start(y[:, k, c], src[:, c, k * BLK:(k + 1) * BLK, :]).then_inc(y_in[k], 16)
        with sp.Fori(0, NBLK // RING - 1) as i:
            for k in range(RING):
                sp.wait_ge(ready, i * (RING * BLK) + (k + 1) * BLK)
                for c in range(2):
                    sp.dma_start(y[:, k, c], src[:, c, bass.ds(i * (RING * BLK) + (RING + k) * BLK, BLK), :]).then_inc(y_in[k], 16)

    @block.vector
    def _(dve):
        with dve.Fori(0, NBLK // RING) as i:
            for k in range(RING):
                dve.wait_ge(y_in[k], i * 32 + 32)
                for c, s in enumerate((T.s1, T.s2)):
                    if c:
                        dve.wait_ge(half, i * (RING * BLK) + (k + 1) * BLK)
                    for tt in range(BLK):
                        t = i * (RING * BLK) + (k * BLK + tt)
                        xs = flat(dyn(x, t))
                        dve.scalar_tensor_tensor(out=xs, in0=y[:, k, c, tt, :], scalar=dyn(s, t), in1=xs,
                                                 op0=ALU.mult, op1=ALU.add).then_inc(ready if c else half, 1)

    @block.scalar
    def _(act):
        with act.Fori(0, NBLK) as i:
            act.wait_ge(ready, i * BLK + BLK)
            act.dma_start(dst[:, bass.ds(i * BLK, BLK), :], x[:, bass.ds(i * BLK, BLK), :]).then_inc(stored, 16)
        act.wait_ge(stored, 16 * NBLK)


def layer(nc, ins, out):
    x, wqk, wv, wo, gw, bias, w13, w2, sw13, sw2 = ins
    sorted_dram = nc.dram_tensor("sorted_rows", [PAD_TILES * P, ROW], F32, kind="Internal").ap()
    result_dram = nc.dram_tensor("results", [RESULTS + PADS * P, D], F32, kind="Internal").ap()
    with contextlib.ExitStack() as ctx:
        T = shared(nc, ctx)
        with contextlib.ExitStack() as phase:
            attention(nc, phase, T, x, wqk, wv, wo)
        routing(nc, ctx, T)
        with contextlib.ExitStack() as outer:
            T.xT = outer.enter_context(nc.sbuf_tensor("xT", [P, KB, NT * P], F32))
            with contextlib.ExitStack() as phase:
                gate(nc, phase, T, gw, bias, sorted_dram)
            with contextlib.ExitStack() as phase:
                shared_expert(nc, phase, T, sw13, sw2, sorted_dram)
        with contextlib.ExitStack() as phase:
            load_experts(nc, phase, T, w13, w2)
            experts(nc, phase, T, w13, w2, sorted_dram, result_dram)
        with contextlib.ExitStack() as phase:
            combine(nc, phase, T, result_dram, out)


def routing(nc, ctx, T):
    sb = lambda name, shape, dt=F32: ctx.enter_context(nc.sbuf_tensor(name, shape, dt))
    T.s1, T.s2 = sb("s1", [P, NT]), sb("s2", [P, NT])
    T.r1, T.r2 = sb("r1", [P, NT]), sb("r2", [P, NT])
    T.slot = sb("slot", [P, NT, 2], U32)
    T.dest = sb("dest", [P, NT, 2], I32)
    T.expert = sb("expert", [1, ST_TILES], I32)
    T.routed = ctx.enter_context(nc.semaphore("routed"))
    T.padded = ctx.enter_context(nc.semaphore("padded"))


def load_experts(nc, ctx, T, w13_dram, w2_dram):
    T.w13 = ctx.enter_context(nc.sbuf_tensor("w13_sb", [P, NE * KB, 2 * HID], F32))
    T.w2 = ctx.enter_context(nc.sbuf_tensor("w2_sb", [P, NE * KB, D], F32))
    T.w_in = ctx.enter_context(nc.semaphore("ew_in"))
    nc.sync.dma_start(T.w13[:], w13_dram.rearrange("(k p) n -> p k n", p=P)).then_inc(T.w_in, 16)
    nc.sync.dma_start(T.w2[:], w2_dram.rearrange("(k p) n -> p k n", p=P)).then_inc(T.w_in, 16)


def kernel(L0_attn_x, L0_attn_WQ, L0_attn_WK, L0_attn_WV, L0_attn_WO, L0_ffn_gate_w, L0_ffn_w1, L0_ffn_w2,
           L0_ffn_w3, L0_ffn_sw1, L0_ffn_sw2, L0_ffn_sw3, L0_ffn_expert_bias):
    import concourse.bacc as bacc
    from concourse.bass_utils import run_bass_kernel_spmd

    lay = lambda a: np.ascontiguousarray(np.asarray(a))
    WQ, WK, WV, WO, w1, w2, w3, sw1, sw2, sw3 = (
        lay(a) for a in (L0_attn_WQ, L0_attn_WK, L0_attn_WV, L0_attn_WO, L0_ffn_w1, L0_ffn_w2, L0_ffn_w3,
                         L0_ffn_sw1, L0_ffn_sw2, L0_ffn_sw3))
    wqk, wv, wo = attention_weights(WQ, WK, WV, WO)
    arrays = {
        "x": lay(L0_attn_x).reshape(NT * P, D),
        "wqk": wqk, "wv": wv, "wo": wo,
        "gate_wT": lay(lay(L0_ffn_gate_w).T),
        "expert_bias": lay(L0_ffn_expert_bias),
        "ew13": lay(np.concatenate([w1.transpose(0, 2, 1), w3.transpose(0, 2, 1)], axis=2).reshape(NE * D, 2 * HID)),
        "ew2": lay(w2.transpose(0, 2, 1).reshape(NE * HID, D)),
        "ws13": lay(np.concatenate([sw1.T, sw3.T], axis=1)),
        "ws2": lay(sw2.T),
    }
    nc = bacc.Bacc("TRN2", target_bir_lowering=False, num_devices=1)
    ins = [nc.dram_tensor(n, a.shape, F32, kind="ExternalInput").ap() for n, a in arrays.items()]
    out = nc.dram_tensor("out", [NT * P, D], F32, kind="ExternalOutput").ap()
    layer(nc, ins, out)
    got = run_bass_kernel_spmd(nc, [arrays], core_ids=[0])
    return got.results[0]["out"].reshape(NB, S, D)
```

```python
import contextlib

import numpy as np
import concourse.bass as bass
import concourse.mybir as mybir
from concourse.alu_op_type import AluOpType as ALU

F32 = mybir.dt.float32
BF16 = mybir.dt.bfloat16
I32 = mybir.dt.int32
U32 = mybir.dt.uint32
ACT = mybir.ActivationFunctionType
AX = mybir.AxisListType

P = 128
NB, S, D = 16, 512, 256
H, DH = 16, 16
TB = S // P
NT = NB * TB
KB = D // P
GH = 4
NG = H // GH
NE, HID = 8, 256
EPS = 1e-5
QSCALE = 0.25
NPROD = 6
Q_PART = (0, 0, 1, 1, 0, 2)
K_PART = (0, 1, 0, 1, 2, 0)
ROWS1 = NPROD * DH
ROWS2 = ROWS1 + 2
MASKED = -1e30

ST_TILES = 2 * NT + NE
SLOTS = ST_TILES * P


class Batch:

    def __init__(self, c, i=None):
        self.c, self.i = c, i

    def times(self, per_batch, more=0):
        v = per_batch * self.c + more
        return v if self.i is None else self.i * (2 * per_batch) + v

    first = property(lambda self: self.i is None and self.c == 0)
    last = property(lambda self: self.i is None and self.c == NB - 1)
    odd = property(lambda self: self.c % 2)
    next = property(lambda self: Batch(self.c + 1, self.i))
    prev = property(lambda self: Batch(self.c - 1, self.i))


def settle(eng, passed):
    eng.sem_inc(passed, 1)


def batches(eng):
    yield Batch(0)
    yield Batch(1)
    with eng.Fori(0, (NB - 4) // 2) as i:
        yield Batch(2, i)
        yield Batch(3, i)
    yield Batch(NB - 2)
    yield Batch(NB - 1)


TASK_PLACES = (
    (("OT", (2,)), ("Q0", (3, 5)), ("K0", (5, 7))),
    (("OT", (3,)), ("Q1", (3, 4)), ("K1", (6, 7)), ("AT0", (9,)), ("AT1", (12,))),
    (("OT", (1,)), ("V0", (2, 8)), ("V1", (9, 11))),
    (("OT", (1,)), ("WO0", (1, 4)), ("WO1", (6, 7)), ("X0", (9,)), ("X1", (10,))),
)
TASKS = tuple(tuple(t for t, _ in step) for step in TASK_PLACES)
PER_BATCH = sum(len(t) for t in TASKS)
PRO = tuple((t, 0) for t in ("X0", "X1", "Q0", "K0", "Q1", "K1", "V0", "V1")) + (("X0", 1), ("X1", 1))
OT_LAG = 2
EARLY_MAX = 7


def tasks(b, g):
    out = []
    for t in TASKS[g]:
        if t == "OT" and b.first and g < OT_LAG:
            continue
        if t[:2] in ("AT", "WO") and b.first:
            continue
        if t[0] in "QKV" and b.last:
            continue
        if t[0] == "X" and b.i is None and b.c >= NB - 2:
            continue
        out.append(t)
    return out


def misc_no(b, g, t):
    n = sum(len(tasks(b, k)) for k in range(g)) + tasks(b, g).index(t)
    if b.first:
        return len(PRO) + n
    lack = PER_BATCH - sum(len(tasks(Batch(0), k)) for k in range(NG)) + (2 if b.last else 0)
    return b.times(PER_BATCH, len(PRO) - lack + n)


def misc_bank(b, g, t):
    return misc_no(Batch(b.c), g, t) % 2


def whose(b, g, t):
    if t == "OT":
        return (b.prev, g + NG - OT_LAG) if g < OT_LAG else (b, g - OT_LAG)
    return (b.prev if t[:2] in ("AT", "WO") else b.next.next if t[0] == "X" else b.next), None


def two_before(b, g, t):
    here = [(b, k, x) for k in range(g + 1) for x in tasks(b, k)]
    here = here[:[x[1:] for x in here].index((g, t))]
    if len(here) >= 2:
        sb, k, x = here[-2]
        return x, *whose(sb, k, x)
    if b.first:
        t, n = PRO[len(here) - 2]
        return t, Batch(n), None
    prev = [(b.prev, k, x) for k in range(NG) for x in tasks(b.prev, k)]
    sb, k, x = prev[len(here) - 2]
    return x, *whose(sb, k, x)


def parts_at(b, g, u):
    return [(t, places.index(u)) for t, places in TASK_PLACES[g] if t in tasks(b, g) and u in places]


def due(b, g, u):
    return [t for t, places in TASK_PLACES[g] if t in tasks(b, g) and places[-1] + 1 == u]


def kb_place(j, kb):
    pair, i = divmod(j, 2)
    if kb == 0:
        return pair, 3 * i, 0, S
    if kb == 1:
        return pair, 3 * i + 1, P, S - P
    if kb == 3:
        return pair, 3 * i + 1, 0, P
    return pair, 2, 2 * P * i, 2 * P


PAIR_BANKS = (((0, 0),), ((0, 3), (0, 1)), ((0, 2), (1, 2)), ((1, 0),), ((1, 3), (1, 1)))
MAX_UNITS = ((0, (0, 1, 2, 3)), (1, (0, 1)), (1, (2, 3)),
             (2, (0,)), (2, (1,)), (2, (2,)), (2, (3,)),
             (3, (0,)), (3, (1,)), (3, (2,)), (3, (3,)))
NMU = len(MAX_UNITS)
U1 = NMU + 1
U2 = 10
LAG = 4
TURN = 13
MID_LAG = 3
PLACES = LAG + U2
PV_AT = (4, 6, 8, 10)
EARLY = 4


def attention(nc, ctx, T, x_dram, wqk_dram, wv_dram, wo_dram):
    sb = lambda name, shape, dt=F32: ctx.enter_context(nc.sbuf_tensor(name, shape, dt))
    sem = lambda name: ctx.enter_context(nc.semaphore(name))
    x, mean, rstd, stats = T.x, T.mean, T.rstd, T.stats

    xn = sb("xn", [P, TB, D])
    xnT = sb("xnT", [P, KB, S])
    qf = sb("qf", [P, 2, S])
    rem = sb("rem", [P, 2, S])
    part = sb("part", [P, 2, 2, 3, S], BF16)
    QS = sb("QS", [P, H, S], BF16)
    KS = sb("KS", [P, H, S], BF16)
    V = sb("V_sb", [P, 2, TB, H, 2 * DH])
    PR = sb("PR", [P, 2, 2, 5, S])
    O = sb("O_sb", [P, 2, S])
    attn = sb("attn", [P, TB, D])
    attnT = sb("attnT", [P, KB, S])
    rec = sb("rec", [P, TB, GH])
    mx = sb("mx", [P, 2, GH, TB])
    nm = sb("nm", [GH * TB, 2, 2, P], BF16)
    wqk = sb("wqk_sb", [P, KB, 2 * D])
    wv = sb("wv_sb", [P, KB, D])
    wo = sb("wo_sb", [P, KB, D])
    identb = sb("identb", [P, P], BF16)
    tri = sb("tri", [P, P], BF16)

    score = ctx.enter_context(nc.psum_tensor("score", [P, 3, S], F32))
    logit = ctx.enter_context(nc.psum_tensor("logit", [P, 2, S], F32))
    opsum = ctx.enter_context(nc.psum_tensor("opsum", [P, S], F32))
    misc = ctx.enter_context(nc.psum_tensor("misc", [P, 2, S], F32))

    x_in = [sem(f"x_in{q}") for q in range(4)]
    w_in = sem("w_in")
    const_a, const_ready = sem("const_a"), sem("const_ready")
    stat_ready, std_ready, rstd_ready = sem("stat_ready"), sem("std_ready"), sem("rstd_ready")
    xn_ready = sem("xn_ready")
    misc_full = sem("misc_full")
    misc_free = [sem("misc_free0"), sem("misc_free1")]
    qf_ready, rem_ready, mid_ready, parts_ready = sem("qf_ready"), sem("rem_ready"), sem("mid_ready"), sem("parts_ready")
    high_ready = sem("high_ready")
    stacked = [sem("stacked0"), sem("stacked1")]
    max_full, max_free = sem("max_full"), sem("max_free")
    nm_high = sem("nm_high")
    nm_ready = sem("nm_ready")
    nm_in = [sem("nm_in0"), sem("nm_in1")]
    logit_full, logit_free = sem("logit_full"), sem("logit_free")
    masked = sem("masked")
    o_full, o_free = sem("o_full"), sem("o_free")
    rec_ready, attn_ready = sem("rec_ready"), sem("attn_ready")
    v_ready, xnT_ready, attnT_ready = sem("v_ready"), sem("xnT_ready"), sem("attnT_ready")
    x_out = sem("x_out")
    ones_ready = sem("ones_ready")

    xv = x_dram.rearrange("(n p) d -> p n d", p=P)
    block = ctx.enter_context(nc.Block())
    HALF = (("Q0", "K0"), ("Q1", "K1"))

    def proj(t):
        half, qk = int(t[1]), "QK".index(t[0])
        return half, qk, 2 * half + qk

    TAIL = misc_no(Batch(NB - 1), 3, tasks(Batch(NB - 1), 3)[-1]) + 1
    TAIL_AT = TAIL + 2
    TAIL_USES = len(tasks(Batch(NB - 1), NG - 1))

    @block.sync
    def _(sp):
        q = NT // 4
        sp.dma_start(x[:, 0:q, :], xv[:, 0:q, :]).then_inc(x_in[0], 16)
        sp.dma_start(wqk[:], wqk_dram.rearrange("(k p) n -> p k n", p=P)).then_inc(w_in, 16)
        sp.dma_start(wv[:], wv_dram.rearrange("(k p) n -> p k n", p=P)).then_inc(w_in, 16)
        sp.dma_start(wo[:], wo_dram.rearrange("(k p) n -> p k n", p=P)).then_inc(w_in, 16)
        for k in range(1, 4):
            sp.dma_start(x[:, q * k:q * (k + 1), :], xv[:, q * k:q * (k + 1), :]).then_inc(x_in[k], 16)

        def stack(b, half):
            for s in (parts_ready, high_ready, mid_ready):
                sp.wait_ge(s, b.times(4, 2 * half + 2))
            settle(sp, T.passed)
            if not b.first:
                sp.wait_ge(logit_full, b.prev.times(NG * U2, (2 * half + 2) * U2))
            for qk, (dst, order) in enumerate(((QS, Q_PART), (KS, K_PART))):
                for r in range(NPROD):
                    src = part[:, half, qk, order[r], :]
                    sp.dma_start(dst[DH * r:DH * r + DH, 8 * half:8 * half + 8, :], src).then_inc(stacked[half], 16)

        def maxima(b, g):
            par = g % 2
            sp.wait_ge(nm_ready, b.times(NG, g + 1))
            for k in range(2):
                dst = QS[ROWS1 + k:ROWS1 + k + 1, GH * g:GH * g + GH, :].rearrange("p h (t q) -> p h t q", t=TB)
                sp.dma_start(dst, nm[:, par, k, :]).then_inc(nm_in[par], 16)

        stack(Batch(0), 0)
        stack(Batch(0), 1)
        maxima(Batch(0), 0)
        for b in batches(sp):
            if not b.first:
                stack(b, 1)
            maxima(b, 1)
            maxima(b, 2)
            if not b.last:
                stack(b.next, 0)
            maxima(b, 3)
            if not b.last:
                maxima(b.next, 0)

    @block.gpsimd
    def _(pool):
        ident = T.ident
        pool.memset(ident[:], 0.0).then_inc(const_a, 1)
        pool.memset(identb[:], 0.0).then_inc(const_a, 1)
        pool.memset(tri[:], 0.0).then_inc(const_a, 1)
        pool.memset(V[:, :, :, :, DH:], 1.0).then_inc(ones_ready, 1)
        pool.wait_ge(const_a, 3)
        for a in (ident, identb):
            pool.affine_select(out=a[:], in_=a[:], compare_op=ALU.not_equal, fill=1.0, base=0,
                               pattern=[[-1, P]], channel_multiplier=1).then_inc(const_ready, 1)
        pool.affine_select(out=tri[:], in_=tri[:], compare_op=ALU.is_ge, fill=MASKED, base=0,
                           pattern=[[-1, P]], channel_multiplier=1).then_inc(const_ready, 1)

        def split_rem(b, t):
            half, qk, n = proj(t)
            pool.wait_ge(high_ready, b.times(4, n + 1))
            if not (b.first and n < 2):
                pool.wait_ge(parts_ready, b.times(4, n - 1))
            pool.tensor_tensor(rem[:, n % 2, :], qf[:, n % 2, :], part[:, half, qk, 0, :], ALU.subtract).then_inc(rem_ready, 1)

        def split_low(b, t):
            half, qk, n = proj(t)
            pool.wait_ge(mid_ready, b.times(4, n + 1))
            pool.tensor_tensor(part[:, half, qk, 2, :], rem[:, n % 2, :], part[:, half, qk, 1, :], ALU.subtract).then_inc(parts_ready, 1)

        def mask_pair(b, g, pair):
            pool.wait_ge(logit_free, b.times(NG * U2, g * U2 + 5 * pair + 5))
            settle(pool, T.passed)
            blocks = PR[:, g % 2, pair].rearrange("p k (c q) -> p (k c) q", q=P)
            sels = (blocks[:, 0:20:4, :], blocks[:, 5:18:12, :], blocks[:, 10, :])
            for k, v in enumerate(sels):
                pool.affine_select(out=v, in_=v, compare_op=ALU.is_ge, fill=0.0, base=0,
                                   pattern=([[0, v.shape[1]]] if k < 2 else []) + [[1, P]], channel_multiplier=-1).then_inc(masked, 1)

        for t, _ in PRO:
            if t[0] in "QK":
                split_rem(Batch(0), t)
                split_low(Batch(0), t)
        for b in batches(pool):
            for g in range(NG):
                split = [t for t in tasks(b, g) if t[0] in "QK"]
                for t in split:
                    split_rem(b.next, t)
                for t in split[:1]:
                    split_low(b.next, t)
                mask_pair(b, g, 0)
                for t in split[1:]:
                    split_low(b.next, t)
                mask_pair(b, g, 1)

    @block.scalar
    def _(act):
        def root(part):
            lo, hi = (0, EARLY * TB) if part == 0 else (EARLY * TB, NT)
            act.wait_ge(stat_ready, 5 * (part + 1))
            act.activation(rstd[:, lo:hi], rstd[:, lo:hi], ACT.Sqrt).then_inc(std_ready, 1)

        root(0)

        def evac(b, t, n, bank):
            if t[:2] in ("OT", "WO"):
                return
            src = misc[:, bank, :]
            act.wait_ge(misc_full, n + 1)
            if t[0] == "X":
                act.activation(xnT[:, int(t[1]), :], src, ACT.Copy).then_inc(xnT_ready, 1)
            elif t[0] in "QK":
                half, qk, k = proj(t)
                if not (b.first and k < 2):
                    act.wait_ge(parts_ready, b.times(4, k - 1))
                if not b.first:
                    act.wait_ge(stacked[half], b.times(16 * 2 * NPROD))
                act.activation(qf[:, k % 2, :], src, ACT.Copy, scale=QSCALE if qk == 0 else 1.0).then_inc(qf_ready, 1)
                act.wait_ge(qf_ready, b.times(4, k + 1))
                act.activation(part[:, half, qk, 0, :], qf[:, k % 2, :], ACT.Copy).then_inc(high_ready, 1)
            elif t[0] == "V":
                i = int(t[1])
                act.activation(V[:, b.odd, 2 * i:2 * i + 2, :, 0:DH],
                               src.rearrange("p (t h d) -> p t h d", t=2, h=H), ACT.Copy).then_inc(v_ready, 1)
            elif t[:2] == "AT":
                act.activation(attnT[:, int(t[2]), :], src, ACT.Copy).then_inc(attnT_ready, 1)

        def step(b, g):
            for u in range(PLACES):
                if u >= LAG:
                    n = g * U2 + u - LAG
                    act.wait_ge(logit_full, b.times(NG * U2, n + 1))
                    if u == LAG and not (b.first and g < 2):
                        act.wait_ge(o_full, b.times(NG, g - 1))
                    act.activation(PR[:, g % 2, (u - LAG) // 5, (u - LAG) % 5, :], logit[:, n % 2, :], ACT.Exp).then_inc(logit_free, 1)
                for t in due(b, g, u):
                    evac(whose(b, g, t)[0], t, misc_no(b, g, t), misc_bank(b, g, t))
            if not (b.first and g == 0):
                evac_o(b, g - 1)

        def evac_o(b, g):
            act.wait_ge(o_full, b.times(NG, g + 1))
            if not (b.first and g < 2):
                act.wait_ge(rec_ready, b.times(NG, g - 1))
            act.activation(O[:, g % 2, :], opsum[:], ACT.Copy).then_inc(o_free, 1)

        for n, (t, k) in enumerate(PRO):
            evac(Batch(k), t, n, n % 2)
        for b in batches(act):
            for g in range(NG):
                step(b, g)
                if b.first and g == NG - 1:
                    root(1)
        last = Batch(NB)
        evac_o(last, -1)
        for k in range(2):
            n = TAIL_AT + k
            evac(last.prev, f"AT{k}", n, n % 2)

    @block.tensor
    def _(pe):
        ident = T.ident

        def emptied(kind, who, g):
            if kind[0] == "X":
                return xnT_ready, who.times(2, int(kind[1]) + 1)
            if kind[0] in "QK":
                return qf_ready, who.times(4, proj(kind)[2] + 1)
            if kind[0] == "V":
                return v_ready, who.times(2, int(kind[1]) + 1)
            if kind == "OT":
                return attn_ready, who.times(NG, g + 1)
            if kind[:2] == "AT":
                return attnT_ready, who.times(2, int(kind[2]) + 1)
            return x_out, who.times(2, int(kind[2]) + 1)

        def do(t, b, g, k, before, part=None):
            bank = misc[:, k, :]
            if before and not part:
                pe.wait_ge(*emptied(*before))
            if t[0] == "X":
                k = int(t[1])
                pe.wait_ge(xn_ready, b.times(TB, TB))
                for tt in range(TB):
                    mm = pe.transpose(bank[:, tt * P:(tt + 1) * P], xn[:, tt, k * P:(k + 1) * P], ident[:])
            elif t[0] in "QK":
                half, qk, _ = proj(t)
                if not part:
                    pe.wait_ge(xnT_ready, b.times(2, 2))
                m = 2 * qk + half
                for k in range(KB) if part is None else (part,):
                    mm = pe.matmul(bank, wqk[:, k, m * P:(m + 1) * P], xnT[:, k, :], start=(k == 0), stop=(k == KB - 1))
            elif t == "OT":
                pe.wait_ge(o_free, b.times(NG, g + 1))
                for tt in range(TB):
                    mm = pe.transpose(bank[:, tt * P:(tt + 1) * P], O[:, g % 2, tt * P:(tt + 1) * P], ident[:])
            elif t[:2] == "AT":
                k = int(t[2])
                pe.wait_ge(attn_ready, b.times(NG, NG))
                for tt in range(TB):
                    mm = pe.transpose(bank[:, tt * P:(tt + 1) * P], attn[:, tt, k * P:(k + 1) * P], ident[:])
            else:
                src, w = (xnT, wv) if t[0] == "V" else (attnT, wo)
                if not part:
                    pe.wait_ge(xnT_ready if t[0] == "V" else attnT_ready, b.times(2, 2))
                for tt in range(2) if part is None else (part,):
                    tile = 2 * int(t[-1]) + tt
                    for k in range(KB):
                        mm = pe.matmul(bank[:, tt * D:(tt + 1) * D], src[:, k, tile * P:(tile + 1) * P], w[:, k, :],
                                       start=(k == 0), stop=(k == KB - 1))
            if part is None or part == 1:
                mm.then_inc(misc_full, 1)

        def max_unit(b, g, u):
            n = g * U1 + u
            if not (b.first and n < 3):
                pe.wait_ge(max_free, b.times(NG * U1, n - 2))
            if u == 0 and g % 2 == 0:
                pe.wait_ge(stacked[g // 2], b.times(16 * 2 * NPROD, 16 * 2 * NPROD))
            bank = score[:, n % 3, :]
            qt, heads = MAX_UNITS[u]
            cols = (qt + 1) * P
            for k, j in enumerate(heads):
                h = GH * g + j
                out = bank[:, k * cols:(k + 1) * cols]
                pe.matmul(out, QS[0:ROWS1, h, qt * P:(qt + 1) * P], KS[0:ROWS1, h, 0:cols], start=True, stop=False)
                mm = pe.matmul(out[:, cols - P:cols], identb[:], tri[:], start=False, stop=True)
            mm.then_inc(max_full, 1)

        def max_turn(b, g):
            n = g * U1 + NMU
            pe.wait_ge(max_free, b.times(NG * U1, n))
            pe.transpose(score[0:GH * TB, n % 3, 0:P], mx[:, g % 2].rearrange("p j t -> p (j t)"), ident[:]).then_inc(max_full, 1)

        def logit_unit(b, g, u):
            n = g * U2 + u
            if not (b.first and n < 2):
                pe.wait_ge(logit_free, b.times(NG * U2, n - 1))
            if u == 0:
                pe.wait_ge(nm_in[g % 2], b.times(64, 32 * (g // 2) + 32))
            pair = u // 5
            for i, kb in PAIR_BANKS[u % 5]:
                j = 2 * pair + i
                _, _, off, cols = kb_place(j, kb)
                h = GH * g + j
                mm = pe.matmul(logit[:, n % 2, off:off + cols], KS[0:ROWS2, h, kb * P:(kb + 1) * P],
                               QS[0:ROWS2, h, kb * P:S], start=True, stop=True)
            mm.then_inc(logit_full, 1)

        def pv(b, g, kb):
            if kb == 0:
                if not (b.first and g == 0):
                    pe.wait_ge(o_free, b.times(NG, g))
                pe.wait_ge(masked, b.times(NG * 6, 6 * g + 6))
                pe.wait_ge(v_ready, b.times(2, 2))
            for j in range(GH):
                pair, bank, off, cols = kb_place(j, kb)
                mm = pe.matmul(opsum[32 * j:32 * j + 32, kb * P:S], V[:, b.odd, kb, GH * g + j, :],
                               PR[:, g % 2, pair, bank, off:off + cols], start=(kb == 0), stop=(kb == TB - 1))
            if kb == TB - 1:
                mm.then_inc(o_full, 1)

        pe.wait_ge(const_ready, 3)
        pe.wait_ge(ones_ready, 2)
        pe.wait_ge(w_in, 48)
        for n, (t, k) in enumerate(PRO):
            do(t, Batch(k), None, n % 2, (PRO[n - 2][0], Batch(PRO[n - 2][1]), None) if n >= 2 else None)
            if n == EARLY_MAX:
                for u in range(NMU):
                    max_unit(Batch(0), 0, u)
                max_turn(Batch(0), 0)
        for b in batches(pe):
            for g in range(NG):
                ahead = None if b.last and g == NG - 1 else (b, g + 1) if g < NG - 1 else (b.next, 0)
                before = (b, g - 1) if g else None if b.first else (b.prev, NG - 1)
                for u in range(PLACES):
                    if ahead and u < NMU:
                        max_unit(*ahead, u)
                    if ahead and u == TURN:
                        max_turn(*ahead)
                    if u >= LAG:
                        logit_unit(b, g, u - LAG)
                    for t, k in parts_at(b, g, u):
                        whole = t[:2] in ("OT", "AT", "X0", "X1")
                        do(t, *whose(b, g, t), misc_bank(b, g, t), two_before(b, g, t), None if whole else k)
                    if before and u in PV_AT:
                        pv(*before, PV_AT.index(u))
        last = Batch(NB - 1)
        end = [(x, *whose(last, NG - 1, x)) for x in tasks(last, NG - 1)]
        for t, g in (("OT", 2), ("OT", 3), ("AT0", None), ("AT1", None), ("WO0", None), ("WO1", None)):
            if (t, g) == ("OT", 3):
                for kb in range(TB):
                    pv(last, NG - 1, kb)
            do(t, last, g, (TAIL + len(end) - TAIL_USES) % 2, end[-2])
            end.append((t, last, g))

    @block.vector
    def _(dve):
        dve.memset(KS[ROWS1:P, :, :], 1.0).then_inc(ones_ready, 1)
        def statistics(tiles_done, n):
            with dve.Fori(0, n) as i:
                for k in range(TB):
                    t = i * TB + (tiles_done + k)
                    dve.bn_stats(flat(dyn(stats, t)), flat(dyn(x, t))).then_inc(T.bn, 1)

        def deviations(part):
            lo, hi = (0, EARLY * TB) if part == 0 else (EARLY * TB, NT)
            dve.wait_ge(T.bn, hi)
            norm_stats(dve, T, stat_ready, 5 * part, lo, hi)

        def invert(part):
            lo, hi = (0, EARLY * TB) if part == 0 else (EARLY * TB, NT)
            dve.wait_ge(std_ready, part + 1)
            dve.reciprocal(rstd[:, lo:hi], rstd[:, lo:hi]).then_inc(rstd_ready, 1)
            dve.wait_ge(rstd_ready, part + 1)

        dve.wait_ge(x_in[0], 16)
        statistics(0, EARLY)
        deviations(0)
        invert(0)

        def norm(b):
            if not b.first:
                dve.wait_ge(xnT_ready, b.times(2))
            for tt in range(TB):
                t = b.times(TB, tt)
                sl = (lambda a: a[:, t:t + 1]) if b.i is None else (lambda a: a[:, bass.ds(t, 1)])
                xin = (x[:, t, :] if b.i is None else x[:, bass.ds(t, 1), :].rearrange("p a d -> p (a d)"))
                dve.tensor_scalar(xn[:, tt, :], xin, sl(mean), sl(rstd), ALU.subtract, ALU.mult).then_inc(xn_ready, 1)

        def reduce_max(b, g, u):
            n = g * U1 + u
            qt, heads = MAX_UNITS[u]
            cols = (qt + 1) * P
            dve.wait_ge(max_full, b.times(NG * U1, n + 1))
            dve.tensor_reduce(mx[:, g % 2, heads[0]:heads[0] + len(heads), qt],
                              score[:, n % 3, 0:cols * len(heads)].rearrange("p (j k) -> p j k", k=cols),
                              AX.X, ALU.max).then_inc(max_free, 1)

        def max_parts(b, g):
            n = g * U1 + NMU
            dve.wait_ge(max_full, b.times(NG * U1, n + 1))
            if not (b.first and g < 2):
                dve.wait_ge(nm_in[g % 2], b.times(64, 32 * (g // 2)))
            src = score[0:GH * TB, n % 3, 0:P]
            dve.tensor_scalar(nm[:, g % 2, 0, :], src, -1.0, None, ALU.mult).then_inc(nm_high, 1)
            dve.wait_ge(nm_high, b.times(NG, g + 1))
            dve.scalar_tensor_tensor(out=nm[:, g % 2, 1, :], in0=src, scalar=-1.0, in1=nm[:, g % 2, 0, :],
                                     op0=ALU.mult, op1=ALU.subtract).then_inc(nm_ready, 1)
            dve.wait_ge(nm_ready, b.times(NG, g + 1))
            dve.sem_inc(max_free, 1)

        def split_mid(b, t):
            half, qk, n = proj(t)
            dve.wait_ge(rem_ready, b.times(4, n + 1))
            dve.tensor_copy(part[:, half, qk, 1, :], rem[:, n % 2, :]).then_inc(mid_ready, 1)

        def scale_out(b, g, n, bank):
            v = misc[:, bank, :].rearrange("p (t j c) -> p t j c", t=TB, j=GH)
            dve.wait_ge(misc_full, n + 1)
            if g == 0 and not b.first:
                dve.wait_ge(attnT_ready, b.times(2))
            if not (b.first and g == 0):
                dve.wait_ge(attn_ready, b.times(NG, g))
            dve.reciprocal(rec[:], v[:, :, :, DH]).then_inc(rec_ready, 1)
            dve.wait_ge(rec_ready, b.times(NG, g + 1))
            out = attn[:, :, GH * DH * g:GH * DH * (g + 1)].rearrange("p t (j c) -> p t j c", j=GH)
            dve.tensor_tensor(out, v[:, :, :, 0:DH], rec[:].unsqueeze(3).to_broadcast([P, TB, GH, DH]), ALU.mult).then_inc(attn_ready, 1)

        def add_out(b, k, n, bank):
            dve.wait_ge(misc_full, n + 1)
            t0 = b.times(TB, 2 * k)
            xs = x[:, t0:t0 + 2, :] if b.i is None else x[:, bass.ds(t0, 2), :]
            dve.tensor_tensor(xs, misc[:, bank, :].rearrange("p (t d) -> p t d", t=2), xs, ALU.add).then_inc(x_out, 1)
            dve.wait_ge(x_out, b.times(2, k + 1))
            for i in range(2):
                t = b.times(TB, 2 * k + i)
                if b.i is None:
                    dve.bn_stats(stats[:, t, :], x[:, t, :]).then_inc(T.bn, 1)
                else:
                    dve.bn_stats(stats[:, bass.ds(t, 1), :].rearrange("p a s -> p (a s)"),
                                 x[:, bass.ds(t, 1), :].rearrange("p a d -> p (a d)")).then_inc(T.bn, 1)

        def empty(t, b, g, n, bank):
            if t == "OT":
                scale_out(b, g, n, bank)
            elif t[:2] == "WO":
                add_out(b, int(t[2]), n, bank)

        def maxima(b, g):
            for u in range(NMU):
                reduce_max(b, g, u)
            max_parts(b, g)

        norm(Batch(0))
        for n, (t, _) in enumerate(PRO):
            if t[0] in "QK":
                split_mid(Batch(0), t)
            if t == "X1" and n == 1:
                norm(Batch(1))
            if n == EARLY_MAX:
                maxima(Batch(0), 0)
        for b in batches(dve):
            for g in range(NG):
                ahead = None if b.last and g == NG - 1 else (b, g + 1) if g < NG - 1 else (b.next, 0)
                for u in range(PLACES):
                    if ahead and u < NMU:
                        reduce_max(*ahead, u)
                    for t in due(b, g, u):
                        empty(t, *whose(b, g, t), misc_no(b, g, t), misc_bank(b, g, t))
                    for t in due(b, g, u - MID_LAG):
                        if t[0] in "QK":
                            split_mid(whose(b, g, t)[0], t)
                    if ahead and u == TURN:
                        max_parts(*ahead)
                if b.first:
                    if g < 3:
                        dve.wait_ge(x_in[g + 1], 16)
                    more = (NB - EARLY) // NG
                    statistics((EARLY + more * g) * TB, more)
                    if g == NG - 1:
                        deviations(1)
                if b.i is None and b.c == 1 and g == 0:
                    invert(1)
                if g == 1 and not (b.i is None and b.c >= NB - 2):
                    norm(b.next.next)
        last = Batch(NB - 1)
        for k, g in enumerate((2, 3)):
            scale_out(last, g, TAIL + k, (TAIL + k) % 2)
        for k in range(2):
            add_out(last, k, TAIL_AT + 2 + k, (TAIL_AT + 2 + k) % 2)


def norm_stats(dve, T, done, had, lo, hi):
    s, mean, rstd, tmp = T.stats[:, lo:hi], T.mean[:, lo:hi], T.rstd[:, lo:hi], T.tmp[:, lo:hi]
    n = T.norm_steps
    dve.tensor_tensor(mean, s[:, :, 1], s[:, :, 4], ALU.add).then_inc(done, 1)
    dve.tensor_tensor(tmp, s[:, :, 1], s[:, :, 4], ALU.subtract).then_inc(done, 1)
    dve.tensor_tensor(rstd, s[:, :, 2], s[:, :, 5], ALU.add).then_inc(done, 1)
    dve.wait_ge(done, had + 3)
    dve.tensor_scalar(mean, mean, 0.5, None, ALU.mult).then_inc(n, 1)
    dve.tensor_tensor(tmp, tmp, tmp, ALU.mult).then_inc(n, 1)
    dve.tensor_scalar(rstd, rstd, 1.0 / D, EPS, ALU.mult, ALU.add).then_inc(n, 1)
    T.norm_done += 3
    dve.wait_ge(n, T.norm_done)
    dve.scalar_tensor_tensor(out=rstd, in0=tmp, scalar=0.25, in1=rstd, op0=ALU.mult, op1=ALU.add).then_inc(done, 2)


class Tensors:
    pass


def shared(nc, ctx):
    T = Tensors()
    sb = lambda name, shape, dt=F32: ctx.enter_context(nc.sbuf_tensor(name, shape, dt))
    T.x = sb("x_sb", [P, NT, D])
    T.mean, T.rstd, T.tmp = (sb(n, [P, NT]) for n in ("mean", "rstd", "tmp"))
    T.stats = sb("stats", [P, NT, 6])
    T.ident = sb("ident", [P, P])
    T.bn = ctx.enter_context(nc.semaphore("bn"))
    T.norm_steps = ctx.enter_context(nc.semaphore("norm_steps"))
    T.norm_done = 0
    T.passed = ctx.enter_context(nc.semaphore("passed"))
    return T


def attention_weights(WQ, WK, WV, WO):
    def cols(w):
        return w.reshape(2, H // 2, DH, D).transpose(3, 0, 2, 1).reshape(D, D)
    wqk = np.concatenate([cols(WQ), cols(WK)], axis=1)
    return (np.ascontiguousarray(wqk), np.ascontiguousarray(WV.reshape(H * DH, D).T),
            np.ascontiguousarray(WO.transpose(0, 2, 1).reshape(H * DH, D)))


BLK = 4
PAD_TILES = ST_TILES + NE
ROW = D + 2
PADS = 2 * NE
BIG = 1e30
NBLK = NT // BLK
STRIP = 32
APART = 4
ROUND = 3
LOG2P = 7


CREDIT = 1


def first_apart(eng, n):
    yield 0
    with eng.Fori(1, n) as i:
        yield i


def dyn(a, start, n=1):
    return a[:, bass.ds(start, n)]


def flat(a):
    return a.rearrange("p a b -> p (a b)")


def blocks(eng):
    return first_apart(eng, (NBLK - APART) // ROUND)


def after(eng, semaphore, value):
    if not isinstance(value, int) or value > 0:
        eng.wait_ge(semaphore, value)


def front(nc, ctx, T, gw_dram, bias_dram, sw13_dram, sw2_dram, ew_dram, sorted_dram, out_dram):
    sb = lambda name, shape, dt=F32: ctx.enter_context(nc.sbuf_tensor(name, shape, dt))
    sem = lambda name: ctx.enter_context(nc.semaphore(name))
    x, mean, rstd, big = T.x, T.mean, T.rstd, T.big
    gw = sb("gw", [P, KB, STRIP])
    gs = sb("gs", [P, 2, P])
    score = sb("gate_score", [P, NT, NE])
    rows = sb("rows", [P, 2, BLK, 2, ROW])
    xn = rows[:, :, :, 0, 0:D]
    idx = sb("idx", [P, 2, BLK, 2], U32)
    w13 = sb("sw13", [P, KB, 2 * HID])
    w2 = sb("sw2", [P, KB, D])
    turned = sb("turned", [P, 2, KB, S])
    g, hT = turned[:, 0], turned[:, 1]
    sums = sb("sums", [P, ROUND, BLK, D])
    four = ctx.enter_context(nc.psum_tensor("four", [P, 2, KB, S], F32))
    gp = ctx.enter_context(nc.psum_tensor("gp", [P, 2, S], F32))
    two = ctx.enter_context(nc.psum_tensor("two", [P, 2, S], F32))
    tr, up = four, four
    gt = two
    down = two[:].rearrange("p a (b d) -> p a b d", b=2)
    gw_in, pad_in, bias_in, zeroed = sem("gw_in"), sem("pad_in"), sem("bias_in"), sem("zeroed")
    gw_zero = sem("gw_zero")
    stat, std, rs = sem("g_stat"), sem("g_std"), sem("g_rstd")
    xn_ready, tr_full, xT_ready = sem("g_xn"), sem("g_tr_full"), sem("g_xT")
    big_ready = [sem("big_ready0"), sem("big_ready1")]
    gp_full, gs_ready, gt_full, logits_ready, score_ready = sem("gp_full"), sem("gs_ready"), sem("gt_full"), sem("logits_ready"), sem("score_ready")
    zero_ready = sem("zero_ready")
    zero = sb("zero", [P, NE, ROW])

    desc = sb("desc", [P, NE])
    desc_i = sb("desc_i", [P, NE], I32)
    bias = sb("bias", [P, NE])
    biased = sb("biased", [P, NT, NE])
    one1 = sb("one1", [P, NT, NE])
    one2 = sb("one2", [P, NT, NE])
    scr = sb("scr", [P, NT, NE])
    both = sb("both", [P, NT * NE], BF16)
    best = sb("best", [P, NT])
    before = sb("before", [P, P], BF16)
    ones = sb("ones_b", [P, P], BF16)
    pad = NT // 2
    pre = sb("pre", [P, 2, pad + NT, NE])
    tiles = sb("tiles", [P, NE])
    tiles_i = sb("tiles_i", [P, NE], I32)
    first = sb("first", [P, 2, NE + NE])
    jt = sb("jt", [1, ST_TILES])
    jt_i = sb("jt_i", [1, ST_TILES], I32)
    past = pre[0:1].rearrange("p a t e -> p (a t e)")[:, 0:ST_TILES * (NE - 1)].rearrange("p (t e) -> p t e", e=NE - 1)
    et = sb("et", [1, ST_TILES])
    slot_f = sb("slot_f", [P, NT])
    pad_f = sb("pad_f", [P, NE])
    pad_g = sb("pad_g", [P, NE])
    pad_i = sb("pad_i", [P, NE], U32)
    row_i = sb("row_i", [P, NE], I32)
    row_f = sb("row_f", [P, NE])
    c = sem("route")
    consts, both_ready, cnt_full = sem("g_consts"), sem("both_ready"), sem("cnt_full")
    ca = sem("g_const_a")

    w_in = sem("s_w_in")
    stored = [sem(f"stored{k}") for k in range(ROUND)]
    rows_ready = sem("rows_ready")
    scattered = [sem(f"scattered{k}") for k in range(2 * BLK)]
    up_full, g_ready, h_ready, down_full, sum_ready = sem("up_full"), sem("g_ready"), sem("h_ready"), sem("down_full"), sem("sum_ready")
    NPAIR = NBLK // 2
    CREDIT2 = 2

    block = ctx.enter_context(nc.Block())

    @block.sync
    def _(sp):
        sp.dma_start(bias[:], bias_dram.rearrange("(a n) -> a n", a=1).partition_broadcast(P)).then_inc(bias_in, 16)
        sp.dma_start(w13[:], sw13_dram.rearrange("(k p) n -> p k n", p=P)).then_inc(w_in, 16)
        sp.dma_start(w2[:], sw2_dram.rearrange("(k p) n -> p k n", p=P)).then_inc(w_in, 16)
        sp.wait_ge(gw_zero, 1)
        sp.dma_start(gw[:, :, 0:NE], gw_dram.rearrange("(k p) n -> p k n", p=P)).then_inc(gw_in, 16)
        sp.wait_ge(zero_ready, 2)
        for t in range(2 * NT, ST_TILES):
            sp.dma_start(sorted_dram[t * P:(t + 1) * P, :], zero[:, t - 2 * NT, :]).then_inc(pad_in, 16)
        for k in range(2):
            r = (NT + k * NE) * P
            sp.dma_start(out_dram[r:r + NE * P, :].rearrange("(k p) d -> p k d", p=P), zero[:, :, 0:D]).then_inc(zeroed, 16)
        dst = out_dram[0:NT * P, :].rearrange("(t p) d -> p t d", p=P)

        def store(i, place):
            sp.wait_ge(sum_ready, i * 2 + 2)
            sp.dma_start(dyn(dst, i * BLK, BLK), sums[:, place]).then_inc(stored[place], 16)

        def weights(k):
            sp.dma_start(dyn(big, k * KB, KB), ew_dram[bass.ds(k * P, P), :].rearrange("p (a n) -> p a n", a=KB)).then_inc(T.w_in, 16)

        for i in range(APART):
            store(i, i % ROUND)
            weights(i)
        for j in blocks(sp):
            for u in range(ROUND):
                store(j * ROUND + (APART + u), (APART + u) % ROUND)
            for u in range(2):
                weights(j * 2 + (APART + u))
        sp.wait_ge(zeroed, 32)
        for place in range(ROUND):
            sp.wait_ge(stored[place], 16 * len(range(place, NBLK, ROUND)))

    @block.gpsimd
    def _(pool):
        pool.memset(gw[:], 0.0).then_inc(gw_zero, 1)
        pool.memset(before[:], 1.0).then_inc(ca, 1)
        pool.memset(ones[:], 1.0).then_inc(consts, 1)
        pool.memset(zero[:], 0.0).then_inc(zero_ready, 1)
        pool.wait_ge(zero_ready, 1)
        number = zero[:, :, D:D + 1].bitcast(I32).rearrange("p k a -> p (k a)")
        pool.iota(number, pattern=[[P, NE]], base=(NT + NE) * P, channel_multiplier=1).then_inc(zero_ready, 1)
        pool.iota(desc_i[:], pattern=[[-1, NE]], base=NE, channel_multiplier=0).then_inc(consts, 1)
        pool.iota(jt_i[:], pattern=[[1, ST_TILES]], base=0, channel_multiplier=0).then_inc(consts, 1)
        pool.iota(row_i[:], pattern=[[P, NE]], base=ST_TILES * P, channel_multiplier=1).then_inc(consts, 1)
        pool.iota(T.dest[:], pattern=[[P, NT], [0, 2]], base=0, channel_multiplier=1).then_inc(consts, 1)
        pool.wait_ge(ca, 1)
        pool.affine_select(out=before[:], in_=before[:], compare_op=ALU.is_gt, fill=0.0, base=0,
                           pattern=[[1, P]], channel_multiplier=-1).then_inc(consts, 1)
        with pool.Fori(0, NPAIR) as i:
            for u in range(2):
                pool.wait_ge(xT_ready, i * 4 + (2 * u + 1))
                settle(pool, T.passed)
                pool.tensor_copy(flat(dyn(big, (i * 2 + u) * KB)), turned[:, u, 0]).then_inc(big_ready[0], 1)
        pool.wait_ge(pad_in, 16 * (ST_TILES - 2 * NT))
        pool.iota(number, pattern=[[P, NE]], base=NT * P, channel_multiplier=1).then_inc(zero_ready, 1)
        pool.wait_ge(zero_ready, 3)
        pool.wait_ge(T.routed, 1)
        for e in range(NE):
            pool.indirect_dma_start(out=sorted_dram[:, :], out_offset=bass.IndirectOffsetOnAxis(ap=pad_i[:, e:e + 1], axis=0),
                                    in_=zero[:, e, :], in_offset=None).then_inc(T.padded, 16)
        pool.wait_ge(T.padded, 16 * NE)
        with pool.Fori(0, NBLK // 2) as i:
            for k in range(2 * BLK):
                pool.wait_ge(rows_ready, i * (2 * BLK) + (k + 1))
                settle(pool, T.passed)
                half, tt = divmod(k, BLK)
                for choice in range(2):
                    pool.indirect_dma_start(out=sorted_dram[:, :],
                                            out_offset=bass.IndirectOffsetOnAxis(ap=idx[:, half, tt, choice:choice + 1], axis=0),
                                            in_=rows[:, half, tt, choice, :], in_offset=None).then_inc(scattered[k], 16)
        for k in range(2 * BLK):
            pool.wait_ge(scattered[k], 32 * (NBLK // 2))

    @block.scalar
    def _(act):
        act.wait_ge(stat, 5)
        act.activation(rstd[:], rstd[:], ACT.Sqrt).then_inc(std, 1)
        for i in first_apart(act, NPAIR):
            for u in range(2):
                if not isinstance(i, int):
                    act.wait_ge(gp_full, i * 2 + (u - 1))
                    act.wait_ge(big_ready[0], i * 2 + (u - 1))
                for k in range(KB):
                    act.wait_ge(tr_full, i * 4 + (2 * u + k + 1))
                    act.activation(turned[:, u, k, :], tr[:, u, k, :], ACT.Copy).then_inc(xT_ready, 1)
                act.activation(flat(dyn(big, (i * 2 + u) * KB + 1)), tr[:, u, 1, :], ACT.Copy).then_inc(big_ready[1], 1)
        act.wait_ge(logits_ready, NBLK + CREDIT2)
        act.activation(score[:], score[:], ACT.Sigmoid).then_inc(score_ready, 1)

        def silu(i, m):
            act.wait_ge(up_full, i * 4 + (2 * m + 1))
            after(act, h_ready, i * 2 + (m - 1))
            act.activation(g[:, m, :], up[:, m, 0, :], ACT.Silu).then_inc(g_ready, 1)

        for i in range(APART):
            for m in range(KB):
                silu(i, m)
        for j in blocks(act):
            for u in range(ROUND):
                for m in range(KB):
                    silu(j * ROUND + (APART + u), m)

    @block.tensor
    def _(pe):
        def turn(n, u):
            pe.wait_ge(xn_ready, n + 1)
            if not isinstance(n, int):
                pe.wait_ge(xT_ready, n * 2 - 2)
                pe.wait_ge(big_ready[1], n - 1)
            for k in range(KB):
                for tt in range(BLK):
                    mm = pe.transpose(tr[:, u, k, tt * P:(tt + 1) * P], xn[:, u, tt, k * P:(k + 1) * P], T.ident[:])
                mm.then_inc(tr_full, 1)

        def logits(n, u):
            pe.wait_ge(xT_ready, n * 2 + 2)
            pe.wait_ge(gs_ready, n + (CREDIT2 - 1))
            for k in range(KB):
                for tt in range(BLK):
                    mm = pe.matmul(gp[STRIP * tt:STRIP * (tt + 1), u, 0:P], gw[:, k, :],
                                   turned[:, u, k, tt * P:(tt + 1) * P], start=(k == 0), stop=(k == KB - 1))
            mm.then_inc(gp_full, 1)

        def back(n, u):
            pe.wait_ge(gs_ready, n + (CREDIT2 + 1))
            pe.wait_ge(logits_ready, n + (CREDIT2 - 1))
            pe.transpose(gt[:, u, 0:P], gs[:, u, :], T.ident[:]).then_inc(gt_full, 1)

        pe.sem_inc(gs_ready, CREDIT2)
        pe.sem_inc(logits_ready, CREDIT2)
        pe.wait_ge(gw_in, 16)
        for i in first_apart(pe, NPAIR):
            if not isinstance(i, int):
                for u in range(2):
                    logits(i * 2 + (u - 2), u)
            for u in range(2):
                turn(i * 2 + u, u)
            if not isinstance(i, int):
                for u in range(2):
                    back(i * 2 + (u - 2), u)
        for f in (logits, back):
            for u in range(2):
                f(NBLK - 2 + u, u)

        def product(i, m):
            after(pe, h_ready, i * 2 + (m - 1))
            for w in range(2):
                for k in range(KB):
                    mm = pe.matmul(up[:, m, w, :], w13[:, k, w * HID + m * P:w * HID + (m + 1) * P], flat(dyn(big, i * KB + k)),
                                   start=(k == 0), stop=(k == KB - 1))
                mm.then_inc(up_full, 1)

        def output(i):
            pe.wait_ge(h_ready, i * 2 + 2)
            after(pe, sum_ready, i * 2)
            for pair in range(2):
                for tt in range(2):
                    for k in range(KB):
                        mm = pe.matmul(down[:, pair, tt, :], hT[:, k, (2 * pair + tt) * P:(2 * pair + tt + 1) * P],
                                       w2[:, k, :], start=(k == 0), stop=(k == KB - 1))
                mm.then_inc(down_full, 1)

        pe.wait_ge(w_in, 32)
        pe.wait_ge(xT_ready, NBLK * KB)
        for k in range(KB):
            pe.wait_ge(big_ready[k], NBLK)
        pe.wait_ge(logits_ready, NBLK + CREDIT2)
        for i in range(APART):
            product(i, 0)
            if i:
                output(i - 1)
            product(i, 1)
            if i == 1:
                pe.wait_ge(consts, 6)
                pe.wait_ge(both_ready, 1)
                pe.matmul(gp[:, 0, :], before[:], both[:], start=True, stop=True).then_inc(cnt_full, 1)
                pe.matmul(gp[:, 1, :], ones[:], both[:], start=True, stop=True).then_inc(cnt_full, 1)
        for j in blocks(pe):
            for u in range(ROUND):
                i = j * ROUND + (APART + u)
                product(i, 0)
                output(i - 1)
                product(i, 1)
        output(NBLK - 1)

    @block.vector
    def _(dve):
        def normed(n, u):
            if not isinstance(n, int):
                dve.wait_ge(tr_full, n * 2 - 2)
            for tt in range(BLK):
                t = n * BLK + tt
                ins = dve.tensor_scalar(xn[:, u, tt, :], flat(dyn(x, t)), dyn(mean, t), dyn(rstd, t), ALU.subtract, ALU.mult)
            ins.then_inc(xn_ready, 1)

        def logits_out(n, u):
            dve.wait_ge(gp_full, n + 1)
            dve.wait_ge(gt_full, n + (CREDIT2 - 1))
            dve.tensor_copy(gs[:, u, :], gp[:, u, 0:P]).then_inc(gs_ready, 1)

        def logits_back(n, u):
            dve.wait_ge(gt_full, n + (CREDIT2 + 1))
            dve.tensor_copy(dyn(score, n * BLK, BLK), gt[:, u, 0:P].rearrange("p (t e) -> p t e", e=STRIP)[:, :, 0:NE]).then_inc(logits_ready, 1)

        norm_stats(dve, T, stat, 0, 0, NT)
        dve.wait_ge(std, 1)
        dve.reciprocal(rstd[:], rstd[:]).then_inc(rs, 1)
        dve.wait_ge(rs, 1)
        dve.sem_inc(gt_full, CREDIT2)
        for i in first_apart(dve, NPAIR):
            for u in range(2):
                normed(i * 2 + u, u)
            if not isinstance(i, int):
                for f in (logits_out, logits_back):
                    for u in range(2):
                        f(i * 2 + (u - 2), u)
        for f in (logits_out, logits_back):
            for u in range(2):
                f(NBLK - 2 + u, u)

        def gated(i):
            for m in range(KB):
                dve.wait_ge(up_full, i * 4 + (2 * m + 2))
                dve.wait_ge(g_ready, i * 2 + (m + 1))
                after(dve, down_full, i * 2)
                dve.tensor_tensor(hT[:, m, :], g[:, m, :], up[:, m, 1, :], ALU.mult).then_inc(h_ready, 1)

        def add(i, place, uses):
            after(dve, stored[place], uses * 16)
            for pair in range(2):
                dve.wait_ge(down_full, i * 2 + (pair + 1))
                dve.tensor_tensor(sums[:, place, 2 * pair:2 * pair + 2, :], down[:, pair], dyn(x, i * BLK + 2 * pair, 2), ALU.add).then_inc(sum_ready, 1)

        def token_rows(i, half, uses):
            for tt in range(BLK):
                t = i * BLK + tt
                after(dve, scattered[half * BLK + tt], uses * 32)
                for k in range(2):
                    dve.tensor_scalar(rows[:, half, tt, k, 0:D], flat(dyn(x, t)), dyn(mean, t), flat(dyn(T.r[:, :, k:k + 1], t)), ALU.subtract, ALU.mult)
                dve.tensor_copy(rows[:, half, tt, :, D].bitcast(I32), flat(dyn(T.dest, t)))
                dve.tensor_copy(rows[:, half, tt, :, D + 1], flat(dyn(T.s, t)))
                dve.tensor_copy(idx[:, half, tt, :], flat(dyn(T.slot, t))).then_inc(rows_ready, 1)

        n = [0]

        def step(ins):
            n[0] += 1
            ins.then_inc(c, 1)
            dve.wait_ge(c, n[0])

        per_e = lambda a: a.unsqueeze(1).to_broadcast([P, NT, NE])
        per_t = lambda a: a.unsqueeze(2).to_broadcast([P, NT, NE])

        def choose(one):
            step(dve.tensor_reduce(best[:], biased[:], AX.X, ALU.max))
            step(dve.tensor_tensor(scr[:], biased[:], per_t(best[:]), ALU.is_equal))
            step(dve.tensor_tensor(scr[:], scr[:], per_e(desc[:]), ALU.mult))
            step(dve.tensor_reduce(best[:], scr[:], AX.X, ALU.max))
            step(dve.tensor_tensor(one[:], per_e(desc[:]), per_t(best[:]), ALU.is_equal))

        def chosen_score(one, s):
            step(dve.tensor_tensor(scr[:], one[:], score[:], ALU.mult))
            step(dve.tensor_reduce(s, scr[:], AX.X, ALU.add))

        dve.wait_ge(consts, 6)
        dve.wait_ge(bias_in, 16)
        dve.tensor_copy(desc[:], desc_i[:]).then_inc(T.tables, 1)
        dve.tensor_copy(jt[:], jt_i[:]).then_inc(T.tables, 1)
        dve.tensor_copy(row_f[:], row_i[:]).then_inc(T.tables, 1)
        dve.memset(pre[:, :, 0:pad, :], 0.0).then_inc(T.tables, 1)
        dve.memset(first[:, :, 0:NE], 0.0).then_inc(T.tables, 1)
        dve.wait_ge(T.tables, 5)
        dve.wait_ge(score_ready, 1)
        step(dve.tensor_tensor(biased[:], score[:], per_e(bias[:]), ALU.add))
        choose(one1)
        step(dve.scalar_tensor_tensor(out=biased[:], in0=one1[:], scalar=-BIG, in1=biased[:], op0=ALU.mult, op1=ALU.add))
        gated(0)
        choose(one2)
        dve.tensor_tensor(both[:], one1[:].rearrange("p t e -> p (t e)"), one2[:].rearrange("p t e -> p (t e)"), ALU.add).then_inc(both_ready, 1)
        add(0, 0, 0)
        gated(1)
        chosen_score(one1, T.s[:, :, 0])
        chosen_score(one2, T.s[:, :, 1])
        step(dve.tensor_tensor(T.r[:], T.s[:], rstd[:].unsqueeze(2).to_broadcast([P, NT, 2]), ALU.mult))
        dve.wait_ge(cnt_full, 2)
        total = gp[:, 1, :].rearrange("p (t e) -> p t e", e=NE)
        inner = gp[:, 0, :].rearrange("p (t e) -> p t e", e=NE)
        step(dve.tensor_copy(pre[:, 0, pad:, :], total))
        a, k = 0, 1
        while k < NT:
            step(dve.tensor_tensor(pre[:, 1 - a, pad:, :], pre[:, a, pad:, :], pre[:, a, pad - k:pad + NT - k, :], ALU.add))
            a, k = 1 - a, 2 * k
        step(dve.tensor_scalar(tiles_i[:], pre[:, a, pad + NT - 1, :], float(P - 1), None, ALU.add))
        step(dve.tensor_scalar(tiles_i[:], tiles_i[:], LOG2P, None, ALU.logical_shift_right))
        step(dve.tensor_copy(tiles[:], tiles_i[:]))
        step(dve.tensor_copy(first[:, 0, NE:], tiles[:]))
        f, k = 0, 1
        while k < NE:
            step(dve.tensor_tensor(first[:, 1 - f, NE:], first[:, f, NE:], first[:, f, NE - k:2 * NE - k], ALU.add))
            f, k = 1 - f, 2 * k
        ends = first[:, f, NE:]
        starts = first[:, f, NE - 1:2 * NE - 1]
        step(dve.tensor_scalar(pad_f[:], ends, 1.0, float(P), ALU.subtract, ALU.mult))
        step(dve.tensor_scalar(pad_f[:], pad_f[:], row_f[:, 0:1], float(-ST_TILES * P), ALU.add, ALU.add))
        step(dve.tensor_scalar(pad_g[:], tiles[:], 0.0, None, ALU.is_equal))
        step(dve.tensor_tensor(row_f[:], row_f[:], pad_f[:], ALU.subtract))
        step(dve.tensor_tensor(row_f[:], row_f[:], pad_g[:], ALU.mult))
        step(dve.tensor_tensor(pad_f[:], pad_f[:], row_f[:], ALU.add))
        dve.tensor_copy(pad_i[:], pad_f[:]).then_inc(T.routed, 1)
        add(1, 1, 0)
        gated(2)
        step(dve.tensor_tensor(scr[:], pre[:, a, pad:, :], total, ALU.subtract))
        step(dve.tensor_tensor(scr[:], scr[:], inner, ALU.add))
        step(dve.tensor_scalar(pad_g[:], starts, float(P), None, ALU.mult))
        step(dve.tensor_tensor(biased[:], scr[:], per_e(pad_g[:]), ALU.add))
        for k, one in enumerate((one1, one2)):
            step(dve.tensor_tensor(scr[:], one[:], biased[:], ALU.mult))
            step(dve.tensor_reduce(slot_f[:], scr[:], AX.X, ALU.add))
            step(dve.tensor_copy(T.slot[:, :, k], slot_f[:]))
        add(2, 2, 0)
        gated(3)
        for j in blocks(dve):
            for u in range(ROUND + 1):
                token_rows(j * (ROUND + 1) + u, u % 2, j * 2 + u // 2)
                if u < ROUND:
                    i = APART + u
                    add(j * ROUND + (i - 1), (i - 1) % ROUND, j + (i - 1) // ROUND)
                    gated(j * ROUND + i)
        add(NBLK - 1, (NBLK - 1) % ROUND, (NBLK - 1) // ROUND)
        per = lambda a: a.unsqueeze(1).to_broadcast([1, ST_TILES, NE - 1])
        step(dve.tensor_tensor(past, jt[:].unsqueeze(2).to_broadcast([1, ST_TILES, NE - 1]), per(ends[0:1, 0:NE - 1]), ALU.is_ge))
        step(dve.tensor_reduce(et[:], past, AX.X, ALU.add))
        step(dve.tensor_copy(T.expert[:], et[:]))
        step(dve.tensor_tensor(past, past, per(tiles[0:1, 0:NE - 1]), ALU.mult))
        step(dve.tensor_reduce(et[:], past, AX.X, ALU.add))
        step(dve.tensor_copy(T.begins[:], et[:]))


RING = 8


class Step:

    def __init__(self, c, i=None):
        self.c, self.i = c, i

    def times(self, k, more=0):
        return k * self.c + more if self.i is None else self.i * (RING * k) + (k * self.c + more)

    @property
    def ring(self):
        return self.c % RING

    def uses(self, k, more=0):
        v = k * (self.c // RING) + more
        return v if self.i is None else self.i * k + v

    def back(self, n):
        return Step(self.c - n, self.i)


def experts(nc, ctx, T, sorted_dram, out_dram):
    sb = lambda name, shape, dt=F32: ctx.enter_context(nc.sbuf_tensor(name, shape, dt))
    sem = lambda name: ctx.enter_context(nc.semaphore(name))
    rows = sb("e_rows", [P, RING, ROW])
    xT = sb("e_xT", [P, 2, KB, P])
    g = sb("e_gate", [P, 2, HID])
    h = sb("e_h", [P, 2, HID])
    hT = sb("e_hT", [P, 2, KB, P])
    y = sb("e_y", [P, RING, D])
    ps = lambda name, n: ctx.enter_context(nc.psum_tensor(name, [P, n, S], F32))
    px, pu, ph, py = ps("e_px", 1), ps("e_pu", 2), ps("e_ph", 1), ps("e_py", 2)
    rows_in = [sem(f"e_rows_in{k}") for k in range(RING)]
    sent = [sem(f"e_sent{k}") for k in range(RING)]
    px_full, xT_ready, pu_full, g_ready, h_ready = sem("px_full"), sem("e_xT_ready"), sem("pu_full"), sem("e_g_ready"), sem("e_h_ready")
    ph_full, hT_ready, py_full, y_ready = sem("ph_full"), sem("e_hT_ready"), sem("py_full"), sem("y_ready")
    done = sem("e_done")
    w13 = T.big[:, 0:NE * KB, :]
    w2 = T.big[:, NE * KB:NE * KB + NE * KB // 2, :].rearrange("p a (b n) -> p (a b) n", b=2)

    LAST = ST_TILES + 3

    def steps(eng):
        for j in range(RING):
            yield Step(j)
        with eng.Fori(0, ST_TILES // RING - 1) as i:
            for u in range(RING):
                yield Step(RING + u, i)
        for j in range(ST_TILES, LAST):
            yield Step(j)

    def tile(s, lag):
        b = s.back(lag)
        return b if s.i is not None or 0 <= b.c < ST_TILES else None

    block = ctx.enter_context(nc.Block())

    @block.sync
    def _(sp):
        def load(t):
            k = t.ring
            if t.c >= RING:
                sp.wait_ge(sent[k], t.uses(16))
                sp.sem_inc(done, 1)
            settle(sp, T.passed)
            r = t.times(P)
            src = sorted_dram[r:r + P, :] if t.i is None else sorted_dram[bass.ds(r, P), :]
            sp.dma_start(rows[:, k, :], src).then_inc(rows_in[k], 16)

        sp.sem_inc(done, CREDIT)
        for s in steps(sp):
            t = tile(s, 0)
            if t:
                load(t)
        for k in range(RING):
            sp.wait_ge(sent[k], 16 * (ST_TILES // RING))
            sp.sem_inc(done, 1)

    @block.tensor
    def _(pe):
        pe.wait_ge(T.w_in, 16 * (NE + NE // 2))
        for s in steps(pe):
            if t := tile(s, 0):
                k = t.ring
                pe.wait_ge(rows_in[k], t.uses(16, 16))
                if t.c:
                    pe.wait_ge(xT_ready, t.times(1))
                for kb in range(KB):
                    mm = pe.transpose(px[:, 0, kb * P:(kb + 1) * P], rows[:, k, kb * P:(kb + 1) * P], T.ident[:])
                mm.then_inc(px_full, 1)
            if t := tile(s, 1):
                pe.wait_ge(xT_ready, t.times(1, 1))
                if t.c >= 2:
                    pe.wait_ge(h_ready, t.times(1, -1))
                settle(pe, T.passed)
                e = pe.value_load(T.expert[0:1, bass.ds(t.times(1), 1)] if t.i is not None else T.expert[0:1, t.c:t.c + 1],
                                  min_val=0, max_val=NE - 1)
                for kb in range(KB):
                    mm = pe.matmul(pu[:, t.c % 2, :], xT[:, t.c % 2, kb, :], w13[:, bass.ds(e * KB + kb, 1), :].rearrange("p a n -> p (a n)"),
                                   start=(kb == 0), stop=(kb == KB - 1))
                mm.then_inc(pu_full, 1)
            if t := tile(s, 2):
                pe.wait_ge(h_ready, t.times(1, 1))
                if t.c:
                    pe.wait_ge(hT_ready, t.times(1))
                for kb in range(KB):
                    mm = pe.transpose(ph[:, 0, kb * P:(kb + 1) * P], h[:, t.c % 2, kb * P:(kb + 1) * P], T.ident[:])
                mm.then_inc(ph_full, 1)
            if t := tile(s, 3):
                pe.wait_ge(hT_ready, t.times(1, 1))
                if t.c >= 2:
                    pe.wait_ge(y_ready, t.times(1, -1))
                settle(pe, T.passed)
                e = pe.value_load(T.expert[0:1, bass.ds(t.times(1), 1)] if t.i is not None else T.expert[0:1, t.c:t.c + 1],
                                  min_val=0, max_val=NE - 1)
                for kb in range(KB):
                    mm = pe.matmul(py[:, t.c % 2, 0:D], hT[:, t.c % 2, kb, :], w2[:, bass.ds(e * KB + kb, 1), :].rearrange("p a n -> p (a n)"),
                                   start=(kb == 0), stop=(kb == KB - 1))
                mm.then_inc(py_full, 1)

    @block.scalar
    def _(act):
        for s in steps(act):
            if t := tile(s, 0):
                act.wait_ge(px_full, t.times(1, 1))
                if t.c >= 2:
                    act.wait_ge(pu_full, t.times(1, -1))
                act.activation(flat(xT[:, t.c % 2]), px[:, 0, 0:D], ACT.Copy).then_inc(xT_ready, 1)
            if t := tile(s, 1):
                act.wait_ge(pu_full, t.times(1, 1))
                if t.c >= 2:
                    act.wait_ge(h_ready, t.times(1, -1))
                act.activation(g[:, t.c % 2, :], pu[:, t.c % 2, 0:HID], ACT.Silu).then_inc(g_ready, 1)
            if t := tile(s, 3):
                k = t.ring
                act.wait_ge(py_full, t.times(1, 1))
                if t.c >= RING:
                    act.wait_ge(sent[k], t.uses(16))
                act.activation(y[:, k, :], py[:, t.c % 2, 0:D], ACT.Copy, scale=rows[:, k, D + 1:D + 2]).then_inc(y_ready, 1)

    @block.vector
    def _(dve):
        for s in steps(dve):
            if t := tile(s, 1):
                dve.wait_ge(g_ready, t.times(1, 1))
                if t.c >= 2:
                    dve.wait_ge(ph_full, t.times(1, -1))
                dve.tensor_tensor(h[:, t.c % 2, :], g[:, t.c % 2, :], pu[:, t.c % 2, HID:2 * HID], ALU.mult).then_inc(h_ready, 1)
            if t := tile(s, 2):
                dve.wait_ge(ph_full, t.times(1, 1))
                if t.c >= 2:
                    dve.wait_ge(py_full, t.times(1, -1))
                dve.tensor_copy(flat(hT[:, t.c % 2]), ph[:, 0, 0:HID]).then_inc(hT_ready, 1)

    @block.gpsimd
    def _(pool):
        for s in steps(pool):
            if t := tile(s, 3):
                k = t.ring
                pool.wait_ge(y_ready, t.times(1, 1))
                if t.c:
                    settle(pool, T.passed)
                    begins = pool.value_load(T.begins[0:1, bass.ds(t.times(1), 1)] if t.i is not None else T.begins[0:1, t.c:t.c + 1],
                                             min_val=0, max_val=ST_TILES - 1)
                    pool.wait_ge(done, begins + CREDIT)
                settle(pool, T.passed)
                pool.indirect_dma_start(out=out_dram[:, :],
                                        out_offset=bass.IndirectOffsetOnAxis(ap=rows[:, k, D:D + 1].bitcast(U32), axis=0),
                                        in_=y[:, k, :], in_offset=None, compute_op=ALU.add).then_inc(sent[k], 16)
        for k in range(RING):
            pool.wait_ge(sent[k], 16 * (ST_TILES // RING))


def layer(nc, ins, out):
    x, wqk, wv, wo, gw, bias, ew, sw13, sw2 = ins
    sorted_dram = nc.dram_tensor("sorted_rows", [PAD_TILES * P, ROW], F32, kind="Internal").ap()
    with contextlib.ExitStack() as ctx:
        T = shared(nc, ctx)
        with contextlib.ExitStack() as phase:
            attention(nc, phase, T, x, wqk, wv, wo)
        routing(nc, ctx, T)
        with contextlib.ExitStack() as outer:
            T.big = outer.enter_context(nc.sbuf_tensor("big", [P, NBLK * KB, S], F32))
            with contextlib.ExitStack() as phase:
                front(nc, phase, T, gw, bias, sw13, sw2, ew, sorted_dram, out)
            with contextlib.ExitStack() as phase:
                experts(nc, phase, T, sorted_dram, out)


def routing(nc, ctx, T):
    sb = lambda name, shape, dt=F32: ctx.enter_context(nc.sbuf_tensor(name, shape, dt))
    T.s = sb("s", [P, NT, 2])
    T.r = sb("r", [P, NT, 2])
    T.slot = sb("slot", [P, NT, 2], U32)
    T.dest = sb("dest", [P, NT, 2], I32)
    T.expert = sb("expert", [1, ST_TILES], I32)
    T.begins = sb("begins", [1, ST_TILES], I32)
    T.routed = ctx.enter_context(nc.semaphore("routed"))
    T.padded = ctx.enter_context(nc.semaphore("padded"))
    T.tables = ctx.enter_context(nc.semaphore("tables"))
    T.w_in = ctx.enter_context(nc.semaphore("ew_in"))


def expert_weights(w1, w2, w3):
    w13 = np.concatenate([w1.transpose(0, 2, 1), w3.transpose(0, 2, 1)], axis=2).reshape(NE, KB, P, 2 * HID)
    w2 = w2.transpose(0, 2, 1).reshape(NE // 2, 2 * KB, P, D)
    pieces = [w.transpose(0, 2, 1, 3).reshape(-1, KB * S) for w in (w13, w2)]
    return np.ascontiguousarray(np.concatenate(pieces))


def kernel(L0_attn_x, L0_attn_WQ, L0_attn_WK, L0_attn_WV, L0_attn_WO, L0_ffn_gate_w, L0_ffn_w1, L0_ffn_w2,
           L0_ffn_w3, L0_ffn_sw1, L0_ffn_sw2, L0_ffn_sw3, L0_ffn_expert_bias):
    import concourse.bacc as bacc
    from concourse.bass_utils import run_bass_kernel_spmd

    lay = lambda a: np.ascontiguousarray(np.asarray(a))
    WQ, WK, WV, WO, w1, w2, w3, sw1, sw2, sw3 = (
        lay(a) for a in (L0_attn_WQ, L0_attn_WK, L0_attn_WV, L0_attn_WO, L0_ffn_w1, L0_ffn_w2, L0_ffn_w3,
                         L0_ffn_sw1, L0_ffn_sw2, L0_ffn_sw3))
    wqk, wv, wo = attention_weights(WQ, WK, WV, WO)
    arrays = {
        "x": lay(L0_attn_x).reshape(NT * P, D),
        "wqk": wqk, "wv": wv, "wo": wo,
        "gate_wT": lay(lay(L0_ffn_gate_w).T),
        "expert_bias": lay(L0_ffn_expert_bias),
        "ew": expert_weights(w1, w2, w3),
        "ws13": lay(np.concatenate([sw1.T, sw3.T], axis=1)),
        "ws2": lay(sw2.T),
    }
    nc = bacc.Bacc("TRN2", target_bir_lowering=False, num_devices=1)
    ins = [nc.dram_tensor(n, a.shape, F32, kind="ExternalInput").ap() for n, a in arrays.items()]
    out = nc.dram_tensor("out", [(NT + PADS) * P, D], F32, kind="ExternalOutput").ap()
    layer(nc, ins, out)
    got = run_bass_kernel_spmd(nc, [arrays], core_ids=[0])
    return got.results[0]["out"][0:NT * P].reshape(NB, S, D)
```

```python
import contextlib

import numpy as np
import concourse.bass as bass
import concourse.mybir as mybir
from concourse.alu_op_type import AluOpType as ALU

F32 = mybir.dt.float32
F32R = mybir.dt.float32r
BF16 = mybir.dt.bfloat16
I32 = mybir.dt.int32
U32 = mybir.dt.uint32
ACT = mybir.ActivationFunctionType
AX = mybir.AxisListType

P = 128
NB, S, D = 16, 512, 256
H, DH = 16, 16
TB = S // P
NT = NB * TB
KB = D // P
GH = 4
NG = H // GH
NE, HID = 8, 256
EPS = 1e-5
QSCALE = 0.25
NPROD = 6
Q_PART = (0, 0, 1, 1, 0, 2)
K_PART = (0, 1, 0, 1, 2, 0)
PASSES = ((0, 0), (0, 1), (1, 0))
ROWS1 = NPROD * DH
ROWS2 = ROWS1 + 2
MASKED = -1e30

ST_TILES = 2 * NT + NE


class Batch:

    def __init__(self, c, i=None):
        self.c, self.i = c, i

    def times(self, per_batch, more=0):
        v = per_batch * self.c + more
        return v if self.i is None else self.i * (2 * per_batch) + v

    first = property(lambda self: self.i is None and self.c == 0)
    last = property(lambda self: self.i is None and self.c == NB - 1)
    odd = property(lambda self: self.c % 2)
    next = property(lambda self: Batch(self.c + 1, self.i))
    prev = property(lambda self: Batch(self.c - 1, self.i))


def settle(eng, passed):
    eng.sem_inc(passed, 1)


def batches(eng):
    yield Batch(0)
    yield Batch(1)
    with eng.Fori(0, (NB - 4) // 2) as i:
        yield Batch(2, i)
        yield Batch(3, i)
    yield Batch(NB - 2)
    yield Batch(NB - 1)


TASK_PLACES = (
    (("OT", (2,)), ("Q0", (3, 4)), ("K0", (5, 7))),
    (("OT", (3,)), ("Q1", (3, 4)), ("K1", (6, 7)), ("AT0", (9,)), ("AT1", (10,))),
    (("OT", (1,)), ("V0", (1, 7)), ("V1", (8, 11))),
    (("OT", (1,)), ("WO0", (1, 2)), ("WO1", (4, 7)), ("X0", (8,)), ("X1", (10,))),
)
TASKS = tuple(tuple(t for t, _ in step) for step in TASK_PLACES)
PER_BATCH = sum(len(t) for t in TASKS)
PRO = tuple((t, 0) for t in ("X0", "X1", "Q0", "K0", "Q1", "K1", "V0", "V1")) + (("X0", 1), ("X1", 1))
OT_LAG = 2
EARLY_MAX = 7


def tasks(b, g):
    out = []
    for t in TASKS[g]:
        if t == "OT" and b.first and g < OT_LAG:
            continue
        if t[:2] in ("AT", "WO") and b.first:
            continue
        if t[0] in "QKV" and b.last:
            continue
        if t[0] == "X" and b.i is None and b.c >= NB - 2:
            continue
        out.append(t)
    return out


def misc_no(b, g, t):
    n = sum(len(tasks(b, k)) for k in range(g)) + tasks(b, g).index(t)
    if b.first:
        return len(PRO) + n
    lack = PER_BATCH - sum(len(tasks(Batch(0), k)) for k in range(NG)) + (2 if b.last else 0)
    return b.times(PER_BATCH, len(PRO) - lack + n)


def misc_bank(b, g, t):
    return misc_no(Batch(b.c), g, t) % 2


def whose(b, g, t):
    if t == "OT":
        return (b.prev, g + NG - OT_LAG) if g < OT_LAG else (b, g - OT_LAG)
    return (b.prev if t[:2] in ("AT", "WO") else b.next.next if t[0] == "X" else b.next), None


def two_before(b, g, t):
    here = [(b, k, x) for k in range(g + 1) for x in tasks(b, k)]
    here = here[:[x[1:] for x in here].index((g, t))]
    if len(here) >= 2:
        sb, k, x = here[-2]
        return x, *whose(sb, k, x)
    if b.first:
        t, n = PRO[len(here) - 2]
        return t, Batch(n), None
    prev = [(b.prev, k, x) for k in range(NG) for x in tasks(b.prev, k)]
    sb, k, x = prev[len(here) - 2]
    return x, *whose(sb, k, x)


def parts_at(b, g, u):
    return [(t, places.index(u)) for t, places in TASK_PLACES[g] if t in tasks(b, g) and u in places]


def due(b, g, u):
    return [t for t, places in TASK_PLACES[g] if t in tasks(b, g) and places[-1] + 1 == u]


def kb_place(j, kb):
    pair, i = divmod(j, 2)
    if kb == 0:
        return pair, 3 * i, 0, S
    if kb == 1:
        return pair, 3 * i + 1, P, S - P
    if kb == 3:
        return pair, 3 * i + 1, 0, P
    return pair, 2, 2 * P * i, 2 * P


PAIR_BANKS = (((0, 0),), ((0, 3), (0, 1)), ((0, 2), (1, 2)), ((1, 0),), ((1, 3), (1, 1)))
MAX_UNITS = ((0, (0, 1, 2, 3)), (1, (0, 1)), (1, (2, 3)),
             (2, (0,)), (2, (1,)), (2, (2,)), (2, (3,)),
             (3, (0,)), (3, (1,)), (3, (2,)), (3, (3,)))
NMU = len(MAX_UNITS)
U1 = NMU + 1
U2 = 10
LAG = 4
TURN = 13
MID_LAG = 3
PLACES = LAG + U2
PV_AT = (4, 6, 8, 10)
EVAC_O_AT = 11
NORM_AT = ((2, 2), (2, 4), (2, 6), (2, 8))
EARLY = 4
MORE = (NB - EARLY) * TB // NG


def attention(nc, ctx, T, x_dram, wqk_dram, wv_dram, wo_dram):
    sb = lambda name, shape, dt=F32: ctx.enter_context(nc.sbuf_tensor(name, shape, dt))
    sem = lambda name: ctx.enter_context(nc.semaphore(name))
    x, mean, rstd, stats = T.x, T.mean, T.rstd, T.stats

    xnT = sb("xnT", [P, 2, KB, S], F32R)
    qf = sb("qf", [P, 2, S])
    xn = qf[:].rearrange("p a (b d) -> p (a b) d", d=D)
    rem = sb("rem", [P, 2, S])
    part = sb("part", [P, 2, 2, 3, S], BF16)
    QS = sb("QS", [P, H, S], BF16)
    KS = sb("KS", [P, H, S], BF16)
    V = sb("V_sb", [P, 2, TB, H, 2 * DH])
    PR = sb("PR", [P, 2, 2, 5, S])
    O = sb("O_sb", [P, S])
    attn = sb("attn", [P, TB, D])
    attnT = sb("attnT", [P, KB, S])
    rec = sb("rec", [P, TB, GH])
    mx = sb("mx", [P, 2, GH, TB])
    nm = sb("nm", [GH * TB, 2, P], BF16)
    wqk = sb("wqk_sb", [P, 2, KB, 2 * D], F32R)
    wv = sb("wv_sb", [P, 2, KB, D], F32R)
    wo = sb("wo_sb", [P, KB, D])
    came = PR[:, 0, 0]
    weights = ((came[:, 0:2, :], wqk_dram, wqk), (came[:, 2, :].rearrange("p (k n) -> p k n", k=KB), wv_dram, wv))
    identb = sb("identb", [P, P], BF16)
    tri = sb("tri", [P, P], BF16)

    score = ctx.enter_context(nc.psum_tensor("score", [P, 3, S], F32))
    logit = ctx.enter_context(nc.psum_tensor("logit", [P, 2, S], F32))
    opsum = ctx.enter_context(nc.psum_tensor("opsum", [P, S], F32))
    misc = ctx.enter_context(nc.psum_tensor("misc", [P, 2, S], F32))

    x_first = [sem(f"x_first{b}") for b in range(EARLY)]
    x_in = [sem(f"x_in{q}") for q in range(1, 4)]
    w_in, wo_in, w_high, w_ready = sem("w_in"), sem("wo_in"), sem("w_high"), sem("w_ready")
    xnT_high = sem("xnT_high")
    const_a, const_ready = sem("const_a"), sem("const_ready")
    stat_ready, std_ready, rstd_ready = sem("stat_ready"), sem("std_ready"), sem("rstd_ready")
    xn_ready = sem("xn_ready")
    misc_full = sem("misc_full")
    qf_ready, rem_ready, mid_ready, parts_ready = sem("qf_ready"), sem("rem_ready"), sem("mid_ready"), sem("parts_ready")
    high_ready = sem("high_ready")
    stacked = [sem("stacked0"), sem("stacked1")]
    max_full, max_free = sem("max_full"), sem("max_free")
    nm_high = sem("nm_high")
    nm_ready = sem("nm_ready")
    nm_in = [sem("nm_in0"), sem("nm_in1")]
    logit_full, logit_free = sem("logit_full"), sem("logit_free")
    masked = sem("masked")
    o_full, o_free = sem("o_full"), sem("o_free")
    rec_ready, attn_ready = sem("rec_ready"), sem("attn_ready")
    v_ready, xnT_ready, attnT_ready = sem("v_ready"), sem("xnT_ready"), sem("attnT_ready")
    x_out = sem("x_out")
    ones_ready = sem("ones_ready")

    xv = x_dram.rearrange("(n p) d -> p n d", p=P)
    block = ctx.enter_context(nc.Block())

    def proj(t):
        half, qk = int(t[1]), "QK".index(t[0])
        return half, qk, 2 * half + qk

    TAIL = misc_no(Batch(NB - 1), 3, tasks(Batch(NB - 1), 3)[-1]) + 1
    TAIL_AT = TAIL + 2
    TAIL_USES = len(tasks(Batch(NB - 1), NG - 1))

    @block.sync
    def _(sp):
        q = NT // 4
        for b in range(EARLY):
            tiles = slice(b * TB, (b + 1) * TB)
            sp.dma_start(x[:, tiles, :], xv[:, tiles, :]).then_inc(x_first[b], 16)
        for raw, dram, _ in weights:
            sp.dma_start(raw, dram.rearrange("(k p) n -> p k n", p=P)).then_inc(w_in, 16)
        sp.dma_start(wo[:], wo_dram.rearrange("(k p) n -> p k n", p=P)).then_inc(wo_in, 16)
        for k in range(1, 4):
            sp.dma_start(x[:, q * k:q * (k + 1), :], xv[:, q * k:q * (k + 1), :]).then_inc(x_in[k - 1], 16)

        def stack(b, half):
            for s in (parts_ready, high_ready, mid_ready):
                sp.wait_ge(s, b.times(4, 2 * half + 2))
            settle(sp, T.passed)
            if not b.first:
                sp.wait_ge(logit_full, b.prev.times(NG * U2, (2 * half + 2) * U2))
            for qk, (dst, order) in enumerate(((QS, Q_PART), (KS, K_PART))):
                for r in range(NPROD):
                    src = part[:, half, qk, order[r], :]
                    sp.dma_start(dst[DH * r:DH * r + DH, 8 * half:8 * half + 8, :], src).then_inc(stacked[half], 16)

        def maxima(b, g):
            par = g % 2
            sp.wait_ge(nm_ready, b.times(NG, g + 1))
            for k in range(2):
                dst = QS[ROWS1 + k:ROWS1 + k + 1, GH * g:GH * g + GH, :].rearrange("p h (t q) -> p h t q", t=TB)
                sp.dma_start(dst, nm[:, k, :]).then_inc(nm_in[par], 16)

        stack(Batch(0), 0)
        stack(Batch(0), 1)
        maxima(Batch(0), 0)
        for b in batches(sp):
            if not b.first:
                stack(b, 1)
            maxima(b, 1)
            maxima(b, 2)
            if not b.last:
                stack(b.next, 0)
            maxima(b, 3)
            if not b.last:
                maxima(b.next, 0)

    @block.gpsimd
    def _(pool):
        ident = T.ident
        pool.memset(ident[:], 0.0).then_inc(const_a, 1)
        pool.memset(identb[:], 0.0).then_inc(const_a, 1)
        pool.memset(tri[:], 0.0).then_inc(const_a, 1)
        pool.memset(V[:, :, :, :, DH:], 1.0).then_inc(ones_ready, 1)
        pool.wait_ge(const_a, 3)
        for a in (ident, identb):
            pool.affine_select(out=a[:], in_=a[:], compare_op=ALU.not_equal, fill=1.0, base=0,
                               pattern=[[-1, P]], channel_multiplier=1).then_inc(const_ready, 1)
        pool.affine_select(out=tri[:], in_=tri[:], compare_op=ALU.is_ge, fill=MASKED, base=0,
                           pattern=[[-1, P]], channel_multiplier=1).then_inc(const_ready, 1)

        def split_rem(b, t):
            half, qk, n = proj(t)
            pool.wait_ge(high_ready, b.times(4, n + 1))
            if not (b.first and n < 2):
                pool.wait_ge(parts_ready, b.times(4, n - 1))
            pool.tensor_tensor(rem[:, n % 2, :], qf[:, n % 2, :], part[:, half, qk, 0, :], ALU.subtract).then_inc(rem_ready, 1)

        def split_low(b, t):
            half, qk, n = proj(t)
            pool.wait_ge(mid_ready, b.times(4, n + 1))
            pool.tensor_tensor(part[:, half, qk, 2, :], rem[:, n % 2, :], part[:, half, qk, 1, :], ALU.subtract).then_inc(parts_ready, 1)

        def mask_pair(b, g, pair):
            pool.wait_ge(logit_free, b.times(NG * U2, g * U2 + 5 * pair + 5))
            settle(pool, T.passed)
            blocks = PR[:, g % 2, pair].rearrange("p k (c q) -> p (k c) q", q=P)
            sels = (blocks[:, 0:20:4, :], blocks[:, 5:18:12, :], blocks[:, 10, :])
            for k, v in enumerate(sels):
                pool.affine_select(out=v, in_=v, compare_op=ALU.is_ge, fill=0.0, base=0,
                                   pattern=([[0, v.shape[1]]] if k < 2 else []) + [[1, P]], channel_multiplier=-1).then_inc(masked, 1)

        for t, _ in PRO:
            if t[0] in "QK":
                split_rem(Batch(0), t)
                split_low(Batch(0), t)
        for b in batches(pool):
            for g in range(NG):
                split = [t for t in tasks(b, g) if t[0] in "QK"]
                for t in split:
                    split_rem(b.next, t)
                for t in split[:1]:
                    split_low(b.next, t)
                mask_pair(b, g, 0)
                for t in split[1:]:
                    split_low(b.next, t)
                mask_pair(b, g, 1)

    @block.scalar
    def _(act):
        def root(part):
            lo, hi = (0, EARLY * TB) if part == 0 else (EARLY * TB, NT)
            act.wait_ge(stat_ready, 5 * (part + 1))
            act.activation(rstd[:, lo:hi], rstd[:, lo:hi], ACT.Sqrt).then_inc(std_ready, 1)

        root(0)
        act.wait_ge(w_in, 16 * len(weights))
        for raw, _, w in weights:
            act.activation(w[:, 0], raw, ACT.Copy).then_inc(w_high, 1)

        def evac(b, t, n, bank):
            if t[:2] in ("OT", "WO"):
                return
            src = misc[:, bank, :]
            act.wait_ge(misc_full, n + 1)
            if t[0] == "X":
                act.activation(xnT[:, 0, int(t[1]), :], src, ACT.Copy).then_inc(xnT_high, 1)
            elif t[0] in "QK":
                half, qk, k = proj(t)
                if not (b.first and k < 2):
                    act.wait_ge(parts_ready, b.times(4, k - 1))
                if not b.first:
                    act.wait_ge(stacked[half], b.times(16 * 2 * NPROD))
                act.activation(qf[:, k % 2, :], src, ACT.Copy, scale=QSCALE if qk == 0 else 1.0).then_inc(qf_ready, 1)
                act.wait_ge(qf_ready, b.times(4, k + 1))
                act.activation(part[:, half, qk, 0, :], qf[:, k % 2, :], ACT.Copy).then_inc(high_ready, 1)
            elif t[0] == "V":
                i = int(t[1])
                act.activation(V[:, b.odd, 2 * i:2 * i + 2, :, 0:DH],
                               src.rearrange("p (t h d) -> p t h d", t=2, h=H), ACT.Copy).then_inc(v_ready, 1)
            elif t[:2] == "AT":
                act.activation(attnT[:, int(t[2]), :], src, ACT.Copy).then_inc(attnT_ready, 1)

        def step(b, g):
            for u in range(PLACES):
                if u >= LAG:
                    n = g * U2 + u - LAG
                    act.wait_ge(logit_full, b.times(NG * U2, n + 1))
                    if u == LAG and not (b.first and g < 2):
                        act.wait_ge(o_full, b.times(NG, g - 1))
                    act.activation(PR[:, g % 2, (u - LAG) // 5, (u - LAG) % 5, :], logit[:, n % 2, :], ACT.Exp).then_inc(logit_free, 1)
                for t in due(b, g, u):
                    evac(whose(b, g, t)[0], t, misc_no(b, g, t), misc_bank(b, g, t))
                if u == EVAC_O_AT and not (b.first and g == 0):
                    evac_o(b, g - 1)

        def evac_o(b, g):
            act.wait_ge(o_full, b.times(NG, g + 1))
            if not (b.first and g < 1):
                act.wait_ge(rec_ready, b.times(NG, g))
            act.activation(O[:], opsum[:], ACT.Copy).then_inc(o_free, 1)

        for n, (t, k) in enumerate(PRO):
            evac(Batch(k), t, n, n % 2)
        for b in batches(act):
            for g in range(NG):
                step(b, g)
                if b.first and g == NG - 1:
                    root(1)
        last = Batch(NB)
        evac_o(last, -1)
        for k in range(2):
            n = TAIL_AT + k
            evac(last.prev, f"AT{k}", n, n % 2)

    @block.tensor
    def _(pe):
        ident = T.ident

        def emptied(kind, who, g):
            if kind[0] == "X":
                return xnT_ready, who.times(2, int(kind[1]) + 1)
            if kind[0] in "QK":
                return qf_ready, who.times(4, proj(kind)[2] + 1)
            if kind[0] == "V":
                return v_ready, who.times(2, int(kind[1]) + 1)
            if kind == "OT":
                return attn_ready, who.times(NG, g + 1)
            if kind[:2] == "AT":
                return attnT_ready, who.times(2, int(kind[2]) + 1)
            return x_out, who.times(2, int(kind[2]) + 1)

        def do(t, b, g, k, before, part=None):
            bank = misc[:, k, :]
            if before and not part:
                pe.wait_ge(*emptied(*before))
            if t[0] == "X":
                k = int(t[1])
                pe.wait_ge(xn_ready, b.times(TB, TB))
                for tt in range(TB):
                    mm = pe.transpose(bank[:, tt * P:(tt + 1) * P], xn[:, tt, k * P:(k + 1) * P], ident[:])
            elif t[0] in "QK":
                half, qk, _ = proj(t)
                if not part:
                    pe.wait_ge(xnT_ready, b.times(2, 2))
                m = 2 * qk + half
                for k in range(KB) if part is None else (part,):
                    for i, j in PASSES:
                        mm = pe.matmul(bank, wqk[:, i, k, m * P:(m + 1) * P], xnT[:, j, k, :],
                                       start=((i, j, k) == (*PASSES[0], 0)), stop=((i, j, k) == (*PASSES[-1], KB - 1)))
            elif t == "OT":
                pe.wait_ge(o_free, b.times(NG, g + 1))
                for tt in range(TB):
                    mm = pe.transpose(bank[:, tt * P:(tt + 1) * P], O[:, tt * P:(tt + 1) * P], ident[:])
            elif t[:2] == "AT":
                k = int(t[2])
                pe.wait_ge(attn_ready, b.times(NG, NG))
                for tt in range(TB):
                    mm = pe.transpose(bank[:, tt * P:(tt + 1) * P], attn[:, tt, k * P:(k + 1) * P], ident[:])
            elif t[0] == "V":
                if not part:
                    pe.wait_ge(xnT_ready, b.times(2, 2))
                for tt in range(2) if part is None else (part,):
                    tile = 2 * int(t[-1]) + tt
                    for k in range(KB):
                        for i, j in PASSES:
                            mm = pe.matmul(bank[:, tt * D:(tt + 1) * D], xnT[:, i, k, tile * P:(tile + 1) * P], wv[:, j, k, :],
                                           start=((i, j, k) == (*PASSES[0], 0)), stop=((i, j, k) == (*PASSES[-1], KB - 1)))
            else:
                if not part:
                    pe.wait_ge(attnT_ready, b.times(2, 2))
                for tt in range(2) if part is None else (part,):
                    tile = 2 * int(t[-1]) + tt
                    for k in range(KB):
                        mm = pe.matmul(bank[:, tt * D:(tt + 1) * D], attnT[:, k, tile * P:(tile + 1) * P], wo[:, k, :],
                                       start=(k == 0), stop=(k == KB - 1))
            if part is None or part == 1:
                mm.then_inc(misc_full, 1)

        def max_unit(b, g, u):
            n = g * U1 + u
            if not (b.first and n < 3):
                pe.wait_ge(max_free, b.times(NG * U1, n - 2))
            if u == 0 and g % 2 == 0:
                pe.wait_ge(stacked[g // 2], b.times(16 * 2 * NPROD, 16 * 2 * NPROD))
            bank = score[:, n % 3, :]
            qt, heads = MAX_UNITS[u]
            cols = (qt + 1) * P
            for k, j in enumerate(heads):
                h = GH * g + j
                out = bank[:, k * cols:(k + 1) * cols]
                pe.matmul(out, QS[0:ROWS1, h, qt * P:(qt + 1) * P], KS[0:ROWS1, h, 0:cols], start=True, stop=False)
                mm = pe.matmul(out[:, cols - P:cols], identb[:], tri[:], start=False, stop=True)
            mm.then_inc(max_full, 1)

        def max_turn(b, g):
            n = g * U1 + NMU
            pe.wait_ge(max_free, b.times(NG * U1, n))
            pe.transpose(score[0:GH * TB, n % 3, 0:P], mx[:, g % 2].rearrange("p j t -> p (j t)"), ident[:]).then_inc(max_full, 1)

        def logit_unit(b, g, u):
            n = g * U2 + u
            if not (b.first and n < 2):
                pe.wait_ge(logit_free, b.times(NG * U2, n - 1))
            if u == 0:
                pe.wait_ge(nm_in[g % 2], b.times(64, 32 * (g // 2) + 32))
            pair = u // 5
            for i, kb in PAIR_BANKS[u % 5]:
                j = 2 * pair + i
                _, _, off, cols = kb_place(j, kb)
                h = GH * g + j
                mm = pe.matmul(logit[:, n % 2, off:off + cols], KS[0:ROWS2, h, kb * P:(kb + 1) * P],
                               QS[0:ROWS2, h, kb * P:S], start=True, stop=True)
            mm.then_inc(logit_full, 1)

        def pv(b, g, kb):
            if kb == 0:
                if not (b.first and g == 0):
                    pe.wait_ge(o_free, b.times(NG, g))
                pe.wait_ge(masked, b.times(NG * 6, 6 * g + 6))
                pe.wait_ge(v_ready, b.times(2, 2))
            for j in range(GH):
                pair, bank, off, cols = kb_place(j, kb)
                mm = pe.matmul(opsum[32 * j:32 * j + 32, kb * P:S], V[:, b.odd, kb, GH * g + j, :],
                               PR[:, g % 2, pair, bank, off:off + cols], start=(kb == 0), stop=(kb == TB - 1))
            if kb == TB - 1:
                mm.then_inc(o_full, 1)

        pe.wait_ge(const_ready, 3)
        pe.wait_ge(wo_in, 16)
        for n, (t, k) in enumerate(PRO):
            if t == "Q0":
                pe.wait_ge(w_ready, len(weights))
            do(t, Batch(k), None, n % 2, (PRO[n - 2][0], Batch(PRO[n - 2][1]), None) if n >= 2 else None)
            if n == EARLY_MAX:
                for u in range(NMU):
                    max_unit(Batch(0), 0, u)
                max_turn(Batch(0), 0)
        pe.wait_ge(ones_ready, 3)
        for b in batches(pe):
            for g in range(NG):
                ahead = None if b.last and g == NG - 1 else (b, g + 1) if g < NG - 1 else (b.next, 0)
                before = (b, g - 1) if g else None if b.first else (b.prev, NG - 1)
                for u in range(PLACES):
                    if ahead and u < NMU:
                        max_unit(*ahead, u)
                    if ahead and u == TURN:
                        max_turn(*ahead)
                    if u >= LAG:
                        logit_unit(b, g, u - LAG)
                    for t, k in parts_at(b, g, u):
                        whole = t[:2] in ("OT", "AT", "X0", "X1")
                        do(t, *whose(b, g, t), misc_bank(b, g, t), two_before(b, g, t), None if whole else k)
                    if before and u in PV_AT:
                        pv(*before, PV_AT.index(u))
        last = Batch(NB - 1)
        end = [(x, *whose(last, NG - 1, x)) for x in tasks(last, NG - 1)]
        for t, g in (("OT", 2), ("OT", 3), ("AT0", None), ("AT1", None), ("WO0", None), ("WO1", None)):
            if (t, g) == ("OT", 3):
                for kb in range(TB):
                    pv(last, NG - 1, kb)
            do(t, last, g, (TAIL + len(end) - TAIL_USES) % 2, end[-2])
            end.append((t, last, g))

    @block.vector
    def _(dve):
        def statistics(t):
            dve.bn_stats(stats[:, t, :], x[:, t, :]).then_inc(T.bn, 1)

        def deviations(part):
            lo, hi = (0, EARLY * TB) if part == 0 else (EARLY * TB, NT)
            dve.wait_ge(T.bn, hi)
            norm_stats(dve, T, stat_ready, 5 * part, lo, hi)

        def invert(part):
            lo, hi = (0, EARLY * TB) if part == 0 else (EARLY * TB, NT)
            dve.wait_ge(std_ready, part + 1)
            dve.reciprocal(rstd[:, lo:hi], rstd[:, lo:hi]).then_inc(rstd_ready, 1)
            dve.wait_ge(rstd_ready, part + 1)

        for b in range(EARLY):
            dve.wait_ge(x_first[b], 16)
            for t in range(b * TB, (b + 1) * TB):
                statistics(t)
        deviations(0)
        invert(0)

        def norm(b, tiles=range(TB)):
            if not b.first and 0 in tiles:
                dve.wait_ge(xnT_ready, b.times(2))
                dve.wait_ge(rem_ready, b.times(4))
            for tt in tiles:
                t = b.times(TB, tt)
                sl = (lambda a: a[:, t:t + 1]) if b.i is None else (lambda a: a[:, bass.ds(t, 1)])
                xin = (x[:, t, :] if b.i is None else x[:, bass.ds(t, 1), :].rearrange("p a d -> p (a d)"))
                dve.tensor_scalar(xn[:, tt, :], xin, sl(mean), sl(rstd), ALU.subtract, ALU.mult).then_inc(xn_ready, 1)

        def reduce_max(b, g, u):
            n = g * U1 + u
            qt, heads = MAX_UNITS[u]
            cols = (qt + 1) * P
            dve.wait_ge(max_full, b.times(NG * U1, n + 1))
            dve.tensor_reduce(mx[:, g % 2, heads[0]:heads[0] + len(heads), qt],
                              score[:, n % 3, 0:cols * len(heads)].rearrange("p (j k) -> p j k", k=cols),
                              AX.X, ALU.max).then_inc(max_free, 1)

        def max_parts(b, g):
            n = g * U1 + NMU
            dve.wait_ge(max_full, b.times(NG * U1, n + 1))
            if g:
                dve.wait_ge(nm_in[(g - 1) % 2], b.times(64, 32 * ((g - 1) // 2) + 32))
            elif not b.first:
                dve.wait_ge(nm_in[1], b.times(64))
            src = score[0:GH * TB, n % 3, 0:P]
            dve.tensor_scalar(nm[:, 0, :], src, -1.0, None, ALU.mult).then_inc(nm_high, 1)
            dve.wait_ge(nm_high, b.times(NG, g + 1))
            dve.scalar_tensor_tensor(out=nm[:, 1, :], in0=src, scalar=-1.0, in1=nm[:, 0, :],
                                     op0=ALU.mult, op1=ALU.subtract).then_inc(nm_ready, 1)
            dve.wait_ge(nm_ready, b.times(NG, g + 1))
            dve.sem_inc(max_free, 1)

        def split_mid(b, t):
            half, qk, n = proj(t)
            dve.wait_ge(rem_ready, b.times(4, n + 1))
            dve.tensor_copy(part[:, half, qk, 1, :], rem[:, n % 2, :]).then_inc(mid_ready, 1)

        def scale_out(b, g, n, bank):
            v = misc[:, bank, :].rearrange("p (t j c) -> p t j c", t=TB, j=GH)
            dve.wait_ge(misc_full, n + 1)
            if g == 0 and not b.first:
                dve.wait_ge(attnT_ready, b.times(2))
            if not (b.first and g == 0):
                dve.wait_ge(attn_ready, b.times(NG, g))
            dve.reciprocal(rec[:], v[:, :, :, DH]).then_inc(rec_ready, 1)
            dve.wait_ge(rec_ready, b.times(NG, g + 1))
            out = attn[:, :, GH * DH * g:GH * DH * (g + 1)].rearrange("p t (j c) -> p t j c", j=GH)
            dve.tensor_tensor(out, v[:, :, :, 0:DH], rec[:].unsqueeze(3).to_broadcast([P, TB, GH, DH]), ALU.mult).then_inc(attn_ready, 1)

        def add_out(b, k, n, bank):
            dve.wait_ge(misc_full, n + 1)
            t0 = b.times(TB, 2 * k)
            xs = x[:, t0:t0 + 2, :] if b.i is None else x[:, bass.ds(t0, 2), :]
            dve.tensor_tensor(xs, misc[:, bank, :].rearrange("p (t d) -> p t d", t=2), xs, ALU.add).then_inc(x_out, 1)
            dve.wait_ge(x_out, b.times(2, k + 1))
            for i in range(2):
                t = b.times(TB, 2 * k + i)
                if b.i is None:
                    dve.bn_stats(stats[:, t, :], x[:, t, :]).then_inc(T.bn, 1)
                else:
                    dve.bn_stats(stats[:, bass.ds(t, 1), :].rearrange("p a s -> p (a s)"),
                                 x[:, bass.ds(t, 1), :].rearrange("p a d -> p (a d)")).then_inc(T.bn, 1)

        def low(t, b, bank):
            k = int(t[-1])
            dve.wait_ge(xnT_high, b.times(2, k + 1))
            dve.tensor_tensor(xnT[:, 1, k, :], misc[:, bank, :], xnT[:, 0, k, :], ALU.subtract).then_inc(xnT_ready, 1)

        def empty(t, b, g, n, bank):
            if t == "OT":
                scale_out(b, g, n, bank)
            elif t[:2] == "WO":
                add_out(b, int(t[2]), n, bank)
            elif t[0] == "X":
                low(t, b, bank)

        def maxima(b, g):
            for u in range(NMU):
                reduce_max(b, g, u)
            max_parts(b, g)

        norm(Batch(0))
        for k, (raw, _, w) in enumerate(weights):
            dve.wait_ge(w_high, k + 1)
            dve.tensor_tensor(w[:, 1], raw, w[:, 0], ALU.subtract).then_inc(w_ready, 1)
        for n, (t, k) in enumerate(PRO):
            if t[0] == "X":
                low(t, Batch(k), n % 2)
            if t[0] in "QK":
                split_mid(Batch(0), t)
            if t == "K1":
                norm(Batch(1))
            if t[0] == "V":
                half = slice(int(t[1]) * H // 2, (int(t[1]) + 1) * H // 2)
                dve.memset(KS[ROWS1:P, half, :], 1.0).then_inc(ones_ready, 1)
            if n == EARLY_MAX:
                maxima(Batch(0), 0)
        for b in batches(dve):
            for g in range(NG):
                ahead = None if b.last and g == NG - 1 else (b, g + 1) if g < NG - 1 else (b.next, 0)
                for u in range(PLACES):
                    if b.first and u < MORE:
                        if u == 0 and g < len(x_in):
                            dve.wait_ge(x_in[g], 16)
                        statistics(EARLY * TB + MORE * g + u)
                    if ahead and u < NMU:
                        reduce_max(*ahead, u)
                    for t in due(b, g, u):
                        empty(t, *whose(b, g, t), misc_no(b, g, t), misc_bank(b, g, t))
                    for t in due(b, g, u - MID_LAG):
                        if t[0] in "QK":
                            split_mid(whose(b, g, t)[0], t)
                    if (g, u) in NORM_AT and not (b.i is None and b.c >= NB - 2):
                        norm(b.next.next, (NORM_AT.index((g, u)),))
                    if ahead and u == TURN:
                        max_parts(*ahead)
                if b.first:
                    if g == NG - 1:
                        deviations(1)
                if b.i is None and b.c == 1 and g == 0:
                    invert(1)
        last = Batch(NB - 1)
        for k, g in enumerate((2, 3)):
            scale_out(last, g, TAIL + k, (TAIL + k) % 2)
        for k in range(2):
            add_out(last, k, TAIL_AT + 2 + k, (TAIL_AT + 2 + k) % 2)


def norm_stats(dve, T, done, had, lo, hi):
    s, mean, rstd = T.stats[:, lo:hi], T.mean[:, lo:hi], T.rstd[:, lo:hi]
    tmp = s[:, :, 0]
    n = T.norm_steps
    dve.tensor_tensor(mean, s[:, :, 1], s[:, :, 4], ALU.add).then_inc(done, 1)
    dve.tensor_tensor(tmp, s[:, :, 1], s[:, :, 4], ALU.subtract).then_inc(done, 1)
    dve.tensor_tensor(rstd, s[:, :, 2], s[:, :, 5], ALU.add).then_inc(done, 1)
    dve.wait_ge(done, had + 3)
    dve.tensor_scalar(mean, mean, 0.5, None, ALU.mult).then_inc(n, 1)
    dve.tensor_tensor(tmp, tmp, tmp, ALU.mult).then_inc(n, 1)
    dve.tensor_scalar(rstd, rstd, 1.0 / D, EPS, ALU.mult, ALU.add).then_inc(n, 1)
    T.norm_done += 3
    dve.wait_ge(n, T.norm_done)
    dve.scalar_tensor_tensor(out=rstd, in0=tmp, scalar=0.25, in1=rstd, op0=ALU.mult, op1=ALU.add).then_inc(done, 2)


class Tensors:
    pass


def shared(nc, ctx):
    T = Tensors()
    sb = lambda name, shape, dt=F32: ctx.enter_context(nc.sbuf_tensor(name, shape, dt))
    T.x = sb("x_sb", [P, NT, D])
    T.mean, T.rstd = (sb(n, [P, NT]) for n in ("mean", "rstd"))
    T.stats = sb("stats", [P, NT, 6])
    T.ident = sb("ident", [P, P])
    T.bn = ctx.enter_context(nc.semaphore("bn"))
    T.norm_steps = ctx.enter_context(nc.semaphore("norm_steps"))
    T.norm_done = 0
    T.passed = ctx.enter_context(nc.semaphore("passed"))
    return T


def attention_weights(WQ, WK, WV, WO):
    def cols(w):
        return w.reshape(2, H // 2, DH, D).transpose(3, 0, 2, 1).reshape(D, D)
    wqk = np.concatenate([cols(WQ), cols(WK)], axis=1)
    return (np.ascontiguousarray(wqk), np.ascontiguousarray(WV.reshape(H * DH, D).T),
            np.ascontiguousarray(WO.transpose(0, 2, 1).reshape(H * DH, D)))


BLK = 4
PAD_TILES = ST_TILES + NE
ROW = D + 2
PADS = 2 * NE
BIG = 1e30
NBLK = NT // BLK
STRIP = 32
APART = 4
ROUND = 3
LOG2P = 7


CREDIT = 1


def first_apart(eng, n):
    yield 0
    with eng.Fori(1, n) as i:
        yield i


def dyn(a, start, n=1):
    return a[:, bass.ds(start, n)]


def flat(a):
    return a.rearrange("p a b -> p (a b)")


def blocks(eng):
    return first_apart(eng, (NBLK - APART) // ROUND)


def after(eng, semaphore, value):
    if not isinstance(value, int) or value > 0:
        eng.wait_ge(semaphore, value)


def front(nc, ctx, T, gw_dram, bias_dram, sw13_dram, sw2_dram, ew_dram, sorted_dram, out_dram):
    sb = lambda name, shape, dt=F32: ctx.enter_context(nc.sbuf_tensor(name, shape, dt))
    sem = lambda name: ctx.enter_context(nc.semaphore(name))
    x, mean, rstd = T.x, T.mean, T.rstd
    big = sb("big", [P, NBLK * KB, S])
    gw = sb("gw", [P, KB, STRIP])
    gs = sb("gs", [P, 2, P])
    score = sb("gate_score", [P, NT, NE])
    rows = sb("rows", [P, 2, BLK, 2, ROW])
    xn = rows[:, :, :, 0, 0:D]
    idx = sb("idx", [P, 2, BLK, 2], U32)
    w13 = sb("sw13", [P, KB, 2 * HID])
    w2 = sb("sw2", [P, KB, D])
    turned = sb("turned", [P, 2, KB, S])
    g, hT = turned[:, 0], turned[:, 1]
    sums = sb("sums", [P, ROUND, BLK, D])
    four = ctx.enter_context(nc.psum_tensor("four", [P, 2, KB, S], F32))
    gp = ctx.enter_context(nc.psum_tensor("gp", [P, 2, S], F32))
    two = ctx.enter_context(nc.psum_tensor("two", [P, 2, S], F32))
    tr, up = four, four
    gt = two
    down = two[:].rearrange("p a (b d) -> p a b d", b=2)
    gw_in, pad_in, bias_in, zeroed = sem("gw_in"), sem("pad_in"), sem("bias_in"), sem("zeroed")
    gw_zero = sem("gw_zero")
    stat, std, rs = sem("g_stat"), sem("g_std"), sem("g_rstd")
    xn_ready, tr_full, xT_ready = sem("g_xn"), sem("g_tr_full"), sem("g_xT")
    big_ready = [sem("big_ready0"), sem("big_ready1")]
    gp_full, gs_ready, gt_full, logits_ready, score_ready = sem("gp_full"), sem("gs_ready"), sem("gt_full"), sem("logits_ready"), sem("score_ready")
    zero_ready = sem("zero_ready")
    zero = sb("zero", [P, NE, ROW])

    desc = sb("desc", [P, NE])
    desc_i = sb("desc_i", [P, NE], I32)
    bias = sb("bias", [P, NE])
    biased = sb("biased", [P, NT, NE])
    one1 = sb("one1", [P, NT, NE])
    one2 = sb("one2", [P, NT, NE])
    scr = sb("scr", [P, NT, NE])
    both = sb("both", [P, NT * NE], BF16)
    best = sb("best", [P, NT])
    before = sb("before", [P, P], BF16)
    ones = sb("ones_b", [P, P], BF16)
    pad = NT // 2
    pre = sb("pre", [P, 2, pad + NT, NE])
    tiles = sb("tiles", [P, NE])
    tiles_i = sb("tiles_i", [P, NE], I32)
    first = sb("first", [P, 2, NE + NE])
    jt = sb("jt", [1, ST_TILES])
    jt_i = sb("jt_i", [1, ST_TILES], I32)
    past = pre[0:1].rearrange("p a t e -> p (a t e)")[:, 0:ST_TILES * (NE - 1)].rearrange("p (t e) -> p t e", e=NE - 1)
    et = sb("et", [1, ST_TILES])
    slot_f = sb("slot_f", [P, NT])
    pad_f = sb("pad_f", [P, NE])
    pad_g = sb("pad_g", [P, NE])
    pad_i = sb("pad_i", [P, NE], U32)
    row_i = sb("row_i", [P, NE], I32)
    row_f = sb("row_f", [P, NE])
    c = sem("route")
    consts, both_ready, cnt_full = sem("g_consts"), sem("both_ready"), sem("cnt_full")
    ca = sem("g_const_a")

    w_in = sem("s_w_in")
    stored = [sem(f"stored{k}") for k in range(ROUND)]
    rows_ready = sem("rows_ready")
    scattered = [sem(f"scattered{k}") for k in range(2 * BLK)]
    up_full, g_ready, h_ready, down_full, sum_ready = sem("up_full"), sem("g_ready"), sem("h_ready"), sem("down_full"), sem("sum_ready")
    NPAIR = NBLK // 2
    CREDIT2 = 2

    block = ctx.enter_context(nc.Block())

    @block.sync
    def _(sp):
        sp.dma_start(bias[:], bias_dram.rearrange("(a n) -> a n", a=1).partition_broadcast(P)).then_inc(bias_in, 16)
        sp.dma_start(w13[:], sw13_dram.rearrange("(k p) n -> p k n", p=P)).then_inc(w_in, 16)
        sp.dma_start(w2[:], sw2_dram.rearrange("(k p) n -> p k n", p=P)).then_inc(w_in, 16)
        sp.wait_ge(gw_zero, 1)
        sp.dma_start(gw[:, :, 0:NE], gw_dram.rearrange("(k p) n -> p k n", p=P)).then_inc(gw_in, 16)
        sp.wait_ge(zero_ready, 2)
        for t in range(2 * NT, ST_TILES):
            sp.dma_start(sorted_dram[t * P:(t + 1) * P, :], zero[:, t - 2 * NT, :]).then_inc(pad_in, 16)
        for k in range(2):
            r = (NT + k * NE) * P
            sp.dma_start(out_dram[r:r + NE * P, :].rearrange("(k p) d -> p k d", p=P), zero[:, :, 0:D]).then_inc(zeroed, 16)
        dst = out_dram[0:NT * P, :].rearrange("(t p) d -> p t d", p=P)

        def store(i, place):
            sp.wait_ge(sum_ready, i * 2 + 2)
            sp.dma_start(dyn(dst, i * BLK, BLK), sums[:, place]).then_inc(stored[place], 16)

        def weights(k):
            sp.dma_start(dyn(x, k * BLK, BLK), ew_dram[bass.ds(k * P, P), :].rearrange("p (a n) -> p a n", a=BLK)).then_inc(T.w_in, 16)

        for i in range(APART):
            store(i, i % ROUND)
        for j in blocks(sp):
            for u in range(ROUND):
                store(j * ROUND + (APART + u), (APART + u) % ROUND)
            sp.wait_ge(rows_ready, j * (BLK * (ROUND + 1)) + BLK * ROUND)
            for u in range(ROUND):
                weights(j * ROUND + u)
        sp.wait_ge(zeroed, 32)
        for place in range(ROUND):
            sp.wait_ge(stored[place], 16 * len(range(place, NBLK, ROUND)))

    @block.gpsimd
    def _(pool):
        pool.memset(gw[:], 0.0).then_inc(gw_zero, 1)
        pool.memset(before[:], 1.0).then_inc(ca, 1)
        pool.memset(ones[:], 1.0).then_inc(consts, 1)
        pool.memset(zero[:], 0.0).then_inc(zero_ready, 1)
        pool.wait_ge(zero_ready, 1)
        number = zero[:, :, D:D + 1].bitcast(I32).rearrange("p k a -> p (k a)")
        pool.iota(number, pattern=[[P, NE]], base=(NT + NE) * P, channel_multiplier=1).then_inc(zero_ready, 1)
        pool.iota(desc_i[:], pattern=[[-1, NE]], base=NE, channel_multiplier=0).then_inc(consts, 1)
        pool.iota(jt_i[:], pattern=[[1, ST_TILES]], base=0, channel_multiplier=0).then_inc(consts, 1)
        pool.iota(row_i[:], pattern=[[P, NE]], base=ST_TILES * P, channel_multiplier=1).then_inc(consts, 1)
        pool.iota(T.dest[:], pattern=[[P, NT], [0, 2]], base=0, channel_multiplier=1).then_inc(consts, 1)
        pool.wait_ge(ca, 1)
        pool.affine_select(out=before[:], in_=before[:], compare_op=ALU.is_gt, fill=0.0, base=0,
                           pattern=[[1, P]], channel_multiplier=-1).then_inc(consts, 1)
        with pool.Fori(0, NPAIR) as i:
            for u in range(2):
                pool.wait_ge(xT_ready, i * 4 + (2 * u + 1))
                settle(pool, T.passed)
                pool.tensor_copy(flat(dyn(big, (i * 2 + u) * KB)), turned[:, u, 0]).then_inc(big_ready[0], 1)
        pool.wait_ge(pad_in, 16 * (ST_TILES - 2 * NT))
        pool.iota(number, pattern=[[P, NE]], base=NT * P, channel_multiplier=1).then_inc(zero_ready, 1)
        pool.wait_ge(zero_ready, 3)
        pool.wait_ge(T.routed, 1)
        for e in range(NE):
            pool.indirect_dma_start(out=sorted_dram[:, :], out_offset=bass.IndirectOffsetOnAxis(ap=pad_i[:, e:e + 1], axis=0),
                                    in_=zero[:, e, :], in_offset=None).then_inc(T.padded, 16)
        pool.wait_ge(T.padded, 16 * NE)
        with pool.Fori(0, NBLK // 2) as i:
            for k in range(2 * BLK):
                pool.wait_ge(rows_ready, i * (2 * BLK) + (k + 1))
                settle(pool, T.passed)
                half, tt = divmod(k, BLK)
                for choice in range(2):
                    pool.indirect_dma_start(out=sorted_dram[:, :],
                                            out_offset=bass.IndirectOffsetOnAxis(ap=idx[:, half, tt, choice:choice + 1], axis=0),
                                            in_=rows[:, half, tt, choice, :], in_offset=None).then_inc(scattered[k], 16)
        for k in range(2 * BLK):
            pool.wait_ge(scattered[k], 32 * (NBLK // 2))

    @block.scalar
    def _(act):
        act.wait_ge(stat, 5)
        act.activation(rstd[:], rstd[:], ACT.Sqrt).then_inc(std, 1)
        for i in first_apart(act, NPAIR):
            for u in range(2):
                if not isinstance(i, int):
                    act.wait_ge(gp_full, i * 2 + (u - 1))
                    act.wait_ge(big_ready[0], i * 2 + (u - 1))
                for k in range(KB):
                    act.wait_ge(tr_full, i * 4 + (2 * u + k + 1))
                    act.activation(turned[:, u, k, :], tr[:, u, k, :], ACT.Copy).then_inc(xT_ready, 1)
                act.activation(flat(dyn(big, (i * 2 + u) * KB + 1)), tr[:, u, 1, :], ACT.Copy).then_inc(big_ready[1], 1)
        act.wait_ge(logits_ready, NBLK + CREDIT2)
        act.activation(score[:], score[:], ACT.Sigmoid).then_inc(score_ready, 1)

        def silu(i, m):
            act.wait_ge(up_full, i * 4 + (2 * m + 1))
            after(act, h_ready, i * 2 + (m - 1))
            act.activation(g[:, m, :], up[:, m, 0, :], ACT.Silu).then_inc(g_ready, 1)

        for i in range(APART):
            for m in range(KB):
                silu(i, m)
        for j in blocks(act):
            for u in range(ROUND):
                for m in range(KB):
                    silu(j * ROUND + (APART + u), m)

    @block.tensor
    def _(pe):
        def turn(n, u):
            pe.wait_ge(xn_ready, n + 1)
            if not isinstance(n, int):
                pe.wait_ge(xT_ready, n * 2 - 2)
                pe.wait_ge(big_ready[1], n - 1)
            for k in range(KB):
                for tt in range(BLK):
                    mm = pe.transpose(tr[:, u, k, tt * P:(tt + 1) * P], xn[:, u, tt, k * P:(k + 1) * P], T.ident[:])
                mm.then_inc(tr_full, 1)

        def logits(n, u):
            pe.wait_ge(xT_ready, n * 2 + 2)
            pe.wait_ge(gs_ready, n + (CREDIT2 - 1))
            for k in range(KB):
                for tt in range(BLK):
                    mm = pe.matmul(gp[STRIP * tt:STRIP * (tt + 1), u, 0:P], gw[:, k, :],
                                   turned[:, u, k, tt * P:(tt + 1) * P], start=(k == 0), stop=(k == KB - 1))
            mm.then_inc(gp_full, 1)

        def back(n, u):
            pe.wait_ge(gs_ready, n + (CREDIT2 + 1))
            pe.wait_ge(logits_ready, n + (CREDIT2 - 1))
            pe.transpose(gt[:, u, 0:P], gs[:, u, :], T.ident[:]).then_inc(gt_full, 1)

        pe.sem_inc(gs_ready, CREDIT2)
        pe.sem_inc(logits_ready, CREDIT2)
        pe.wait_ge(gw_in, 16)
        for i in first_apart(pe, NPAIR):
            if not isinstance(i, int):
                for u in range(2):
                    logits(i * 2 + (u - 2), u)
            for u in range(2):
                turn(i * 2 + u, u)
            if not isinstance(i, int):
                for u in range(2):
                    back(i * 2 + (u - 2), u)
        for f in (logits, back):
            for u in range(2):
                f(NBLK - 2 + u, u)

        def product(i, m):
            after(pe, h_ready, i * 2 + (m - 1))
            for w in range(2):
                for k in range(KB):
                    mm = pe.matmul(up[:, m, w, :], w13[:, k, w * HID + m * P:w * HID + (m + 1) * P], flat(dyn(big, i * KB + k)),
                                   start=(k == 0), stop=(k == KB - 1))
                mm.then_inc(up_full, 1)

        def output(i):
            pe.wait_ge(h_ready, i * 2 + 2)
            after(pe, sum_ready, i * 2)
            for pair in range(2):
                for tt in range(2):
                    for k in range(KB):
                        mm = pe.matmul(down[:, pair, tt, :], hT[:, k, (2 * pair + tt) * P:(2 * pair + tt + 1) * P],
                                       w2[:, k, :], start=(k == 0), stop=(k == KB - 1))
                mm.then_inc(down_full, 1)

        pe.wait_ge(w_in, 32)
        pe.wait_ge(xT_ready, NBLK * KB)
        for k in range(KB):
            pe.wait_ge(big_ready[k], NBLK)
        pe.wait_ge(logits_ready, NBLK + CREDIT2)
        for i in range(APART):
            product(i, 0)
            if i:
                output(i - 1)
            product(i, 1)
            if i == 1:
                pe.wait_ge(consts, 6)
                pe.wait_ge(both_ready, 1)
                pe.matmul(gp[:, 0, :], before[:], both[:], start=True, stop=True).then_inc(cnt_full, 1)
                pe.matmul(gp[:, 1, :], ones[:], both[:], start=True, stop=True).then_inc(cnt_full, 1)
        for j in blocks(pe):
            for u in range(ROUND):
                i = j * ROUND + (APART + u)
                product(i, 0)
                output(i - 1)
                product(i, 1)
        output(NBLK - 1)

    @block.vector
    def _(dve):
        def normed(n, u):
            if not isinstance(n, int):
                dve.wait_ge(tr_full, n * 2 - 2)
            for tt in range(BLK):
                t = n * BLK + tt
                ins = dve.tensor_scalar(xn[:, u, tt, :], flat(dyn(x, t)), dyn(mean, t), dyn(rstd, t), ALU.subtract, ALU.mult)
            ins.then_inc(xn_ready, 1)

        def logits_out(n, u):
            dve.wait_ge(gp_full, n + 1)
            dve.wait_ge(gt_full, n + (CREDIT2 - 1))
            dve.tensor_copy(gs[:, u, :], gp[:, u, 0:P]).then_inc(gs_ready, 1)

        def logits_back(n, u):
            dve.wait_ge(gt_full, n + (CREDIT2 + 1))
            dve.tensor_copy(dyn(score, n * BLK, BLK), gt[:, u, 0:P].rearrange("p (t e) -> p t e", e=STRIP)[:, :, 0:NE]).then_inc(logits_ready, 1)

        norm_stats(dve, T, stat, 0, 0, NT)
        dve.wait_ge(std, 1)
        dve.reciprocal(rstd[:], rstd[:]).then_inc(rs, 1)
        dve.wait_ge(rs, 1)
        dve.sem_inc(gt_full, CREDIT2)
        for i in first_apart(dve, NPAIR):
            for u in range(2):
                normed(i * 2 + u, u)
            if not isinstance(i, int):
                for f in (logits_out, logits_back):
                    for u in range(2):
                        f(i * 2 + (u - 2), u)
        for f in (logits_out, logits_back):
            for u in range(2):
                f(NBLK - 2 + u, u)

        def gated(i):
            for m in range(KB):
                dve.wait_ge(up_full, i * 4 + (2 * m + 2))
                dve.wait_ge(g_ready, i * 2 + (m + 1))
                after(dve, down_full, i * 2)
                dve.tensor_tensor(hT[:, m, :], g[:, m, :], up[:, m, 1, :], ALU.mult).then_inc(h_ready, 1)

        def add(i, place, uses):
            after(dve, stored[place], uses * 16)
            for pair in range(2):
                dve.wait_ge(down_full, i * 2 + (pair + 1))
                dve.tensor_tensor(sums[:, place, 2 * pair:2 * pair + 2, :], down[:, pair], dyn(x, i * BLK + 2 * pair, 2), ALU.add).then_inc(sum_ready, 1)

        def token_rows(i, half, uses):
            for tt in range(BLK):
                t = i * BLK + tt
                after(dve, scattered[half * BLK + tt], uses * 32)
                for k in range(2):
                    dve.tensor_scalar(rows[:, half, tt, k, 0:D], flat(dyn(x, t)), dyn(mean, t), flat(dyn(T.r[:, :, k:k + 1], t)), ALU.subtract, ALU.mult)
                dve.tensor_copy(rows[:, half, tt, :, D].bitcast(I32), flat(dyn(T.dest, t)))
                dve.tensor_copy(rows[:, half, tt, :, D + 1], flat(dyn(T.s, t)))
                dve.tensor_copy(idx[:, half, tt, :], flat(dyn(T.slot, t))).then_inc(rows_ready, 1)

        n = [0]

        def step(ins):
            n[0] += 1
            ins.then_inc(c, 1)
            dve.wait_ge(c, n[0])

        per_e = lambda a: a.unsqueeze(1).to_broadcast([P, NT, NE])
        per_t = lambda a: a.unsqueeze(2).to_broadcast([P, NT, NE])

        def choose(one):
            step(dve.tensor_reduce(best[:], biased[:], AX.X, ALU.max))
            step(dve.tensor_tensor(scr[:], biased[:], per_t(best[:]), ALU.is_equal))
            step(dve.tensor_tensor(scr[:], scr[:], per_e(desc[:]), ALU.mult))
            step(dve.tensor_reduce(best[:], scr[:], AX.X, ALU.max))
            step(dve.tensor_tensor(one[:], per_e(desc[:]), per_t(best[:]), ALU.is_equal))

        def chosen_score(one, s):
            step(dve.tensor_tensor(scr[:], one[:], score[:], ALU.mult))
            step(dve.tensor_reduce(s, scr[:], AX.X, ALU.add))

        dve.wait_ge(consts, 6)
        dve.wait_ge(bias_in, 16)
        dve.tensor_copy(desc[:], desc_i[:]).then_inc(T.tables, 1)
        dve.tensor_copy(jt[:], jt_i[:]).then_inc(T.tables, 1)
        dve.tensor_copy(row_f[:], row_i[:]).then_inc(T.tables, 1)
        dve.memset(pre[:, :, 0:pad, :], 0.0).then_inc(T.tables, 1)
        dve.memset(first[:, :, 0:NE], 0.0).then_inc(T.tables, 1)
        dve.wait_ge(T.tables, 5)
        dve.wait_ge(score_ready, 1)
        step(dve.tensor_tensor(biased[:], score[:], per_e(bias[:]), ALU.add))
        choose(one1)
        step(dve.scalar_tensor_tensor(out=biased[:], in0=one1[:], scalar=-BIG, in1=biased[:], op0=ALU.mult, op1=ALU.add))
        gated(0)
        choose(one2)
        dve.tensor_tensor(both[:], one1[:].rearrange("p t e -> p (t e)"), one2[:].rearrange("p t e -> p (t e)"), ALU.add).then_inc(both_ready, 1)
        add(0, 0, 0)
        gated(1)
        chosen_score(one1, T.s[:, :, 0])
        chosen_score(one2, T.s[:, :, 1])
        step(dve.tensor_tensor(T.r[:], T.s[:], rstd[:].unsqueeze(2).to_broadcast([P, NT, 2]), ALU.mult))
        dve.wait_ge(cnt_full, 2)
        total = gp[:, 1, :].rearrange("p (t e) -> p t e", e=NE)
        inner = gp[:, 0, :].rearrange("p (t e) -> p t e", e=NE)
        step(dve.tensor_copy(pre[:, 0, pad:, :], total))
        a, k = 0, 1
        while k < NT:
            step(dve.tensor_tensor(pre[:, 1 - a, pad:, :], pre[:, a, pad:, :], pre[:, a, pad - k:pad + NT - k, :], ALU.add))
            a, k = 1 - a, 2 * k
        step(dve.tensor_scalar(tiles_i[:], pre[:, a, pad + NT - 1, :], float(P - 1), None, ALU.add))
        step(dve.tensor_scalar(tiles_i[:], tiles_i[:], LOG2P, None, ALU.logical_shift_right))
        step(dve.tensor_copy(tiles[:], tiles_i[:]))
        step(dve.tensor_copy(first[:, 0, NE:], tiles[:]))
        f, k = 0, 1
        while k < NE:
            step(dve.tensor_tensor(first[:, 1 - f, NE:], first[:, f, NE:], first[:, f, NE - k:2 * NE - k], ALU.add))
            f, k = 1 - f, 2 * k
        ends = first[:, f, NE:]
        starts = first[:, f, NE - 1:2 * NE - 1]
        step(dve.tensor_scalar(pad_f[:], ends, 1.0, float(P), ALU.subtract, ALU.mult))
        step(dve.tensor_scalar(pad_f[:], pad_f[:], row_f[:, 0:1], float(-ST_TILES * P), ALU.add, ALU.add))
        step(dve.tensor_scalar(pad_g[:], tiles[:], 0.0, None, ALU.is_equal))
        step(dve.tensor_tensor(row_f[:], row_f[:], pad_f[:], ALU.subtract))
        step(dve.tensor_tensor(row_f[:], row_f[:], pad_g[:], ALU.mult))
        step(dve.tensor_tensor(pad_f[:], pad_f[:], row_f[:], ALU.add))
        dve.tensor_copy(pad_i[:], pad_f[:]).then_inc(T.routed, 1)
        add(1, 1, 0)
        gated(2)
        step(dve.tensor_tensor(scr[:], pre[:, a, pad:, :], total, ALU.subtract))
        step(dve.tensor_tensor(scr[:], scr[:], inner, ALU.add))
        step(dve.tensor_scalar(pad_g[:], starts, float(P), None, ALU.mult))
        step(dve.tensor_tensor(biased[:], scr[:], per_e(pad_g[:]), ALU.add))
        for k, one in enumerate((one1, one2)):
            step(dve.tensor_tensor(scr[:], one[:], biased[:], ALU.mult))
            step(dve.tensor_reduce(slot_f[:], scr[:], AX.X, ALU.add))
            step(dve.tensor_copy(T.slot[:, :, k], slot_f[:]))
        add(2, 2, 0)
        gated(3)
        for j in blocks(dve):
            for u in range(ROUND + 1):
                token_rows(j * (ROUND + 1) + u, u % 2, j * 2 + u // 2)
                if u < ROUND:
                    i = APART + u
                    add(j * ROUND + (i - 1), (i - 1) % ROUND, j + (i - 1) // ROUND)
                    gated(j * ROUND + i)
        add(NBLK - 1, (NBLK - 1) % ROUND, (NBLK - 1) // ROUND)
        per = lambda a: a.unsqueeze(1).to_broadcast([1, ST_TILES, NE - 1])
        step(dve.tensor_tensor(past, jt[:].unsqueeze(2).to_broadcast([1, ST_TILES, NE - 1]), per(ends[0:1, 0:NE - 1]), ALU.is_ge))
        step(dve.tensor_reduce(et[:], past, AX.X, ALU.add))
        step(dve.tensor_copy(T.expert[:], et[:]))
        step(dve.tensor_tensor(past, past, per(tiles[0:1, 0:NE - 1]), ALU.mult))
        step(dve.tensor_reduce(et[:], past, AX.X, ALU.add))
        step(dve.tensor_copy(T.begins[:], et[:]))


RING = 8


class Step:

    def __init__(self, c, i=None):
        self.c, self.i = c, i

    def times(self, k, more=0):
        return k * self.c + more if self.i is None else self.i * (RING * k) + (k * self.c + more)

    @property
    def ring(self):
        return self.c % RING

    def uses(self, k, more=0):
        v = k * (self.c // RING) + more
        return v if self.i is None else self.i * k + v

    def back(self, n):
        return Step(self.c - n, self.i)


def experts(nc, ctx, T, sorted_dram, out_dram):
    sb = lambda name, shape, dt=F32: ctx.enter_context(nc.sbuf_tensor(name, shape, dt))
    sem = lambda name: ctx.enter_context(nc.semaphore(name))
    rows = sb("e_rows", [P, RING, ROW])
    xT = sb("e_xT", [P, 2, 2, KB, P], F32R)
    g = sb("e_gate", [P, 2, HID])
    h = sb("e_h", [P, 2, HID])
    hT = sb("e_hT", [P, 2, 2, KB, P], F32R)
    y = sb("e_y", [P, RING, D])
    ps = lambda name, n: ctx.enter_context(nc.psum_tensor(name, [P, n, S], F32))
    px, pu, ph, py = ps("e_px", 1), ps("e_pu", 2), ps("e_ph", 1), ps("e_py", 2)
    rows_in = [sem(f"e_rows_in{k}") for k in range(RING)]
    sent = [sem(f"e_sent{k}") for k in range(RING)]
    px_full, xT_ready, pu_full, g_ready, h_ready = sem("px_full"), sem("e_xT_ready"), sem("pu_full"), sem("e_g_ready"), sem("e_h_ready")
    ph_full, hT_ready, py_full, y_ready = sem("ph_full"), sem("e_hT_ready"), sem("py_full"), sem("y_ready")
    done = sem("e_done")
    PIECES = NE + NE // 2
    w13 = sb("e_w13", [P, NE, 2, KB, 2 * HID], F32R)
    w2 = sb("e_w2", [P, NE, 2, KB, D], F32R)
    pieces = []
    for k in range(PIECES):
        came = T.x[:, BLK * k:BLK * k + BLK, :]
        if k < NE:
            pieces.append((came.rearrange("p (a b) d -> p a (b d)", b=2), w13[:, k, 0], w13[:, k, 1]))
        else:
            pair = slice(2 * (k - NE), 2 * (k - NE) + 2)
            pieces.append((came.rearrange("p (e a) d -> p e a d", a=KB), w2[:, pair, 0], w2[:, pair, 1]))
    whigh_ready, w_ready, x_high, h_high = sem("e_whigh_ready"), [sem("e_wlow_dve"), sem("e_wlow_pool")], sem("e_x_high"), sem("e_h_high")

    UP, BACK, DOWN = 1, 3, 4
    LAST = ST_TILES + DOWN

    def steps(eng):
        for j in range(RING):
            yield Step(j)
        with eng.Fori(0, ST_TILES // RING - 1) as i:
            for u in range(RING):
                yield Step(RING + u, i)
        for j in range(ST_TILES, LAST):
            yield Step(j)

    def tile(s, lag):
        b = s.back(lag)
        return b if s.i is not None or 0 <= b.c < ST_TILES else None

    SHARE = (2, 1)

    def low_parts(eng, who):
        for k, (came, high, low) in enumerate(pieces):
            if (k % sum(SHARE) >= SHARE[0]) == who:
                eng.wait_ge(whigh_ready, k + 1)
                eng.tensor_tensor(low, came, high, ALU.subtract).then_inc(w_ready[who], 1)

    def made(n, who):
        return sum((k % sum(SHARE) >= SHARE[0]) == who for k in range(n))

    block = ctx.enter_context(nc.Block())

    @block.sync
    def _(sp):
        def load(t):
            k = t.ring
            if t.c >= RING:
                sp.wait_ge(sent[k], t.uses(16))
                sp.sem_inc(done, 1)
            settle(sp, T.passed)
            r = t.times(P)
            src = sorted_dram[r:r + P, :] if t.i is None else sorted_dram[bass.ds(r, P), :]
            sp.dma_start(rows[:, k, :], src).then_inc(rows_in[k], 16)

        sp.sem_inc(done, CREDIT)
        for s in steps(sp):
            t = tile(s, 0)
            if t:
                load(t)
        for k in range(RING):
            sp.wait_ge(sent[k], 16 * (ST_TILES // RING))
            sp.sem_inc(done, 1)

    @block.tensor
    def _(pe):
        def product(out, a, w, e, halves=range(KB)):
            we = w[:, bass.ds(e, 1)]
            for kb in halves:
                for i, j in PASSES:
                    mm = pe.matmul(out, a[:, i, kb, :], flat(we[:, :, j, kb, :]),
                                   start=((i, j, kb) == (*PASSES[0], 0)), stop=((i, j, kb) == (*PASSES[-1], KB - 1)))
            return mm

        def expert_of(t):
            return nc.values_load(T.expert[0:1, bass.ds(t.times(1), 1)], engines=(mybir.EngineType.PE,), min_val=0, max_val=NE - 1,
                                  skip_runtime_bounds_check_because="it counts how many of NE - 1 bounds are passed")

        expert = {}
        for s in steps(pe):
            if t := tile(s, 0):
                k = t.ring
                pe.wait_ge(rows_in[k], t.uses(16, 16))
                if t.c:
                    pe.wait_ge(xT_ready, t.times(1))
                for kb in range(KB):
                    mm = pe.transpose(px[:, 0, kb * P:(kb + 1) * P], rows[:, k, kb * P:(kb + 1) * P], T.ident[:])
                mm.then_inc(px_full, 1)
            if s.ring == 0:
                settle(pe, T.passed)
                for lag in (DOWN, UP):
                    if t := tile(s, lag):
                        expert[lag] = expert_of(t)
            ahead = s.back(-1) if s.ring < RING - 1 else None
            if t := tile(s, BACK):
                pe.wait_ge(h_ready, t.times(1, 1))
                if t.c:
                    pe.wait_ge(hT_ready, t.times(1))
                for kb in range(KB):
                    mm = pe.transpose(ph[:, 0, kb * P:(kb + 1) * P], h[:, t.c % 2, kb * P:(kb + 1) * P], T.ident[:])
                mm.then_inc(ph_full, 1)
            if t := tile(s, DOWN):
                pe.wait_ge(hT_ready, t.times(1, 1))
                if t.c >= 2:
                    pe.wait_ge(y_ready, t.times(1, -1))
                if not t.c:
                    for who in range(2):
                        pe.wait_ge(w_ready[who], made(PIECES, who))
                product(py[:, t.c % 2, 0:D], hT[:, t.c % 2], w2, expert[DOWN]).then_inc(py_full, 1)
            if t := tile(s, UP):
                pe.wait_ge(xT_ready, t.times(1, 1))
                if t.c >= 2:
                    pe.wait_ge(h_ready, t.times(1, -1))
                if not t.c:
                    for who in range(2):
                        pe.wait_ge(w_ready[who], made(NE, who))
                product(pu[:, t.c % 2, :], xT[:, t.c % 2], w13, expert[UP], range(1))
                if ahead and (nxt := tile(ahead, DOWN)):
                    expert[DOWN] = expert_of(nxt)
                product(pu[:, t.c % 2, :], xT[:, t.c % 2], w13, expert[UP], range(1, KB)).then_inc(pu_full, 1)
            elif ahead and (nxt := tile(ahead, DOWN)):
                expert[DOWN] = expert_of(nxt)
            if ahead and (nxt := tile(ahead, UP)):
                expert[UP] = expert_of(nxt)

    @block.scalar
    def _(act):
        act.wait_ge(T.w_in, 16 * PIECES)
        for came, high, _ in pieces:
            act.activation(high, came, ACT.Copy).then_inc(whigh_ready, 1)
        for s in steps(act):
            if t := tile(s, 0):
                act.wait_ge(px_full, t.times(1, 1))
                if t.c >= 2:
                    act.wait_ge(pu_full, t.times(1, -1))
                act.activation(flat(xT[:, t.c % 2, 0]), px[:, 0, 0:D], ACT.Copy).then_inc(x_high, 1)
            if t := tile(s, BACK):
                act.wait_ge(ph_full, t.times(1, 1))
                if t.c >= 2:
                    act.wait_ge(py_full, t.times(1, -1))
                act.activation(flat(hT[:, t.c % 2, 0]), ph[:, 0, 0:HID], ACT.Copy).then_inc(h_high, 1)
            if t := tile(s, DOWN):
                k = t.ring
                act.wait_ge(py_full, t.times(1, 1))
                if t.c >= RING:
                    act.wait_ge(sent[k], t.uses(16))
                act.activation(y[:, k, :], py[:, t.c % 2, 0:D], ACT.Copy, scale=rows[:, k, D + 1:D + 2]).then_inc(y_ready, 1)
            if t := tile(s, UP):
                act.wait_ge(pu_full, t.times(1, 1))
                if t.c >= 2:
                    act.wait_ge(h_ready, t.times(1, -1))
                act.activation(g[:, t.c % 2, :], pu[:, t.c % 2, 0:HID], ACT.Silu).then_inc(g_ready, 1)

    @block.vector
    def _(dve):
        low_parts(dve, 0)
        for s in steps(dve):
            if t := tile(s, 0):
                dve.wait_ge(x_high, t.times(1, 1))
                dve.tensor_tensor(flat(xT[:, t.c % 2, 1]), px[:, 0, 0:D], flat(xT[:, t.c % 2, 0]), ALU.subtract).then_inc(xT_ready, 1)
            if t := tile(s, BACK):
                dve.wait_ge(h_high, t.times(1, 1))
                dve.tensor_tensor(flat(hT[:, t.c % 2, 1]), ph[:, 0, 0:HID], flat(hT[:, t.c % 2, 0]), ALU.subtract).then_inc(hT_ready, 1)
            if t := tile(s, UP):
                dve.wait_ge(g_ready, t.times(1, 1))
                if t.c >= 2:
                    dve.wait_ge(ph_full, t.times(1, -1))
                dve.tensor_tensor(h[:, t.c % 2, :], g[:, t.c % 2, :], pu[:, t.c % 2, HID:2 * HID], ALU.mult).then_inc(h_ready, 1)

    @block.gpsimd
    def _(pool):
        low_parts(pool, 1)
        for s in steps(pool):
            if t := tile(s, DOWN):
                k = t.ring
                pool.wait_ge(y_ready, t.times(1, 1))
                if t.c:
                    settle(pool, T.passed)
                    begins = pool.value_load(T.begins[0:1, bass.ds(t.times(1), 1)] if t.i is not None else T.begins[0:1, t.c:t.c + 1],
                                             min_val=0, max_val=ST_TILES - 1)
                    pool.wait_ge(done, begins + CREDIT)
                settle(pool, T.passed)
                pool.indirect_dma_start(out=out_dram[:, :],
                                        out_offset=bass.IndirectOffsetOnAxis(ap=rows[:, k, D:D + 1].bitcast(U32), axis=0),
                                        in_=y[:, k, :], in_offset=None, compute_op=ALU.add).then_inc(sent[k], 16)
        for k in range(RING):
            pool.wait_ge(sent[k], 16 * (ST_TILES // RING))


def layer(nc, ins, out):
    x, wqk, wv, wo, gw, bias, ew, sw13, sw2 = ins
    sorted_dram = nc.dram_tensor("sorted_rows", [PAD_TILES * P, ROW], F32, kind="Internal").ap()
    with contextlib.ExitStack() as ctx:
        T = shared(nc, ctx)
        with contextlib.ExitStack() as phase:
            attention(nc, phase, T, x, wqk, wv, wo)
        routing(nc, ctx, T)
        with contextlib.ExitStack() as phase:
            front(nc, phase, T, gw, bias, sw13, sw2, ew, sorted_dram, out)
        with contextlib.ExitStack() as phase:
            experts(nc, phase, T, sorted_dram, out)


def routing(nc, ctx, T):
    sb = lambda name, shape, dt=F32: ctx.enter_context(nc.sbuf_tensor(name, shape, dt))
    T.s = sb("s", [P, NT, 2])
    T.r = sb("r", [P, NT, 2])
    T.slot = sb("slot", [P, NT, 2], U32)
    T.dest = sb("dest", [P, NT, 2], I32)
    T.expert = sb("expert", [1, ST_TILES], I32)
    T.begins = sb("begins", [1, ST_TILES], I32)
    T.routed = ctx.enter_context(nc.semaphore("routed"))
    T.padded = ctx.enter_context(nc.semaphore("padded"))
    T.tables = ctx.enter_context(nc.semaphore("tables"))
    T.w_in = ctx.enter_context(nc.semaphore("ew_in"))


def expert_weights(w1, w2, w3):
    w13 = np.concatenate([w1.transpose(0, 2, 1), w3.transpose(0, 2, 1)], axis=2).reshape(NE, KB, P, 2 * HID)
    w2 = w2.transpose(0, 2, 1).reshape(NE // 2, 2 * KB, P, D)
    pieces = [w.transpose(0, 2, 1, 3).reshape(-1, KB * S) for w in (w13, w2)]
    return np.ascontiguousarray(np.concatenate(pieces))


def kernel(L0_attn_x, L0_attn_WQ, L0_attn_WK, L0_attn_WV, L0_attn_WO, L0_ffn_gate_w, L0_ffn_w1, L0_ffn_w2,
           L0_ffn_w3, L0_ffn_sw1, L0_ffn_sw2, L0_ffn_sw3, L0_ffn_expert_bias):
    import concourse.bacc as bacc
    from concourse.bass_utils import run_bass_kernel_spmd

    lay = lambda a: np.ascontiguousarray(np.asarray(a))
    WQ, WK, WV, WO, w1, w2, w3, sw1, sw2, sw3 = (
        lay(a) for a in (L0_attn_WQ, L0_attn_WK, L0_attn_WV, L0_attn_WO, L0_ffn_w1, L0_ffn_w2, L0_ffn_w3,
                         L0_ffn_sw1, L0_ffn_sw2, L0_ffn_sw3))
    wqk, wv, wo = attention_weights(WQ, WK, WV, WO)
    arrays = {
        "x": lay(L0_attn_x).reshape(NT * P, D),
        "wqk": wqk, "wv": wv, "wo": wo,
        "gate_wT": lay(lay(L0_ffn_gate_w).T),
        "expert_bias": lay(L0_ffn_expert_bias),
        "ew": expert_weights(w1, w2, w3),
        "ws13": lay(np.concatenate([sw1.T, sw3.T], axis=1)),
        "ws2": lay(sw2.T),
    }
    nc = bacc.Bacc("TRN2", target_bir_lowering=False, num_devices=1)
    ins = [nc.dram_tensor(n, a.shape, F32, kind="ExternalInput").ap() for n, a in arrays.items()]
    out = nc.dram_tensor("out", [(NT + PADS) * P, D], F32, kind="ExternalOutput").ap()
    layer(nc, ins, out)
    got = run_bass_kernel_spmd(nc, [arrays], core_ids=[0])
    return got.results[0]["out"][0:NT * P].reshape(NB, S, D)
```
